# Optimizing a Trainium2 kernel written in Bass

```python
import numpy as np
import jax
import jax.numpy as jnp

def _softmax(x, axis=-1):
    return jax.nn.softmax(x, axis=axis)

def _gelu(x):
    return jax.nn.gelu(x, approximate=True)

def _silu(x):
    return jax.nn.silu(x)

def _sigmoid(x):
    return jax.nn.sigmoid(x)

def _layernorm(x, axis=-1, eps=1e-05):
    m = jnp.mean(x, axis=axis, keepdims=True)
    v = jnp.var(x, axis=axis, keepdims=True)
    return (x - m) / jnp.sqrt(v + eps)

def _scatter_add(tgt, idx, src, axis=0):
    return tgt.at[idx].add(src)

def _segment_sum(src, seg, n):
    return jax.ops.segment_sum(src, seg, n)
kernel_name = 'mk_decoder_preln_d1_seqx_r4_682b52'

def setup_inputs(seed: int=0):
    np.random.seed(seed)
    _w = jnp.asarray

    def _rec_inputs():
        import jax
        import jax.numpy as jnp
        _rk = jax.random.key(seed)
        x = -0.0002928 + 1 * jax.random.normal(jax.random.fold_in(_rk, 1), (8, 512, 256), jnp.float32)
        _lenS = 512 - jax.random.randint(jax.random.fold_in(_rk, 7), (8,), 0, max(1, 512 // 4) + 1, jnp.int32)
        _lenS2 = 64 - jax.random.randint(jax.random.fold_in(_rk, 8), (8,), 0, max(1, 64 // 4) + 1, jnp.int32)
        _ctx_1024P = jax.random.normal(jax.random.fold_in(_rk, 11), (8, 16, 256), jnp.float32)
        _ctx_1024c = jax.random.dirichlet(jax.random.fold_in(_rk, 511), 0.3 * jnp.ones((16,), jnp.float32), (8, 64))
        _ctx_1024t = jnp.einsum('bsk,bkd->bsd', _ctx_1024c, _ctx_1024P)
        _ctx_1024t = _ctx_1024t * jax.lax.rsqrt(jnp.mean(jnp.square(_ctx_1024t)) + 1e-12) * 0.953939
        ctx_1024 = -1.39393e-06 + 0.999914 * (_ctx_1024t + 0.3 * jax.random.normal(jax.random.fold_in(_rk, 611), (8, 64, 256), jnp.float32))
        _validS = jnp.arange(512)[None, :] < _lenS[:, None]
        _validS2 = jnp.arange(64)[None, :] < _lenS2[:, None]
        _causal = jnp.tril(jnp.ones((512, 512), dtype=bool))
        mask_BxSxS2_if1 = jnp.where(jnp.ones((8, 512, 64), dtype=bool), 1, 0).astype(jnp.int32)
        return (x, ctx_1024, mask_BxSxS2_if1)
    x, ctx_1024, mask_BxSxS2_if1 = _rec_inputs()

    def _L0_attn_setup():
        import jax, jax.numpy as jnp
        import numpy as np
        D_MODEL = 256
        N_HEADS = 16
        HEAD_DIM = D_MODEL // N_HEADS
        WINDOW = 128
        PREFIX = 16
        B = 2
        S = 1024

        def _windowed_global_attention(q, k, v):
            Bb, H, S_, Dh = q.shape
            W, P = (WINDOW, PREFIX)
            C = S_ // W
            scale = 1.0 / np.sqrt(Dh).astype(np.float32)
            qc = q.reshape(Bb, H, C, W, Dh)
            kp = jnp.pad(k, ((0, 0), (0, 0), (W, 0), (0, 0)))
            vp = jnp.pad(v, ((0, 0), (0, 0), (W, 0), (0, 0)))
            tail_idx = jnp.arange(C)[:, None] * W + jnp.arange(2 * W)[None, :]
            kt = kp[:, :, tail_idx, :]
            vt = vp[:, :, tail_idx, :]
            kg = k[:, :, :P, :]
            vg = v[:, :, :P, :]
            sg = jnp.einsum('bhcqd,bhkd->bhcqk', qc, kg) * scale
            st = jnp.einsum('bhcqd,bhckd->bhcqk', qc, kt) * scale
            q_pos = jnp.arange(C)[:, None] * W + jnp.arange(W)[None, :]
            kt_pos = jnp.arange(C)[:, None] * W - W + jnp.arange(2 * W)[None, :]
            mg = jnp.arange(P)[None, None, :] <= q_pos[:, :, None]
            diff = q_pos[:, :, None] - kt_pos[:, None, :]
            mt = (diff >= 0) & (diff < W) & (kt_pos[:, None, :] >= P)
            neg = jnp.asarray(-1000000000.0, sg.dtype)
            scores = jnp.concatenate([jnp.where(mg[None, None], sg, neg), jnp.where(mt[None, None], st, neg)], axis=-1)
            attn = jax.nn.softmax(scores, axis=-1)
            vcat = jnp.concatenate([jnp.broadcast_to(vg[:, :, None], (Bb, H, C, P, Dh)), vt], axis=3)
            out = jnp.einsum('bhcqk,bhckd->bhcqd', attn, vcat)
            return out.reshape(Bb, H, S_, Dh)
        key = jax.random.key(seed)
        k1, k2, k3 = jax.random.split(key, 3)
        x = jax.random.normal(k1, (B, S, D_MODEL), dtype=jnp.float32)
        w_qkv = jax.random.normal(k2, (3 * D_MODEL, D_MODEL), dtype=jnp.float32) * 0.02
        w_out = jax.random.normal(k3, (D_MODEL, D_MODEL), dtype=jnp.float32) * 0.02
        return {'x': x, 'w_qkv': w_qkv, 'w_out': w_out}
    _L0_attn_all = _L0_attn_setup()
    _L0_attn_in = {k: v for k, v in _L0_attn_all.items() if k in ('w_qkv', 'w_out')}
    del _L0_attn_all

    def _L0_xattn_setup():
        import jax, jax.numpy as jnp
        import numpy as np
        HIDDEN = 256
        HEADS = 16
        D_K = HIDDEN // HEADS
        B, S = (2, 512)

        def _split_heads(x):
            b, s, _ = x.shape
            return x.reshape(b, s, HEADS, D_K).transpose(0, 2, 1, 3)
        key = jax.random.key(seed)
        ks = jax.random.split(key, 12)
        sc = 1.0 / np.sqrt(HIDDEN)
        return {'q': jax.random.normal(ks[0], (B, S, HIDDEN), jnp.float32), 'k': jax.random.normal(ks[1], (B, S, HIDDEN), jnp.float32), 'v': jax.random.normal(ks[2], (B, S, HIDDEN), jnp.float32), 'mask': jnp.ones((B, S, S), jnp.int32), 'Wq': jax.random.normal(ks[3], (HIDDEN, HIDDEN), jnp.float32) * sc, 'bq': jnp.zeros((HIDDEN,), jnp.float32), 'Wk': jax.random.normal(ks[4], (HIDDEN, HIDDEN), jnp.float32) * sc, 'bk': jnp.zeros((HIDDEN,), jnp.float32), 'Wv': jax.random.normal(ks[5], (HIDDEN, HIDDEN), jnp.float32) * sc, 'bv': jnp.zeros((HIDDEN,), jnp.float32), 'Wo': jax.random.normal(ks[6], (HIDDEN, HIDDEN), jnp.float32) * sc, 'bo': jnp.zeros((HIDDEN,), jnp.float32)}
    _L0_xattn_all = _L0_xattn_setup()
    _L0_xattn_in = {k: v for k, v in _L0_xattn_all.items() if k in ('Wq', 'bq', 'Wk', 'bk', 'Wv', 'bv', 'Wo', 'bo')}
    del _L0_xattn_all

    def _L0_ffn_setup():
        import jax, jax.numpy as jnp
        import numpy as np
        D = 256
        H = 4
        DF = 1024
        E = 8
        EPS = 1e-05

        def _layer_norm(x, g, b):
            mu = jnp.mean(x, axis=-1, keepdims=True)
            var = jnp.mean(jnp.square(x - mu), axis=-1, keepdims=True)
            return (x - mu) * jax.lax.rsqrt(var + EPS) * g + b

        def _mha(x, Wqkv, bqkv, Wo, bo):
            S, B, _ = x.shape
            hd = D // H
            qkv = x @ Wqkv.T + bqkv
            q, k, v = jnp.split(qkv, 3, axis=-1)
            to_heads = lambda t: t.reshape(S, B, H, hd).transpose(1, 2, 0, 3)
            q, k, v = (to_heads(q), to_heads(k), to_heads(v))
            scores = jnp.einsum('bhqd,bhkd->bhqk', q, k) * (1.0 / np.sqrt(hd))
            att = jax.nn.softmax(scores, axis=-1)
            o = jnp.einsum('bhqk,bhkd->bhqd', att, v)
            o = o.transpose(2, 0, 1, 3).reshape(S, B, D)
            return o @ Wo.T + bo

        def _moe(x, Wg, W1, b1, W2, b2):
            S, B, _ = x.shape
            xf = x.reshape(S * B, D)
            logits = xf @ Wg.T
            idx = jnp.argmax(logits, axis=-1)
            out = jnp.zeros_like(xf)
            for e in range(E):
                m = (idx == e)[:, None].astype(xf.dtype)
                h = jax.nn.relu(xf @ W1[e] + b1[e])
                out = out + m * (h @ W2[e] + b2[e])
            return out.reshape(S, B, D)
        key = jax.random.key(seed)
        ks = jax.random.split(key, 16)
        S, B = (128, 8)
        s = lambda k, shape, fan: jax.random.normal(k, shape, jnp.float32) * (1.0 / np.sqrt(fan))
        return {'x': jax.random.normal(ks[0], (S, B, D), jnp.float32), 'Wqkv': s(ks[1], (3 * D, D), D), 'bqkv': jnp.zeros((3 * D,), jnp.float32), 'Wo': s(ks[2], (D, D), D), 'bo': jnp.zeros((D,), jnp.float32), 'g1': jnp.ones((D,), jnp.float32), 'be1': jnp.zeros((D,), jnp.float32), 'g2': jnp.ones((D,), jnp.float32), 'be2': jnp.zeros((D,), jnp.float32), 'Wg': s(ks[3], (E, D), D), 'W1': s(ks[4], (E, D, DF), D), 'b1': jnp.zeros((E, DF), jnp.float32), 'W2': s(ks[5], (E, DF, D), DF), 'b2': jnp.zeros((E, D), jnp.float32)}
    _L0_ffn_all = _L0_ffn_setup()
    _L0_ffn_in = {k: v for k, v in _L0_ffn_all.items() if k in ('Wqkv', 'bqkv', 'Wo', 'bo', 'g1', 'be1', 'g2', 'be2', 'Wg', 'W1', 'b1', 'W2', 'b2')}
    del _L0_ffn_all
    return {'x': x, 'ctx_1024': ctx_1024, 'mask_BxSxS2_if1': mask_BxSxS2_if1, 'L0_attn_w_qkv': _L0_attn_in['w_qkv'], 'L0_attn_w_out': _L0_attn_in['w_out'], 'L0_xattn_Wq': _L0_xattn_in['Wq'], 'L0_xattn_bq': _L0_xattn_in['bq'], 'L0_xattn_Wk': _L0_xattn_in['Wk'], 'L0_xattn_bk': _L0_xattn_in['bk'], 'L0_xattn_Wv': _L0_xattn_in['Wv'], 'L0_xattn_bv': _L0_xattn_in['bv'], 'L0_xattn_Wo': _L0_xattn_in['Wo'], 'L0_xattn_bo': _L0_xattn_in['bo'], 'L0_ffn_Wqkv': _L0_ffn_in['Wqkv'], 'L0_ffn_bqkv': _L0_ffn_in['bqkv'], 'L0_ffn_Wo': _L0_ffn_in['Wo'], 'L0_ffn_bo': _L0_ffn_in['bo'], 'L0_ffn_g1': _L0_ffn_in['g1'], 'L0_ffn_be1': _L0_ffn_in['be1'], 'L0_ffn_g2': _L0_ffn_in['g2'], 'L0_ffn_be2': _L0_ffn_in['be2'], 'L0_ffn_Wg': _L0_ffn_in['Wg'], 'L0_ffn_W1': _L0_ffn_in['W1'], 'L0_ffn_b1': _L0_ffn_in['b1'], 'L0_ffn_W2': _L0_ffn_in['W2'], 'L0_ffn_b2': _L0_ffn_in['b2']}

def reference(x, ctx_1024, mask_BxSxS2_if1, L0_attn_w_qkv, L0_attn_w_out, L0_xattn_Wq, L0_xattn_bq, L0_xattn_Wk, L0_xattn_bk, L0_xattn_Wv, L0_xattn_bv, L0_xattn_Wo, L0_xattn_bo, L0_ffn_Wqkv, L0_ffn_bqkv, L0_ffn_Wo, L0_ffn_bo, L0_ffn_g1, L0_ffn_be1, L0_ffn_g2, L0_ffn_be2, L0_ffn_Wg, L0_ffn_W1, L0_ffn_b1, L0_ffn_W2, L0_ffn_b2):
    import jax
    import jax.numpy as jnp

    def _L0_attn_ref(x, w_qkv, w_out):
        import jax, jax.numpy as jnp
        import numpy as np
        D_MODEL = 256
        N_HEADS = 16
        HEAD_DIM = D_MODEL // N_HEADS
        WINDOW = 128
        PREFIX = 16
        B = 2
        S = 1024

        def _windowed_global_attention(q, k, v):
            Bb, H, S_, Dh = q.shape
            W, P = (WINDOW, PREFIX)
            C = S_ // W
            scale = 1.0 / np.sqrt(Dh).astype(np.float32)
            qc = q.reshape(Bb, H, C, W, Dh)
            kp = jnp.pad(k, ((0, 0), (0, 0), (W, 0), (0, 0)))
            vp = jnp.pad(v, ((0, 0), (0, 0), (W, 0), (0, 0)))
            tail_idx = jnp.arange(C)[:, None] * W + jnp.arange(2 * W)[None, :]
            kt = kp[:, :, tail_idx, :]
            vt = vp[:, :, tail_idx, :]
            kg = k[:, :, :P, :]
            vg = v[:, :, :P, :]
            sg = jnp.einsum('bhcqd,bhkd->bhcqk', qc, kg) * scale
            st = jnp.einsum('bhcqd,bhckd->bhcqk', qc, kt) * scale
            q_pos = jnp.arange(C)[:, None] * W + jnp.arange(W)[None, :]
            kt_pos = jnp.arange(C)[:, None] * W - W + jnp.arange(2 * W)[None, :]
            mg = jnp.arange(P)[None, None, :] <= q_pos[:, :, None]
            diff = q_pos[:, :, None] - kt_pos[:, None, :]
            mt = (diff >= 0) & (diff < W) & (kt_pos[:, None, :] >= P)
            neg = jnp.asarray(-1000000000.0, sg.dtype)
            scores = jnp.concatenate([jnp.where(mg[None, None], sg, neg), jnp.where(mt[None, None], st, neg)], axis=-1)
            attn = jax.nn.softmax(scores, axis=-1)
            vcat = jnp.concatenate([jnp.broadcast_to(vg[:, :, None], (Bb, H, C, P, Dh)), vt], axis=3)
            out = jnp.einsum('bhcqk,bhckd->bhcqd', attn, vcat)
            return out.reshape(Bb, H, S_, Dh)
        Bb, S_, Dm = x.shape
        qkv = x @ w_qkv.T
        q, k, v = jnp.split(qkv, 3, axis=-1)

        def heads(t):
            return t.reshape(Bb, S_, N_HEADS, HEAD_DIM).transpose(0, 2, 1, 3)
        q, k, v = (heads(q), heads(k), heads(v))
        o = _windowed_global_attention(q, k, v)
        o = o.transpose(0, 2, 1, 3).reshape(Bb, S_, Dm)
        return o @ w_out.T

    def _L0_xattn_ref(q, k, v, mask, Wq, bq, Wk, bk, Wv, bv, Wo, bo):
        import jax, jax.numpy as jnp
        import numpy as np
        HIDDEN = 256
        HEADS = 16
        D_K = HIDDEN // HEADS
        B, S = (2, 512)

        def _split_heads(x):
            b, s, _ = x.shape
            return x.reshape(b, s, HEADS, D_K).transpose(0, 2, 1, 3)
        qh = _split_heads(q @ Wq.T + bq)
        kh = _split_heads(k @ Wk.T + bk)
        vh = _split_heads(v @ Wv.T + bv)
        scores = jnp.einsum('bhqd,bhkd->bhqk', qh, kh) / np.sqrt(D_K).astype(np.float32)
        scores = jnp.where(mask[:, None, :, :] == 0, jnp.float32(-1000000000.0), scores)
        probs = jax.nn.softmax(scores, axis=-1)
        ctx = jnp.einsum('bhqk,bhkd->bhqd', probs, vh)
        concat = ctx.transpose(0, 2, 1, 3).reshape(q.shape[0], -1, HIDDEN)
        return concat @ Wo.T + bo

    def _L0_ffn_ref(x, Wqkv, bqkv, Wo, bo, g1, be1, g2, be2, Wg, W1, b1, W2, b2):
        import jax, jax.numpy as jnp
        import numpy as np
        D = 256
        H = 4
        DF = 1024
        E = 8
        EPS = 1e-05

        def _layer_norm(x, g, b):
            mu = jnp.mean(x, axis=-1, keepdims=True)
            var = jnp.mean(jnp.square(x - mu), axis=-1, keepdims=True)
            return (x - mu) * jax.lax.rsqrt(var + EPS) * g + b

        def _mha(x, Wqkv, bqkv, Wo, bo):
            S, B, _ = x.shape
            hd = D // H
            qkv = x @ Wqkv.T + bqkv
            q, k, v = jnp.split(qkv, 3, axis=-1)
            to_heads = lambda t: t.reshape(S, B, H, hd).transpose(1, 2, 0, 3)
            q, k, v = (to_heads(q), to_heads(k), to_heads(v))
            scores = jnp.einsum('bhqd,bhkd->bhqk', q, k) * (1.0 / np.sqrt(hd))
            att = jax.nn.softmax(scores, axis=-1)
            o = jnp.einsum('bhqk,bhkd->bhqd', att, v)
            o = o.transpose(2, 0, 1, 3).reshape(S, B, D)
            return o @ Wo.T + bo

        def _moe(x, Wg, W1, b1, W2, b2):
            S, B, _ = x.shape
            xf = x.reshape(S * B, D)
            logits = xf @ Wg.T
            idx = jnp.argmax(logits, axis=-1)
            out = jnp.zeros_like(xf)
            for e in range(E):
                m = (idx == e)[:, None].astype(xf.dtype)
                h = jax.nn.relu(xf @ W1[e] + b1[e])
                out = out + m * (h @ W2[e] + b2[e])
            return out.reshape(S, B, D)
        y = _layer_norm(x + _mha(x, Wqkv, bqkv, Wo, bo), g1, be1)
        z = _layer_norm(y + _moe(y, Wg, W1, b1, W2, b2), g2, be2)
        return z
    x = x + _L0_attn_ref(_layernorm(x, axis=-1), L0_attn_w_qkv, L0_attn_w_out)
    x = x + _L0_xattn_ref(_layernorm(x, axis=-1), ctx_1024, ctx_1024, mask_BxSxS2_if1, L0_xattn_Wq, L0_xattn_bq, L0_xattn_Wk, L0_xattn_bk, L0_xattn_Wv, L0_xattn_bv, L0_xattn_Wo, L0_xattn_bo)
    x = x + _L0_ffn_ref(_layernorm(x, axis=-1), L0_ffn_Wqkv, L0_ffn_bqkv, L0_ffn_Wo, L0_ffn_bo, L0_ffn_g1, L0_ffn_be1, L0_ffn_g2, L0_ffn_be2, L0_ffn_Wg, L0_ffn_W1, L0_ffn_b1, L0_ffn_W2, L0_ffn_b2)
    return x

_drawn_inputs = setup_inputs


def setup_inputs(seed=0):
    import zlib

    import numpy as np

    out = dict(_drawn_inputs(seed))
    spreads = {'L0_xattn_bq': (0.0, 0.1),
     'L0_xattn_bk': (0.0, 0.8),
     'L0_xattn_bv': (0.0, 0.1),
     'L0_xattn_bo': (0.0, 0.1),
     'L0_ffn_bqkv': (0.0, 0.1),
     'L0_ffn_bo': (0.0, 0.1),
     'L0_ffn_g1': (1.0, 0.2),
     'L0_ffn_be1': (0.0, 0.1),
     'L0_ffn_g2': (1.0, 0.2),
     'L0_ffn_be2': (0.0, 0.1),
     'L0_ffn_b1': (0.0, 0.277),
     'L0_ffn_b2': (0.0, 0.1)}
    factors = {}
    for name, (base, spread) in spreads.items():
        noise = np.random.default_rng([zlib.crc32(name.encode()), seed]).standard_normal(out[name].shape)
        drawn = base * np.exp(spread * noise) if base else spread * noise
        out[name] = jnp.asarray(drawn.astype(out[name].dtype))
    for name, factor in factors.items():
        out[name] = (out[name] * factor).astype(out[name].dtype)
    return out
```

```python
from contextlib import ExitStack

import concourse.bass as bass
from concourse import mybir

F32 = mybir.dt.float32
BF16 = mybir.dt.bfloat16
I32 = mybir.dt.int32
U32 = mybir.dt.uint32
ALU = mybir.AluOpType
ACT = mybir.ActivationFunctionType
AX = mybir.AxisListType

P = 128
B, S, D = 8, 512, 256
KD = D // P
TILES = S // P
HEADS, HD = 16, 16
WINDOW, PREFIX = 128, 16
CTX = 64
PAIRS = HEADS // 2
PARTS = 6
SPLIT_ROWS = PARTS * HD
Q_PARTS = (0, 0, 0, 1, 1, 2)
K_PARTS = (0, 1, 2, 0, 1, 0)
EPS = 1e-5
QK_SCALE = HD ** -0.5
GROUP = 4
GROUPS = HEADS // GROUP
HEAD_COLS = 3 * 256 + 128
GROUP_COLS = GROUP * HEAD_COLS + 256
NEG = -(2.0 ** 30)
NEG_MASK = -(2.0 ** 100)


class Signal:

    def __init__(self, ctx, nc, name, per, ahead=0):
        self.sem = ctx.enter_context(nc.semaphore(name))
        self.per, self.ahead = per, ahead

    def count(self, n, k):
        return n * self.per + (k + self.ahead)


def group_heads(g):
    return [8 * (g // 2) + 2 * j + g % 2 for j in range(GROUP)]


def wait_apart(eng, passed, sem, value):
    eng.wait_ge(sem, value)
    eng.sem_inc(passed.sem, 1)


def layernorm_statistics(nc, dve, x, stats, moments, passed, sig_stats, sig_moments, n):
    for c in range(TILES):
        nc.vector.bn_stats(stats[:, c, :], x[:, c, :]).then_inc(sig_stats.sem, 1)
    wait_apart(dve, passed, sig_stats.sem, sig_stats.count(n, TILES))
    for c in range(TILES):
        nc.vector.bn_aggr(moments[:, c, :], stats[:, c, :]).then_inc(sig_moments.sem, 1)


def layernorm_rstd(nc, pool, moments, veps, eps, half, rstd, sig_moments, sig_veps, sig_rstd, n):
    pool.wait_ge(sig_moments.sem, sig_moments.count(n, TILES))
    nc.gpsimd.tensor_tensor(veps[:, :], moments[:, :, 1], eps, ALU.add).then_inc(sig_veps.sem, 1)
    pool.wait_ge(sig_veps.sem, sig_veps.count(n, 1))
    nc.gpsimd.tensor_tensor(rstd[:, :], veps[:, :], half, ALU.pow).then_inc(sig_rstd.sem, 1)


def layernorm_apply(nc, dve, x, out, moments, rstd, sig_rstd, sig_done, n):
    dve.wait_ge(sig_rstd.sem, sig_rstd.count(n, 1))
    for c in range(TILES):
        nc.vector.tensor_scalar(out[:, c, :], x[:, c, :], moments[:, c, 0:1], rstd[:, c:c + 1],
                                ALU.subtract, ALU.mult).then_inc(sig_done.sem, 1)


QKV_FILLS = ["xT0", "xT1", "q0", "q1", "k0", "k1", "v0", "v1", "vg"]
FILLS = (["shiftT", "ctxT", "k2", "v2", "out0", "out1"] + QKV_FILLS
         + ["xT2_0", "xT2_1", "q2_0", "q2_1", "shiftT2", "out2_0", "out2_1"])
LAST_FILLS = [f for f in FILLS if f not in QKV_FILLS]


def attention_program(nc, t, mem):
    ctx = ExitStack()
    with ctx:
        def sb(name, shape, dt=F32):
            return ctx.enter_context(nc.sbuf_tensor(name, shape, dt))

        def signal(name, per, ahead=0):
            return Signal(ctx, nc, name, per, ahead)

        identf = sb("identf", [P, P])
        ident = sb("ident", [P, P], BF16)
        mask_qk = sb("mask_qk", [P, 2, 256], BF16)
        mask_kq = sb("mask_kq", [P, 640], BF16)
        sel = sb("sel", [P, HEADS, P], BF16)
        sel_prefix = sb("sel_prefix", [P, GROUPS, P], BF16)
        sel_pair = sb("sel_pair", [P, PAIRS, P], BF16)
        half_cols = sb("half_cols", [P, 2, 32])
        prefix_rows = sb("prefix_rows", [P, 2, D])
        ctx_rows = sb("ctx_rows", [P, D])
        head_rows = sb("head_rows", [P, 8])
        w_qkv = sb("w_qkv", [P, KD, 3 * D])
        w_out = sb("w_out", [P, KD, D])
        w_q2 = sb("w_q2", [P, KD, D])
        w_k2 = sb("w_k2", [P, KD, D])
        w_v2 = sb("w_v2", [P, KD, D])
        w_o2 = sb("w_o2", [P, KD, D])
        b_q2 = sb("b_q2", [P, KD])
        b_q2s = sb("b_q2s", [P, KD])
        b_k2 = sb("b_k2", [P, KD])
        b_v2 = sb("b_v2", [P, D])
        b_o2 = sb("b_o2", [P, D])
        half = sb("half", [P, TILES])
        eps = sb("eps", [P, TILES])
        x_in = sb("x_in", [P, TILES, D])
        x_res = sb("x_res", [P, TILES, D])
        stats = sb("stats", [P, TILES, 6])
        moments = sb("moments", [P, TILES, 2])
        veps = sb("veps", [P, TILES])
        rstd = sb("rstd", [P, TILES])
        stats2 = sb("stats2", [P, TILES, 6])
        moments2 = sb("moments2", [P, TILES, 2])
        veps2 = sb("veps2", [P, TILES])
        rstd2 = sb("rstd2", [P, TILES])
        xn = sb("xn", [P, TILES, D])
        xn2 = sb("xn2", [P, TILES, D])
        xT = sb("xT", [P, KD, S])
        xT2 = sb("xT2", [P, KD, S])
        parts = sb("parts", [P, 3, 4, S], BF16)
        rest = sb("rest", [P, 4, S])
        q_rows = sb("q_rows", [SPLIT_ROWS, HEADS, S], BF16)
        k_rows = sb("k_rows", [SPLIT_ROWS, HEADS, S], BF16)
        v_half = sb("v_half", [P, 2, TILES, D])
        v_prefix = sb("v_prefix", [P, 2, D])
        top = sb("top", [P, TILES, HEADS])
        top_prefix = sb("top_prefix", [P, 2, HEADS])
        top2 = sb("top2", [P, TILES, HEADS])
        shift = sb("shift", [P, TILES, P], BF16)
        shiftT = sb("shiftT", [P, S], BF16)
        shift2 = sb("shift2", [P, TILES, P], BF16)
        shiftT2 = sb("shiftT2", [P, S], BF16)
        probs = sb("probs", [P, 2, GROUP_COLS])
        rden = sb("rden", [P, S])
        oT = sb("oT", [P, KD, S])
        x1 = sb("x1", [P, TILES, D])
        x1b = sb("x1b", [P, TILES, D])
        ctx_in = sb("ctx_in", [2 * CTX, D])
        mask_in = sb("mask_in", [P, TILES, CTX], I32)
        mask_add = sb("mask_add", [P, TILES, 2, CTX], BF16)
        ctxT = sb("ctxT", [P, KD, 2, CTX])
        k2 = sb("k2", [P, KD, 8, CTX])
        v2 = sb("v2", [P, D])
        v2pair = sb("v2pair", [P, D])
        q2T = sb("q2T", [P, KD, S])
        x2 = sb("x2", [P, TILES, D])
        ps_max = mem["ps_a"]
        ps_exp = mem["ps_b"]
        ps_out = mem["ps_c"]
        ps_work = mem["ps_d"]

        consts_loaded = signal("consts_loaded", 0)
        consts_set = signal("consts_set", 0)
        x_loaded = signal("x_loaded", 16)
        xres_loaded = signal("xres_loaded", 16)
        ctx_loaded = signal("ctx_loaded", 32)
        mask_loaded = signal("mask_loaded", 16)
        ln_stats = signal("ln_stats", TILES)
        ln_moments = signal("ln_moments", TILES)
        ln_veps = signal("ln_veps", 1)
        ln_rstd = signal("ln_rstd", 1)
        ln_done = signal("ln_done", TILES)
        ln2_stats = signal("ln2_stats", TILES)
        ln2_moments = signal("ln2_moments", TILES)
        ln2_veps = signal("ln2_veps", 1)
        ln2_rstd = signal("ln2_rstd", 1)
        ln2_done = signal("ln2_done", TILES)
        work_full = signal("work_full", len(FILLS), len(QKV_FILLS))
        xT_ready = signal("xT_ready", KD)
        xT2_ready = signal("xT2_ready", KD)
        part_hi = signal("part_hi", 4)
        part_rest = signal("part_rest", 4)
        part_mid = signal("part_mid", 4)
        part_lo = signal("part_lo", 4)
        parts_stored = signal("parts_stored", 16 * 12)
        rows_loaded = signal("rows_loaded", 16 * 12)
        v_ready = signal("v_ready", 4)
        vprefix_ready = signal("vprefix_ready", 2)
        max_full = signal("max_full", 38)
        max_free = signal("max_free", 38, 2)
        top_joined = signal("top_joined", 1)
        shift_hi = signal("shift_hi", 2)
        shift_ready = signal("shift_ready", 2)
        shiftT_ready = signal("shiftT_ready", 2)
        exp_full = signal("exp_full", 44)
        exp_done = signal("exp_done", 44, 2)
        probs_used = signal("probs_used", 6, 2)
        out_recip = signal("out_recip", 4)
        out_free = signal("out_free", 4, 1)
        ctxT_ready = signal("ctxT_ready", 1)
        k2_ready = signal("k2_ready", 2)
        v2_biased = signal("v2_biased", 1)
        v2_ready = signal("v2_ready", 1)
        mask_ready = signal("mask_ready", 1)
        q2_ready = signal("q2_ready", 2)
        x1_ready = signal("x1_ready", 2)
        x1b_ready = signal("x1b_ready", 1)
        x2_ready = signal("x2_ready", 2, 2)
        x2_stored = signal("x2_stored", 16, 16)
        passed = signal("waits_passed_vector", 0)
        pool_passed = signal("waits_passed_pool", 0)

        def released(n, name):
            m = 0 if n is None else n + 1
            kind, k = name.rstrip("01"), int(name[-1]) if name[-1] in "01" else 0
            sig, batch_, count = {
                "shiftT": (shiftT_ready, n, 1), "shiftT2": (shiftT_ready, n, 2), "ctxT": (ctxT_ready, n, 1),
                "k2": (k2_ready, n, 2), "v2": (v2_biased, n, 1), "out": (x1_ready, n, k + 1),
                "xT": (xT_ready, m, k + 1), "q": (part_rest, m, k + 1), "k": (part_rest, m, k + 3),
                "v": (v_ready, m, 2 * k + 2), "vg": (vprefix_ready, m, 2), "xT2_": (xT2_ready, n, k + 1),
                "q2_": (q2_ready, n, k + 1), "out2_": (x2_ready, n, k + 1),
            }[kind]
            return sig.sem, sig.count(batch_, count)

        def work_place(n, name, last):
            order = QKV_FILLS if n is None else LAST_FILLS if last else FILLS
            j = order.index(name)
            return order, j, (j if n is None else j + len(QKV_FILLS)) % 2

        def work_claim(pe, n, name, last):
            order, j, bank = work_place(n, name, last)
            if j >= 2:
                pe.wait_ge(*released(n, order[j - 2]))
            elif n is not None:
                pe.wait_ge(*released(n - 1, FILLS[j - 2]))
            return ps_work[:, bank, :]

        def work_take(eng, n, name, last):
            _, j, bank = work_place(n, name, last)
            eng.wait_ge(work_full.sem, j + 1 if n is None else work_full.count(n, j + 1))
            return ps_work[:, bank, :]

        with nc.Block() as block:

            @block.sync
            def _(sp):
                n_const = 0

                def const(dst, src):
                    nonlocal n_const
                    sp.dma_start(dst, src).then_inc(consts_loaded.sem, 16)
                    n_const += 1

                def load_x(m):
                    sp.dma_start(x_in[:, :, :], t["x"][m].rearrange("(c p) d -> p c d", p=P)).then_inc(x_loaded.sem, 16)

                load_x(0)
                const(identf[:, :], t["c_identity"])
                for k in range(KD):
                    const(w_qkv[:, k, :], t["w_qkvT"][k * P:(k + 1) * P, :])
                const(ident[:, :], t["c_identity16"])
                const(mask_qk[:, :, :], t["c_mask_qk"])
                const(mask_kq[:, :], t["c_mask_kq"])
                const(sel[:, :, :], t["c_sel"])
                const(sel_prefix[:, :, :], t["c_sel_prefix"])
                const(sel_pair[:, :, :], t["c_sel_pair"])
                const(half_cols[:, :, :], t["c_half_cols"])
                const(prefix_rows[:, :, :], t["c_prefix_rows"])
                const(ctx_rows[:, :], t["c_ctx_rows"])
                const(head_rows[:, :], t["c_head_rows"])
                for dst, src in ((w_out, "w_outT"), (w_q2, "w_q2T"), (w_k2, "w_k2T"), (w_v2, "w_v2T"), (w_o2, "w_o2T")):
                    const(dst[:, :, :], t[src].rearrange("(k p) n -> p k n", p=P))
                const(b_q2[:, :], t["b_q2"])
                const(b_k2[:, :], t["b_k2"])
                const(b_v2[:, :], t["b_v2"].partition_broadcast(P))
                const(b_o2[:, :], t["b_o2"].partition_broadcast(P))
                assert n_const == N_CONST

                def store_parts(m):
                    for j in range(4):
                        for part, sig in enumerate((part_hi, part_mid, part_lo)):
                            sp.wait_ge(sig.sem, sig.count(m, j + 1))
                            sp.dma_start(t["qk_parts"][j // 2, part, (j % 2) * P:(j % 2 + 1) * P, :],
                                         parts[:, part, j, :]).then_inc(parts_stored.sem, 16)

                def load_rows(m):
                    sp.wait_ge(parts_stored.sem, parts_stored.count(m, 16 * 12))
                    for side, (dst, order) in enumerate(((q_rows, Q_PARTS), (k_rows, K_PARTS))):
                        for block_, part in enumerate(order):
                            sp.dma_start(dst[block_ * HD:(block_ + 1) * HD, :, :],
                                         t["qk_parts"][side, part].rearrange("(h r) s -> r h s", r=HD)
                                         ).then_inc(rows_loaded.sem, 16)

                def batch(n, last):
                    if not isinstance(n, int) or n > 0:
                        sp.wait_ge(x1_ready.sem, x1_ready.count(n, 0))
                        sp.wait_ge(ctxT_ready.sem, ctxT_ready.count(n, 0))
                        sp.wait_ge(mask_ready.sem, mask_ready.count(n, 0))
                    sp.dma_start(x_res[:, :, :], t["x"][n].rearrange("(c p) d -> p c d", p=P)).then_inc(xres_loaded.sem, 16)
                    for rep in range(2):
                        sp.dma_start(ctx_in[rep * CTX:(rep + 1) * CTX, :], t["ctx"][n]).then_inc(ctx_loaded.sem, 16)
                    sp.dma_start(mask_in[:, :, :], t["mask"][n].rearrange("(c p) k -> p c k", p=P)).then_inc(mask_loaded.sem, 16)
                    if not last:
                        sp.wait_ge(ln_done.sem, ln_done.count(n, TILES))
                        load_x(n + 1)
                        store_parts(n + 1)
                        load_rows(n + 1)
                    sp.wait_ge(x2_ready.sem, x2_ready.count(n, 2))
                    sp.dma_start(t["x2"][n].rearrange("(c p) d -> p c d", p=P), x2[:, :, :]).then_inc(x2_stored.sem, 16)

                store_parts(0)
                load_rows(0)
                batch(0, False)
                with sp.Fori(1, B - 1) as n:
                    batch(n, False)
                batch(B - 1, True)
                sp.wait_ge(x2_stored.sem, x2_stored.count(B, 0))

            @block.gpsimd
            def _(pool):
                nc.gpsimd.memset(half[:, :], -0.5).then_inc(consts_set.sem, 1)
                nc.gpsimd.memset(eps[:, :], EPS).then_inc(consts_set.sem, 1)
                nc.gpsimd.memset(v_half[:, :, :, :], 0.0).then_inc(consts_set.sem, 1)
                nc.gpsimd.memset(shift[:, :, :], 0.0).then_inc(consts_set.sem, 1)
                nc.gpsimd.memset(shift2[:, :, :], 0.0).then_inc(consts_set.sem, 1)
                pool.wait_ge(consts_set.sem, 4)
                nc.gpsimd.memset(shift[:, :, 2 * HEADS:2 * HEADS + 1], 1.0).then_inc(consts_set.sem, 1)
                pool.wait_ge(consts_loaded.sem, 16 * N_CONST)
                nc.gpsimd.tensor_scalar(b_q2s[:, :], b_q2[:, :], QK_SCALE, None, ALU.mult).then_inc(consts_set.sem, 1)

                def split_low_parts(m):
                    for j in range(4):
                        wait_apart(pool, pool_passed, part_rest.sem, part_rest.count(m, j + 1))
                        nc.gpsimd.tensor_copy(parts[:, 1, j, :], rest[:, j, :]).then_inc(part_mid.sem, 1)
                        pool.wait_ge(part_mid.sem, part_mid.count(m, j + 1))
                        nc.gpsimd.tensor_tensor(parts[:, 2, j, :], rest[:, j, :], parts[:, 1, j, :],
                                                ALU.subtract).then_inc(part_lo.sem, 1)

                def batch(n, last):
                    if not last:
                        layernorm_rstd(nc, pool, moments, veps, eps[:, :], half[:, :], rstd, ln_moments, ln_veps, ln_rstd, n + 1)
                    layernorm_rstd(nc, pool, moments2, veps2, eps[:, :], half[:, :], rstd2, ln2_moments, ln2_veps, ln2_rstd, n)
                    nc.gpsimd.tensor_tensor(x1b[:, :, :], x1[:, :, :],
                                            b_o2[:, :].unsqueeze(1).broadcast_to([P, TILES, D]),
                                            ALU.add).then_inc(x1b_ready.sem, 1)
                    if not last:
                        split_low_parts(n + 1)

                pool.wait_ge(consts_set.sem, 6)
                layernorm_rstd(nc, pool, moments, veps, eps[:, :], half[:, :], rstd, ln_moments, ln_veps, ln_rstd, 0)
                split_low_parts(0)
                with pool.Fori(0, B - 1) as n:
                    batch(n, False)
                batch(B - 1, True)

            @block.vector
            def _(dve):
                def ln_first(m):
                    dve.wait_ge(x_loaded.sem, x_loaded.count(m, 16))
                    layernorm_statistics(nc, dve, x_in, stats, moments, passed, ln_stats, ln_moments, m)
                    layernorm_apply(nc, dve, x_in, xn, moments, rstd, ln_rstd, ln_done, m)

                def split_rest(m, n, last):
                    for j, name in enumerate(("q0", "q1", "k0", "k1")):
                        ps = work_take(dve, n, name, last)
                        dve.wait_ge(part_hi.sem, part_hi.count(m, j + 1))
                        nc.vector.scalar_tensor_tensor(rest[:, j, :], ps, QK_SCALE if j < 2 else 1.0, parts[:, 0, j, :],
                                                       ALU.mult, ALU.subtract).then_inc(part_rest.sem, 1)

                def prefix_values(n, last):
                    ps = work_take(dve, n, "vg", last)
                    for odd in range(2):
                        nc.vector.tensor_tensor(v_prefix[:, odd, :], ps[:, 0:D], prefix_rows[:, odd, :],
                                                ALU.mult).then_inc(vprefix_ready.sem, 1)

                def maxima(n, first, count, out_of):
                    for f in range(first, first + count):
                        dve.wait_ge(max_full.sem, max_full.count(n, f + 1))
                        out, src = out_of(f - first, ps_max[:, f % 2, :])
                        nc.vector.tensor_reduce(out, src, AX.X, ALU.max).then_inc(max_free.sem, 1)

                def window_fill(f, ps):
                    if f < 4:
                        return top[:, 0, 4 * f:4 * f + 4], ps.rearrange("p (h k) -> p h k", h=4)
                    f -= 4
                    if f < 8:
                        c, j = 1, f
                    else:
                        c, j = 2 + (f - 8) // 9, (f - 8) % 9
                    if j == 8:
                        return top_prefix[:, c - 2, :], ps[:, 0:HEADS * PREFIX].rearrange("p (h k) -> p h k", h=HEADS)
                    return top[:, c, 2 * j:2 * j + 2], ps.rearrange("p (h k) -> p h k", h=2)

                def context_fill(f, ps):
                    c, tile = f // 2, f % 2
                    return top2[:, c, 8 * tile:8 * tile + 8], ps.rearrange("p (h k) -> p h k", h=8)

                def shift_parts(n, which, tops, out):
                    nc.vector.tensor_scalar(out[:, :, 0:HEADS], tops[:, :, :], -1.0, None,
                                            ALU.mult).then_inc(shift_hi.sem, 1)
                    dve.wait_ge(shift_hi.sem, shift_hi.count(n, which + 1))
                    nc.vector.scalar_tensor_tensor(out[:, :, HEADS:2 * HEADS], tops[:, :, :], -1.0,
                                                   out[:, :, 0:HEADS], ALU.mult, ALU.subtract
                                                   ).then_inc(shift_ready.sem, 1)

                def normalise(n, first):
                    for tile in range(KD):
                        k = first + tile
                        dve.wait_ge(probs_used.sem, probs_used.count(n, 2 * k + 2 if k < 2 else k + 3))
                        nc.vector.reciprocal(rden[:, :], ps_out[:, 1, :]).then_inc(out_recip.sem, 1)
                        dve.wait_ge(out_recip.sem, out_recip.count(n, k + 1))
                        nc.vector.tensor_tensor(oT[:, tile, :], ps_out[:, 0, :], rden[:, :],
                                                ALU.mult).then_inc(out_free.sem, 1)

                def residual(n, names, last, base, out, sig):
                    for i, name in enumerate(names):
                        ps = work_take(dve, n, name, last)
                        nc.vector.tensor_tensor(out[:, 2 * i:2 * i + 2, :], ps.rearrange("p (c d) -> p c d", c=2),
                                                base[:, 2 * i:2 * i + 2, :], ALU.add).then_inc(sig.sem, 1)

                def context_keys(n, last):
                    ps = work_take(dve, n, "k2", last)
                    for tile in range(KD):
                        nc.vector.scalar_tensor_tensor(
                            k2[:, tile, :, :], ps[:, tile * CTX:(tile + 1) * CTX].unsqueeze(1).broadcast_to([P, 8, CTX]),
                            b_k2[:, tile:tile + 1], head_rows[:, :].unsqueeze(2).broadcast_to([P, 8, CTX]),
                            ALU.add, ALU.mult).then_inc(k2_ready.sem, 1)
                    ps = work_take(dve, n, "v2", last)
                    nc.vector.tensor_tensor(v2[:, :], ps[:, 0:D], b_v2[:, :], ALU.add).then_inc(v2_biased.sem, 1)
                    dve.wait_ge(v2_biased.sem, v2_biased.count(n, 1))
                    nc.vector.tensor_tensor(v2pair[:, :], v2[:, :], ctx_rows[:, :], ALU.mult).then_inc(v2_ready.sem, 1)

                def batch(n, last):
                    maxima(n, 0, 30, window_fill)
                    dve.wait_ge(max_free.sem, max_free.count(n, 30))
                    nc.vector.tensor_tensor(top[:, 2:4, :], top[:, 2:4, :], top_prefix[:, :, :],
                                            ALU.max).then_inc(top_joined.sem, 1)
                    dve.wait_ge(top_joined.sem, top_joined.count(n, 1))
                    shift_parts(n, 0, top, shift)
                    if not last:
                        ln_first(n + 1)
                    dve.wait_ge(mask_loaded.sem, mask_loaded.count(n, 16))
                    nc.vector.tensor_scalar(mask_add[:, :, :, :],
                                            mask_in[:, :, :].unsqueeze(2).broadcast_to([P, TILES, 2, CTX]), 0, NEG_MASK,
                                            ALU.is_equal, ALU.mult).then_inc(mask_ready.sem, 1)
                    normalise(n, 0)
                    context_keys(n, last)
                    dve.wait_ge(xres_loaded.sem, xres_loaded.count(n, 16))
                    residual(n, ("out0", "out1"), last, x_res, x1, x1_ready)
                    dve.wait_ge(x1_ready.sem, x1_ready.count(n, 2))
                    layernorm_statistics(nc, dve, x1, stats2, moments2, passed, ln2_stats, ln2_moments, n)
                    layernorm_apply(nc, dve, x1, xn2, moments2, rstd2, ln2_rstd, ln2_done, n)
                    if not last:
                        split_rest(n + 1, n, last)
                        prefix_values(n, last)
                    maxima(n, 30, 8, context_fill)
                    dve.wait_ge(max_free.sem, max_free.count(n, 38))
                    shift_parts(n, 1, top2, shift2)
                    normalise(n, 2)
                    dve.wait_ge(x1b_ready.sem, x1b_ready.count(n, 1))
                    dve.wait_ge(x2_stored.sem, x2_stored.count(n, 0))
                    residual(n, ("out2_0", "out2_1"), last, x1b, x2, x2_ready)

                dve.wait_ge(consts_loaded.sem, 16 * N_CONST)
                dve.wait_ge(consts_set.sem, 6)
                dve.sem_inc(max_free.sem, 2)
                dve.sem_inc(out_free.sem, 1)
                dve.sem_inc(x2_stored.sem, 16)
                ln_first(0)
                split_rest(0, None, False)
                prefix_values(None, False)
                with dve.Fori(0, B - 1) as n:
                    batch(n, False)
                batch(B - 1, True)

            @block.scalar
            def _(act):
                def copy_out(n, name, last, sig, pieces):
                    ps = work_take(act, n, name, last)
                    for out, src in pieces(ps):
                        nc.scalar.activation(out, src, ACT.Copy).then_inc(sig.sem, 1)

                def qkv(m, n, last):
                    for k in range(KD):
                        copy_out(n, f"xT{k}", last, xT_ready,
                                 lambda ps: [(xT[:, k, :], ps)])
                    for j, name in enumerate(("q0", "q1", "k0", "k1")):
                        ps = work_take(act, n, name, last)
                        nc.scalar.activation(parts[:, 0, j, :], ps, ACT.Copy,
                                             scale=QK_SCALE if j < 2 else 1.0).then_inc(part_hi.sem, 1)
                    for i in range(2):
                        copy_out(n, f"v{i}", last, v_ready, lambda ps: [
                            (v_half[:, odd, 2 * i:2 * i + 2, :].rearrange("p c (i w) -> p c i w", w=32)[:, :, :, HD * odd:HD * odd + HD],
                             ps.rearrange("p (c i w) -> p c i w", c=2, w=32)[:, :, :, HD * odd:HD * odd + HD])
                            for odd in range(2)])

                def shift_rows(n, which, name, last, out):
                    ps = work_take(act, n, name, last)
                    nc.scalar.activation(out[:, :], ps.bitcast(BF16)[:, 0:S], ACT.Copy).then_inc(shiftT_ready.sem, 1)

                def exps(n, g, fills):
                    act.wait_ge(probs_used.sem, probs_used.count(n, g - 1))
                    for f, (lo, width) in fills:
                        act.wait_ge(exp_full.sem, exp_full.count(n, f + 1))
                        nc.scalar.activation(probs[:, g % 2, lo:lo + width], ps_exp[:, f % 2, 0:width],
                                             ACT.Exp).then_inc(exp_done.sem, 1)

                def batch(n, last):
                    shift_rows(n, 0, "shiftT", last, shiftT)
                    for g in range(GROUPS):
                        cols = [(HEAD_COLS * j + o, w) for j in range(GROUP) for o, w in ((0, 512), (512, 384))]
                        exps(n, g, list(enumerate(cols + [(GROUP * HEAD_COLS, 256)], 9 * g)))
                    copy_out(n, "ctxT", last, ctxT_ready, lambda ps: [
                        (ctxT[:, :, :, :].rearrange("p k r c -> p (k r c)"), ps[:, 0:KD * P])])
                    if not last:
                        qkv(n + 1, n, last)
                    for k in range(KD):
                        copy_out(n, f"xT2_{k}", last, xT2_ready,
                                 lambda ps: [(xT2[:, k, :], ps)])
                    for tile in range(KD):
                        ps = work_take(act, n, f"q2_{tile}", last)
                        nc.scalar.activation(q2T[:, tile, :], ps, ACT.Identity, scale=QK_SCALE,
                                             bias=b_q2s[:, tile:tile + 1]).then_inc(q2_ready.sem, 1)
                    shift_rows(n, 1, "shiftT2", last, shiftT2)
                    for tile in range(KD):
                        exps(n, 4 + tile, [(36 + 4 * tile + j, (512 * j, 512)) for j in range(4)])

                act.wait_ge(consts_set.sem, 6)
                act.wait_ge(consts_loaded.sem, 16 * N_CONST)
                act.sem_inc(exp_done.sem, 2)
                qkv(0, None, False)
                with act.Fori(0, B - 1) as n:
                    batch(n, False)
                batch(B - 1, True)

            @block.tensor
            def _(pe):
                def qkv(m, n, last):
                    for k in range(KD):
                        ps = work_claim(pe, n, f"xT{k}", last)
                        pe.wait_ge(ln_done.sem, ln_done.count(m, TILES))
                        for c in range(TILES):
                            mm = nc.tensor.transpose(ps[:, c * P:(c + 1) * P], xn[:, c, k * P:(k + 1) * P], identf[:, :])
                        mm.then_inc(work_full.sem, 1)
                    pe.wait_ge(xT_ready.sem, xT_ready.count(m, KD))
                    for j, name in enumerate(("q0", "q1", "k0", "k1")):
                        ps = work_claim(pe, n, name, last)
                        for k in range(KD):
                            mm = nc.tensor.matmul(ps, w_qkv[:, k, j * P:(j + 1) * P], xT[:, k, :],
                                                  start=(k == 0), stop=(k == KD - 1))
                        mm.then_inc(work_full.sem, 1)
                    for i in range(2):
                        ps = work_claim(pe, n, f"v{i}", last)
                        for c in (2 * i, 2 * i + 1):
                            for k in range(KD):
                                mm = nc.tensor.matmul(ps[:, (c % 2) * D:(c % 2 + 1) * D], xT[:, k, c * P:(c + 1) * P],
                                                      w_qkv[:, k, 2 * D:3 * D], start=(k == 0 and c % 2 == 0),
                                                      stop=(k == KD - 1), skip_group_check=True)
                        mm.then_inc(work_full.sem, 1)
                    ps = work_claim(pe, n, "vg", last)
                    for r in range(GROUP):
                        for k in range(KD):
                            mm = nc.tensor.matmul(ps[32 * r:32 * r + 32, 0:D], xT[:, k, 0:32], w_qkv[:, k, 2 * D:3 * D],
                                                  start=(k == 0), stop=(k == KD - 1), skip_group_check=True)
                    mm.then_inc(work_full.sem, 1)

                def max_claim(n, f):
                    pe.wait_ge(max_free.sem, max_free.count(n, f - 1))
                    return ps_max[:, f % 2, :]

                def window_scores(n):
                    pe.wait_ge(rows_loaded.sem, rows_loaded.count(n, 16 * 12))
                    f = 0
                    for c in range(TILES):
                        q0 = c * P
                        heads = 4 if c == 0 else 2
                        width = P if c == 0 else 2 * P
                        mask = mask_qk[:, 1, P:2 * P] if c == 0 else mask_qk[:, min(c, 2) - 1, :]
                        for j in range(HEADS // heads):
                            ps = max_claim(n, f)
                            nc.tensor.matmul(ps.rearrange("p (h k) -> p h k", h=heads), ident[:, :],
                                             mask.unsqueeze(1).broadcast_to([P, heads, width]),
                                             start=True, stop=False, skip_group_check=True)
                            for i in range(heads):
                                h = heads * j + i
                                mm = nc.tensor.matmul(ps[:, i * width:(i + 1) * width], q_rows[:, h, q0:q0 + P],
                                                      k_rows[:, h, q0 + P - width:q0 + P], start=False,
                                                      stop=True, skip_group_check=True)
                            mm.then_inc(max_full.sem, 1)
                            f += 1
                        if c >= 2:
                            ps = max_claim(n, f)
                            for h in range(HEADS):
                                mm = nc.tensor.matmul(ps[:, h * PREFIX:(h + 1) * PREFIX], q_rows[:, h, q0:q0 + P],
                                                      k_rows[:, h, 0:PREFIX], start=(h == 0), stop=True,
                                                      skip_group_check=True)
                            mm.then_inc(max_full.sem, 1)
                            f += 1

                def shift_transposes(n, which, name, last, src):
                    ps = work_claim(pe, n, name, last)
                    pe.wait_ge(shift_ready.sem, shift_ready.count(n, which + 1))
                    for c in range(TILES):
                        mm = nc.tensor.transpose(ps.bitcast(BF16)[:, c * P:(c + 1) * P], src[:, c, :], ident[:, :])
                    mm.then_inc(work_full.sem, 1)

                def exp_claim(n, f):
                    pe.wait_ge(exp_done.sem, exp_done.count(n, f - 1))
                    return ps_exp[:, f % 2, :]

                def window_shifted(n, g):
                    def add(ps, col, lhsT, rhs):
                        width = rhs.shape[-1]
                        return nc.tensor.matmul(ps[:, col:col + width], lhsT, rhs, start=False, stop=True,
                                                skip_group_check=True)
                    f = 9 * g
                    for h in group_heads(g):
                        for tiles, lo, width in (((0, 1), 0, 512), ((2, 3), 256, 384)):
                            ps = exp_claim(n, f)
                            nc.tensor.matmul(ps[:, 0:width], ident[:, :], mask_kq[:, lo:lo + width] if lo == 0 else mask_kq[:, 256:640],
                                             start=True, stop=False, skip_group_check=True)
                            for i, kt in enumerate(tiles):
                                q0, q1 = kt * P, min(kt + 2, TILES) * P
                                add(ps, 256 * i, sel[:, h, :], shiftT[:, q0:q1])
                                mm = add(ps, 256 * i, k_rows[:, h, kt * P:(kt + 1) * P], q_rows[:, h, q0:q1])
                            mm.then_inc(exp_full.sem, 1)
                            f += 1
                    ps = exp_claim(n, f)
                    nc.tensor.matmul(ps[:, 0:256], sel_prefix[:, g, :], shiftT[:, 256:512], start=True, stop=False,
                                     skip_group_check=True)
                    for j, h in enumerate(group_heads(g)):
                        mm = nc.tensor.matmul(ps[32 * j:32 * j + 32, 0:256], k_rows[:, h, 0:32], q_rows[:, h, 256:512],
                                              start=False, stop=True, skip_group_check=True)
                    mm.then_inc(exp_full.sem, 1)

                def out_claim(n, k):
                    pe.wait_ge(out_free.sem, out_free.count(n, k))

                def window_values(n, g):
                    tile, odd = g // 2, g % 2
                    pr = probs[:, g % 2, :]
                    if odd == 0:
                        out_claim(n, tile)
                    pe.wait_ge(exp_done.sem, exp_done.count(n, 9 * g + 9))
                    if g == 0:
                        pe.wait_ge(v_ready.sem, v_ready.count(n, 4))
                        pe.wait_ge(vprefix_ready.sem, vprefix_ready.count(n, 2))
                    for kt in range(TILES + 1):
                        for side in range(2):
                            for j in range(GROUP):
                                w = slice(32 * (4 * tile + j), 32 * (4 * tile + j) + 32)
                                if kt < TILES:
                                    q0, q1 = kt * P, min(kt + 2, TILES) * P
                                    lhsT = v_half[:, odd, kt, w] if side == 0 else half_cols[:, odd, :]
                                    rhs = pr[:, HEAD_COLS * j + 256 * kt:HEAD_COLS * j + 256 * kt + q1 - q0]
                                else:
                                    q0, q1 = 256, 512
                                    lhsT = v_prefix[:, odd, w] if side == 0 else prefix_rows[:, odd, 32 * j:32 * j + 32]
                                    rhs = pr[:, GROUP * HEAD_COLS:GROUP * HEAD_COLS + 256]
                                mm = nc.tensor.matmul(ps_out[32 * j:32 * j + 32, side, q0:q1], lhsT, rhs,
                                                      start=(kt == 0 and odd == 0), stop=True, skip_group_check=True)
                    mm.then_inc(probs_used.sem, 1)

                def output(n, names, last, w, k):
                    pe.wait_ge(out_free.sem, out_free.count(n, k))
                    for i, name in enumerate(names):
                        ps = work_claim(pe, n, name, last)
                        for c in (2 * i, 2 * i + 1):
                            for tile in range(KD):
                                mm = nc.tensor.matmul(ps[:, (c % 2) * D:(c % 2 + 1) * D], oT[:, tile, c * P:(c + 1) * P],
                                                      w[:, tile, :], start=(tile == 0 and c % 2 == 0),
                                                      stop=(tile == KD - 1), skip_group_check=True)
                        mm.then_inc(work_full.sem, 1)

                def context_kv(n, last):
                    ps = work_claim(pe, n, "ctxT", last)
                    pe.wait_ge(ctx_loaded.sem, ctx_loaded.count(n, 32))
                    for k in range(KD):
                        mm = nc.tensor.transpose(ps[:, k * P:(k + 1) * P], ctx_in[:, k * P:(k + 1) * P], identf[:, :])
                    mm.then_inc(work_full.sem, 1)
                    ps = work_claim(pe, n, "k2", last)
                    pe.wait_ge(ctxT_ready.sem, ctxT_ready.count(n, 1))
                    for tile in range(KD):
                        for k in range(KD):
                            mm = nc.tensor.matmul(ps[:, tile * CTX:(tile + 1) * CTX], w_k2[:, k, tile * P:(tile + 1) * P],
                                                  ctxT[:, k, 0, :], start=(tile == 0 and k == 0), stop=(k == KD - 1),
                                                  skip_group_check=True)
                    mm.then_inc(work_full.sem, 1)
                    ps = work_claim(pe, n, "v2", last)
                    for k in range(KD):
                        mm = nc.tensor.matmul(ps[:, 0:D], ctxT[:, k, :, :].rearrange("p r c -> p (r c)"), w_v2[:, k, :],
                                              start=(k == 0), stop=(k == KD - 1))
                    mm.then_inc(work_full.sem, 1)

                def context_attention(n, last):
                    for k in range(KD):
                        ps = work_claim(pe, n, f"xT2_{k}", last)
                        pe.wait_ge(ln2_done.sem, ln2_done.count(n, TILES))
                        for c in range(TILES):
                            mm = nc.tensor.transpose(ps[:, c * P:(c + 1) * P], xn2[:, c, k * P:(k + 1) * P], identf[:, :])
                        mm.then_inc(work_full.sem, 1)
                    pe.wait_ge(xT2_ready.sem, xT2_ready.count(n, KD))
                    for tile in range(KD):
                        ps = work_claim(pe, n, f"q2_{tile}", last)
                        for k in range(KD):
                            mm = nc.tensor.matmul(ps, w_q2[:, k, tile * P:(tile + 1) * P], xT2[:, k, :],
                                                  start=(k == 0), stop=(k == KD - 1))
                        mm.then_inc(work_full.sem, 1)
                    pe.wait_ge(mask_ready.sem, mask_ready.count(n, 1))
                    pe.wait_ge(k2_ready.sem, k2_ready.count(n, 2))
                    pe.wait_ge(q2_ready.sem, q2_ready.count(n, 2))
                    for c in range(TILES):
                        for tile in range(KD):
                            ps = max_claim(n, 30 + 2 * c + tile)
                            nc.tensor.matmul(ps.rearrange("p (h k) -> p h k", h=8), ident[:, :],
                                             mask_add[:, c, 0, :].unsqueeze(1).broadcast_to([P, 8, CTX]),
                                             start=True, stop=False, skip_group_check=True)
                            nc.tensor.matmul(ps, q2T[:, tile, c * P:(c + 1) * P],
                                             k2[:, tile, :, :].rearrange("p h k -> p (h k)"),
                                             start=False, stop=True, skip_group_check=True).then_inc(max_full.sem, 1)
                    shift_transposes(n, 1, "shiftT2", last, shift2)
                    for i in range(PAIRS):
                        tile = i // 4
                        ps = exp_claim(n, 36 + i)
                        for c in range(TILES):
                            nc.tensor.matmul(ps[:, c * P:(c + 1) * P], mask_add[:, c, :, :].rearrange("p r k -> p (r k)"),
                                             ident[:, :], start=(c == 0), stop=False, skip_group_check=True)
                        nc.tensor.matmul(ps, k2[:, tile, 2 * (i % 4):2 * (i % 4) + 2, :].rearrange("p h k -> p (h k)"),
                                         q2T[:, tile, :], start=False, stop=False, skip_group_check=True)
                        if i == 0:
                            pe.wait_ge(shiftT_ready.sem, shiftT_ready.count(n, 2))
                        nc.tensor.matmul(ps, sel_pair[:, i, :], shiftT2[:, :], start=False, stop=True,
                                         skip_group_check=True).then_inc(exp_full.sem, 1)
                    pe.wait_ge(v2_ready.sem, v2_ready.count(n, 1))
                    for tile in range(KD):
                        out_claim(n, 2 + tile)
                        pe.wait_ge(exp_done.sem, exp_done.count(n, 36 + 4 * tile + 4))
                        for side in range(2):
                            for j in range(GROUP):
                                w = slice(32 * (4 * tile + j), 32 * (4 * tile + j) + 32)
                                mm = nc.tensor.matmul(ps_out[32 * j:32 * j + 32, side, :],
                                                      v2pair[:, w] if side == 0 else ctx_rows[:, 0:32],
                                                      probs[:, tile, 512 * j:512 * j + 512],
                                                      start=True, stop=True, skip_group_check=True)
                        mm.then_inc(probs_used.sem, 1)
                    output(n, ("out2_0", "out2_1"), last, w_o2, 4)

                def batch(n, last):
                    window_scores(n)
                    shift_transposes(n, 0, "shiftT", last, shift)
                    pe.wait_ge(shiftT_ready.sem, shiftT_ready.count(n, 1))
                    window_shifted(n, 0)
                    for g in range(1, GROUPS):
                        window_shifted(n, g)
                        window_values(n, g - 1)
                    window_values(n, GROUPS - 1)
                    context_kv(n, last)
                    output(n, ("out0", "out1"), last, w_out, 2)
                    if not last:
                        qkv(n + 1, n, last)
                    context_attention(n, last)

                pe.wait_ge(consts_loaded.sem, 16 * N_CONST)
                pe.sem_inc(probs_used.sem, 2)
                pe.sem_inc(x2_ready.sem, 2)
                qkv(0, None, False)
                pe.wait_ge(v_ready.sem, 4)
                pe.wait_ge(vprefix_ready.sem, 2)
                with pe.Fori(0, B - 1) as n:
                    batch(n, False)
                batch(B - 1, True)


N_CONST = 1 + KD + 10 + 5 + 4
REGION = B * S + P
SPARE_TILES = 10
ROW = 2 * D + 4
NO_TOKEN = float(1 << 20)
E, DF = 8, 1024
KF = DF // P
MH, MD = 4, 64
M_SCALE = MD ** -0.5
POS = 16
NGROUPS = S // (TILES * POS)
STEPS = B * S // P + E
TABLE = STEPS + 2

MIX_QKV = ["xT0", "xT1", "q0", "q1", "k0", "k1", "v0", "v1"]
MIX_FILLS = ["shiftT", "out0", "out1"] + MIX_QKV + ["yT0", "yT1", "logits", "ranks", "totals"]
MIX_LAST = [f for f in MIX_FILLS if f not in MIX_QKV]


def mixing_program(nc, t, mem, keep):
    ctx = ExitStack()
    with ctx:
        def sb(name, shape, dt=F32):
            return ctx.enter_context(nc.sbuf_tensor(name, shape, dt))

        def signal(name, per, ahead=0):
            return Signal(ctx, nc, name, per, ahead)

        identf = sb("m_identf", [P, P])
        ident = sb("m_ident", [P, P], BF16)
        mask_pos = sb("mask_pos", [P, P], BF16)
        sel_head = sb("sel_head", [P, MH, P], BF16)
        before = sb("before", [P, P], BF16)
        ones16 = sb("ones16", [P, P], BF16)
        ones64 = sb("ones64", [P, MD])
        head_half = sb("head_half", [P, 2])
        descending = sb("descending", [P, E])
        region0 = sb("region0", [P, E])
        token0 = sb("token0", [P, TILES])
        row_in_tile = sb("row_in_tile", [P, 1])
        tile_rows = sb("tile_rows", [P, 64])
        upto = sb("upto", [P, E * E])
        steps = sb("steps", [P, TABLE])
        w_qkv = sb("m_w_qkv", [P, KD, 3 * D])
        w_o = sb("m_w_o", [P, KD, D])
        w_g = sb("m_w_g", [P, KD, E])
        b_q = sb("m_b_q", [P, KD])
        b_qs = sb("m_b_qs", [P, KD])
        b_k = sb("m_b_k", [P, KD])
        b_v = sb("m_b_v", [P, D])
        b_o = sb("m_b_o", [P, D])
        g1 = sb("m_g1", [P, D])
        be1 = sb("m_be1", [P, D])
        half = sb("m_half", [P, TILES])
        eps = sb("m_eps", [P, TILES])
        x_in = sb("m_x_in", [P, TILES, D])
        stats = sb("m_stats", [P, TILES, 6])
        moments = sb("m_moments", [P, TILES, 2])
        veps = sb("m_veps", [P, TILES])
        rstd = sb("m_rstd", [P, TILES])
        stats1 = sb("m_stats1", [P, TILES, 6])
        moments1 = sb("m_moments1", [P, TILES, 2])
        veps1 = sb("m_veps1", [P, TILES])
        rstd1 = sb("m_rstd1", [P, TILES])
        xn = sb("m_xn", [P, TILES, D])
        xnb = sb("m_xnb", [P, TILES, D])
        xT = sb("m_xT", [P, KD, S])
        qT = sb("m_qT", [P, KD, S])
        kT = sb("m_kT", [P, MH, S])
        v = sb("m_v", [P, TILES, D])
        top = sb("m_top", [P, TILES, MH])
        shift = sb("m_shift", [P, TILES, P], BF16)
        shiftT = sb("m_shiftT", [P, S], BF16)
        probs = sb("m_probs", [P, 2, MH * P])
        rden = sb("m_rden", [P, 2, D])
        oT = sb("m_oT", [P, KD, S])
        mixed = sb("m_mixed", [P, TILES, D])
        rows = sb("m_rows", [P, TILES, ROW])
        yT = oT
        best = sb("m_best", [P, TILES])
        is_best = sb("m_is_best", [P, TILES, E])
        order = sb("m_order", [P, TILES, E])
        first = sb("m_first", [P, TILES])
        chosen = sb("m_chosen", [P, TILES, E], BF16)
        place = sb("m_place", [P, TILES, E])
        own_place = sb("m_own_place", [P, TILES, E])
        slot_f = sb("m_slot_f", [P, TILES])
        slot = sb("m_slot", [P, TILES], U32)
        next_row = sb("m_next_row", [P, 2, E])
        token = sb("m_token", [P, TILES])
        filler = sb("m_filler", [P, ROW])
        filler_slot_f = sb("m_filler_slot_f", [P, E])
        filler_slot = sb("m_filler_slot", [P, E], U32)
        counts = sb("m_counts", [P, E])
        tiles_of = sb("m_tiles_of", [P, E])
        tiles_upto_all = sb("m_tiles_upto_all", [P, E, E])
        tiles_upto = sb("m_tiles_upto", [P, E])
        expert_f = sb("m_expert_f", [P, TABLE])
        step0 = sb("m_step0", [P, TABLE])
        row_a = sb("m_row_a", [P, TABLE])
        row_b = sb("m_row_b", [P, TABLE])
        row_f = sb("m_row_f", [P, TABLE])
        tile_need = probs[:, 0, :].rearrange("p (e k) -> p e k", e=E)
        gone = probs[:, 1, 0:TABLE * E].rearrange("p (j e) -> p j e", e=E)
        passed_tiles = qT[:, 0, 0:TABLE * E].rearrange("p (j e) -> p j e", e=E)
        ps_max, ps_exp, ps_out, ps_work = mem["ps_a"], mem["ps_b"], mem["ps_c"], mem["ps_d"]

        consts_loaded = signal("m_consts_loaded", 0)
        consts_set = signal("m_consts_set", 0)
        x_loaded = signal("m_x_loaded", 16 * B)
        rows_loaded = signal("m_rows_loaded", 16 * B)
        ln_stats = signal("m_ln_stats", TILES)
        ln_moments = signal("m_ln_moments", TILES)
        ln_veps = signal("m_ln_veps", 1)
        ln_rstd = signal("m_ln_rstd", 1)
        ln_done = signal("m_ln_done", TILES)
        xnb_ready = signal("m_xnb_ready", 1)
        ln1_stats = signal("m_ln1_stats", TILES)
        ln1_moments = signal("m_ln1_moments", TILES)
        ln1_veps = signal("m_ln1_veps", 1)
        ln1_rstd = signal("m_ln1_rstd", 1)
        ln1_scaled = signal("m_ln1_scaled", TILES)
        y_ready = signal("m_y_ready", TILES)
        work_full = signal("m_work_full", len(MIX_FILLS), len(MIX_QKV))
        xT_ready = signal("m_xT_ready", KD)
        q_ready = signal("m_q_ready", KD)
        k_ready = signal("m_k_ready", MH)
        v_ready = signal("m_v_ready", 2)
        max_full = signal("m_max_full", TILES)
        max_free = signal("m_max_free", TILES, 2)
        shift_hi = signal("m_shift_hi", 1)
        shift_ready = signal("m_shift_ready", 1)
        shiftT_ready = signal("m_shiftT_ready", 1)
        exp_full = signal("m_exp_full", TILES)
        exp_done = signal("m_exp_done", TILES, 2)
        probs_used = signal("m_probs_used", TILES, 2)
        recip_done = signal("m_recip_done", TILES)
        out_free = signal("m_out_free", TILES, 2)
        mixed_ready = signal("m_mixed_ready", 2)
        yT_ready = signal("m_yT_ready", KD)
        best_ready = signal("m_best_ready", 1)
        is_best_ready = signal("m_is_best_ready", 1)
        order_ready = signal("m_order_ready", 1)
        first_ready = signal("m_first_ready", 1)
        chosen_ready = signal("m_chosen_ready", 1)
        place_ready = signal("m_place_ready", 1)
        own_place_ready = signal("m_own_place_ready", 1)
        slot_f_ready = signal("m_slot_f_ready", 1)
        slot_ready = signal("m_slot_ready", 1)
        next_row_ready = signal("m_next_row_ready", 1, 1)
        next_row_kept = signal("m_next_row_kept", 1)
        token_written = signal("m_token_written", 1)
        token_next = signal("m_token_next", 1, 1)
        rows_sent = signal("m_rows_sent", 16 * TILES, 16)
        filler_sent = signal("m_filler_sent", 0)
        tables = signal("m_tables", 0)
        weights_loaded = signal("m_weights_loaded", 0)
        passed = signal("m_waits_passed_vector", 0)
        pool_passed = signal("m_waits_passed_pool", 0)

        def released(n, name):
            m = 0 if n is None else n + 1
            kind, k = name.rstrip("01"), int(name[-1]) if name[-1] in "01" else 0
            sig, group, count = {
                "shiftT": (shiftT_ready, n, 1), "out": (mixed_ready, n, k + 1), "xT": (xT_ready, m, k + 1),
                "q": (q_ready, m, k + 1), "k": (k_ready, m, 2 * k + 2), "v": (v_ready, m, k + 1),
                "yT": (yT_ready, n, k + 1), "logits": (is_best_ready, n, 1), "ranks": (place_ready, n, 1),
                "totals": (next_row_ready, n, 1),
            }[kind]
            return sig.sem, sig.count(group, count)

        def work_place(n, name, last):
            fills = MIX_QKV if n is None else MIX_LAST if last else MIX_FILLS
            j = fills.index(name)
            return fills, j, j % 2

        def work_claim(pe, n, name, last):
            fills, j, bank = work_place(n, name, last)
            if j >= 2:
                pe.wait_ge(*released(n, fills[j - 2]))
            elif n is not None and j == 1:
                pe.wait_ge(*released(n - 1, "totals"))
            elif n is not None:
                pe.wait_ge(*released(n - 1, "totals"))
            return ps_work[:, bank, :]

        def work_take(eng, n, name, last):
            _, j, bank = work_place(n, name, last)
            eng.wait_ge(work_full.sem, j + 1 if n is None else work_full.count(n, j + 1))
            return ps_work[:, bank, :]

        with nc.Block() as block:

            @block.sync
            def _(sp):
                n_const = 0

                def const(dst, src):
                    nonlocal n_const
                    sp.dma_start(dst, src).then_inc(consts_loaded.sem, 16)
                    n_const += 1

                def load_x(m):
                    for s in range(B):
                        sp.dma_start(x_in[s * POS:(s + 1) * POS, :, :],
                                     t["x2_groups"][m, s].rearrange("(c i) d -> i c d", i=POS)).then_inc(x_loaded.sem, 16)

                def load_rows(m):
                    for s in range(B):
                        sp.dma_start(rows[s * POS:(s + 1) * POS, :, D:2 * D],
                                     t["x2_groups"][m, s].rearrange("(c i) d -> i c d", i=POS)).then_inc(rows_loaded.sem, 16)

                load_x(0)
                for dst, src in ((identf, "c_identity"), (ident, "c_identity16"), (mask_pos, "c_mask_pos"),
                                 (before, "c_before"), (head_half, "c_head_half"), (descending, "c_descending"),
                                 (region0, "c_region0"), (token0, "c_token0"), (row_in_tile, "c_row_in_tile"),
                                 (tile_rows, "c_tile_rows"), (upto, "c_upto"), (steps, "c_steps"),
                                 (b_q, "m_b_q"), (b_k, "m_b_k")):
                    const(dst[:, :], t[src])
                const(sel_head[:, :, :], t["c_sel_head"])
                for dst, src in ((w_qkv, "m_w_qkvT"), (w_o, "m_w_oT"), (w_g, "m_w_gT")):
                    const(dst[:, :, :], t[src].rearrange("(k p) n -> p k n", p=P))
                for dst, src in ((b_v, "m_b_v"), (b_o, "m_b_o"), (g1, "m_g1"), (be1, "m_be1")):
                    const(dst[:, :], t[src].partition_broadcast(P))
                assert n_const == MIX_CONST
                sp.wait_ge(consts_set.sem, 8)
                for i in range(1, SPARE_TILES):
                    sp.dma_start(t["sorted"][E * REGION + i * P:E * REGION + (i + 1) * P, :],
                                 filler[:, :]).then_inc(filler_sent.sem, 16)

                def group(n, last):
                    if not last:
                        sp.wait_ge(ln_done.sem, ln_done.count(n, TILES))
                        load_x(n + 1)
                    sp.wait_ge(rows_sent.sem, rows_sent.count(n, 0))
                    load_rows(n)

                with sp.Fori(0, NGROUPS - 1) as n:
                    group(n, False)
                group(NGROUPS - 1, True)
                sp.wait_ge(filler_sent.sem, 16 * (SPARE_TILES - 1))

            @block.gpsimd
            def _(pool):
                nc.gpsimd.memset(half[:, :], -0.5).then_inc(consts_set.sem, 1)
                nc.gpsimd.memset(eps[:, :], EPS).then_inc(consts_set.sem, 1)
                nc.gpsimd.memset(shift[:, :, :], 0.0).then_inc(consts_set.sem, 1)
                nc.gpsimd.memset(ones16[:, :], 1.0).then_inc(consts_set.sem, 1)
                nc.gpsimd.memset(ones64[:, :], 1.0).then_inc(consts_set.sem, 1)
                nc.gpsimd.memset(rows[:, :, 2 * D:ROW], 0.0).then_inc(consts_set.sem, 1)
                nc.gpsimd.memset(filler[:, :], 0.0).then_inc(consts_set.sem, 1)
                pool.wait_ge(consts_set.sem, 7)
                nc.gpsimd.memset(filler[:, 2 * D:2 * D + 1], NO_TOKEN).then_inc(consts_set.sem, 1)
                pool.wait_ge(consts_loaded.sem, 16 * MIX_CONST)
                nc.gpsimd.tensor_scalar(b_qs[:, :], b_q[:, :], M_SCALE, None, ALU.mult).then_inc(consts_set.sem, 1)
                nc.gpsimd.tensor_copy(token[:, :], token0[:, :]).then_inc(token_next.sem, 1)
                pool.wait_ge(consts_set.sem, 9)
                pool.dma_start(t["sorted"][E * REGION:E * REGION + P, :], filler[:, :]).then_inc(rows_sent.sem, 16)

                def ln_first(m):
                    layernorm_rstd(nc, pool, moments, veps, eps[:, :], half[:, :], rstd, ln_moments, ln_veps, ln_rstd, m)
                    pool.wait_ge(ln_done.sem, ln_done.count(m, TILES))
                    if not (isinstance(m, int) and m == 0):
                        pool.wait_ge(mixed_ready.sem, mixed_ready.count(m - 1, 2))
                    nc.gpsimd.tensor_tensor(xnb[:, :, :], xn[:, :, :], b_o[:, :].unsqueeze(1).broadcast_to([P, TILES, D]),
                                            ALU.add).then_inc(xnb_ready.sem, 1)

                def group(n, last):
                    wait_apart(pool, pool_passed, rows_sent.sem, rows_sent.count(n, 0))
                    wait_apart(pool, pool_passed, token_next.sem, token_next.count(n, 0))
                    nc.gpsimd.tensor_copy(rows[:, :, 2 * D], token[:, :]).then_inc(token_written.sem, 1)
                    wait_apart(pool, pool_passed, token_written.sem, token_written.count(n, 1))
                    nc.gpsimd.tensor_scalar(token[:, :], token[:, :], float(TILES * POS), None,
                                            ALU.add).then_inc(token_next.sem, 1)
                    layernorm_rstd(nc, pool, moments1, veps1, eps[:, :], half[:, :], rstd1, ln1_moments, ln1_veps, ln1_rstd, n)
                    if not last:
                        ln_first(n + 1)
                    wait_apart(pool, pool_passed, rows_loaded.sem, rows_loaded.count(n, 16 * B))
                    wait_apart(pool, pool_passed, y_ready.sem, y_ready.count(n, TILES))
                    wait_apart(pool, pool_passed, slot_ready.sem, slot_ready.count(n, 1))
                    for c in range(TILES):
                        nc.gpsimd.indirect_dma_start(
                            out=t["sorted"], out_offset=bass.IndirectOffsetOnAxis(ap=slot[:, c:c + 1], axis=0),
                            in_=rows[:, c, :], in_offset=None).then_inc(rows_sent.sem, 16)

                ln_first(0)
                with pool.Fori(0, NGROUPS - 1) as n:
                    group(n, False)
                group(NGROUPS - 1, True)
                pool.wait_ge(tables.sem, 2)
                for e in range(E):
                    nc.gpsimd.indirect_dma_start(
                        out=t["sorted"], out_offset=bass.IndirectOffsetOnAxis(ap=filler_slot[:, e:e + 1], axis=0),
                        in_=filler[:, :], in_offset=None).then_inc(rows_sent.sem, 16)
                pool.wait_ge(rows_sent.sem, rows_sent.count(NGROUPS, 16 * E))

            @block.vector
            def _(dve):
                def ln_first(m):
                    dve.wait_ge(x_loaded.sem, x_loaded.count(m, 16 * B))
                    layernorm_statistics(nc, dve, x_in, stats, moments, passed, ln_stats, ln_moments, m)
                    if not (isinstance(m, int) and m == 0):
                        dve.wait_ge(xnb_ready.sem, xnb_ready.count(m, 0))
                    layernorm_apply(nc, dve, x_in, xn, moments, rstd, ln_rstd, ln_done, m)

                def keys(m, n, last):
                    for tile in range(KD):
                        ps = work_take(dve, n, f"k{tile}", last)
                        for odd in range(2):
                            nc.vector.tensor_scalar(kT[:, 2 * tile + odd, :], ps, b_k[:, tile:tile + 1],
                                                    head_half[:, odd:odd + 1], ALU.add, ALU.mult).then_inc(k_ready.sem, 1)
                    for i in range(2):
                        ps = work_take(dve, n, f"v{i}", last)
                        nc.vector.tensor_tensor(v[:, 2 * i:2 * i + 2, :], ps.rearrange("p (c d) -> p c d", c=2),
                                                b_v[:, :].unsqueeze(1).broadcast_to([P, 2, D]),
                                                ALU.add).then_inc(v_ready.sem, 1)

                def attention(n):
                    for c in range(TILES):
                        dve.wait_ge(max_full.sem, max_full.count(n, c + 1))
                        nc.vector.tensor_reduce(top[:, c, :], ps_max[:, c % 2, :].rearrange("p (h k) -> p h k", h=MH),
                                                AX.X, ALU.max).then_inc(max_free.sem, 1)
                    dve.wait_ge(max_free.sem, max_free.count(n, TILES))
                    nc.vector.tensor_scalar(shift[:, :, 0:MH], top[:, :, :], -1.0, None, ALU.mult).then_inc(shift_hi.sem, 1)
                    dve.wait_ge(shift_hi.sem, shift_hi.count(n, 1))
                    nc.vector.scalar_tensor_tensor(shift[:, :, MH:2 * MH], top[:, :, :], -1.0, shift[:, :, 0:MH],
                                                   ALU.mult, ALU.subtract).then_inc(shift_ready.sem, 1)
                    for c in range(TILES):
                        dve.wait_ge(probs_used.sem, probs_used.count(n, c + 1))
                        nc.vector.reciprocal(rden[:, c % 2, :], ps_out[:, c % 2, D:2 * D]).then_inc(recip_done.sem, 1)
                        dve.wait_ge(recip_done.sem, recip_done.count(n, c + 1))
                        nc.vector.tensor_tensor(oT[:, :, c * P:(c + 1) * P],
                                                ps_out[:, c % 2, 0:D].rearrange("p (t q) -> p t q", t=KD),
                                                rden[:, c % 2, :].rearrange("p (t q) -> p t q", t=KD),
                                                ALU.mult).then_inc(out_free.sem, 1)

                def post_norm(n, last):
                    dve.wait_ge(xnb_ready.sem, xnb_ready.count(n, 1))
                    for i in range(2):
                        ps = work_take(dve, n, f"out{i}", last)
                        nc.vector.tensor_tensor(mixed[:, 2 * i:2 * i + 2, :], ps.rearrange("p (c d) -> p c d", c=2),
                                                xnb[:, 2 * i:2 * i + 2, :], ALU.add).then_inc(mixed_ready.sem, 1)
                    dve.wait_ge(mixed_ready.sem, mixed_ready.count(n, 2))
                    layernorm_statistics(nc, dve, mixed, stats1, moments1, passed, ln1_stats, ln1_moments, n)
                    dve.wait_ge(ln1_moments.sem, ln1_moments.count(n, TILES))
                    for c in range(TILES):
                        nc.vector.scalar_tensor_tensor(mixed[:, c, :], mixed[:, c, :], moments1[:, c, 0:1], g1[:, :],
                                                       ALU.subtract, ALU.mult).then_inc(ln1_scaled.sem, 1)
                    dve.wait_ge(ln1_rstd.sem, ln1_rstd.count(n, 1))
                    dve.wait_ge(ln1_scaled.sem, ln1_scaled.count(n, TILES))
                    dve.wait_ge(rows_sent.sem, rows_sent.count(n, 0))
                    for c in range(TILES):
                        nc.vector.scalar_tensor_tensor(rows[:, c, 0:D], mixed[:, c, :], rstd1[:, c:c + 1], be1[:, :],
                                                       ALU.mult, ALU.add).then_inc(y_ready.sem, 1)

                def choose(n, last):
                    wide = [P, TILES, E]
                    ps = work_take(dve, n, "logits", last)[:, 0:TILES * E].rearrange("p (c e) -> p c e", c=TILES)
                    nc.vector.tensor_reduce(best[:, :], ps, AX.X, ALU.max).then_inc(best_ready.sem, 1)
                    dve.wait_ge(best_ready.sem, best_ready.count(n, 1))
                    nc.vector.tensor_tensor(is_best[:, :, :], ps, best[:, :].unsqueeze(2).broadcast_to(wide),
                                            ALU.is_equal).then_inc(is_best_ready.sem, 1)
                    dve.wait_ge(is_best_ready.sem, is_best_ready.count(n, 1))
                    nc.vector.tensor_tensor(order[:, :, :], is_best[:, :, :], descending[:, :].unsqueeze(1).broadcast_to(wide),
                                            ALU.mult).then_inc(order_ready.sem, 1)
                    dve.wait_ge(order_ready.sem, order_ready.count(n, 1))
                    nc.vector.tensor_reduce(first[:, :], order[:, :, :], AX.X, ALU.max).then_inc(first_ready.sem, 1)
                    dve.wait_ge(first_ready.sem, first_ready.count(n, 1))
                    nc.vector.tensor_tensor(chosen[:, :, :], order[:, :, :], first[:, :].unsqueeze(2).broadcast_to(wide),
                                            ALU.is_equal).then_inc(chosen_ready.sem, 1)

                def slots(n, last):
                    wide = [P, TILES, E]
                    ps = work_take(dve, n, "ranks", last)[:, 0:TILES * E].rearrange("p (c e) -> p c e", c=TILES)
                    dve.wait_ge(next_row_kept.sem, next_row_kept.count(n, 1))
                    nc.vector.tensor_tensor(place[:, :, :], ps, next_row[:, 0, :].unsqueeze(1).broadcast_to(wide),
                                            ALU.add).then_inc(place_ready.sem, 1)
                    ps = work_take(dve, n, "totals", last)[:, 0:E]
                    nc.vector.tensor_tensor(next_row[:, 1, :], ps, next_row[:, 0, :], ALU.add).then_inc(next_row_ready.sem, 1)
                    dve.wait_ge(place_ready.sem, place_ready.count(n, 1))
                    nc.vector.tensor_tensor(own_place[:, :, :], place[:, :, :], chosen[:, :, :],
                                            ALU.mult).then_inc(own_place_ready.sem, 1)
                    dve.wait_ge(own_place_ready.sem, own_place_ready.count(n, 1))
                    nc.vector.tensor_reduce(slot_f[:, :], own_place[:, :, :], AX.X, ALU.add).then_inc(slot_f_ready.sem, 1)
                    dve.wait_ge(slot_f_ready.sem, slot_f_ready.count(n, 1))
                    nc.vector.tensor_copy(slot[:, :], slot_f[:, :]).then_inc(slot_ready.sem, 1)
                    dve.wait_ge(next_row_ready.sem, next_row_ready.count(n, 1))
                    nc.vector.tensor_copy(next_row[:, 0, :], next_row[:, 1, :]).then_inc(next_row_kept.sem, 1)

                def group(n, last):
                    attention(n)
                    post_norm(n, last)
                    if not last:
                        ln_first(n + 1)
                        keys(n + 1, n, last)
                    choose(n, last)
                    slots(n, last)

                def step_tables():
                    done = 1

                    def then(instruction):
                        nonlocal done
                        done += 1
                        instruction.then_inc(tables.sem, 1)
                        dve.wait_ge(tables.sem, done)

                    dve.wait_ge(next_row_kept.sem, NGROUPS + 1)
                    nc.vector.tensor_scalar(filler_slot_f[:, :], next_row[:, 0, :], row_in_tile[:, 0:1], None,
                                            ALU.add).then_inc(tables.sem, 1)
                    dve.wait_ge(tables.sem, 1)
                    then(nc.vector.tensor_copy(filler_slot[:, :], filler_slot_f[:, :]))
                    then(nc.vector.tensor_tensor(counts[:, :], next_row[:, 0, :], region0[:, :], ALU.subtract))
                    wide = [P, E, 64]
                    then(nc.vector.tensor_tensor(tile_need[:, :, :], counts[:, :].unsqueeze(2).broadcast_to(wide),
                                                 tile_rows[:, :].unsqueeze(1).broadcast_to(wide), ALU.is_gt))
                    then(nc.vector.tensor_reduce(tiles_of[:, :], tile_need[:, :, :], AX.X, ALU.add))
                    wide = [P, E, E]
                    then(nc.vector.tensor_tensor(tiles_upto_all[:, :, :], tiles_of[:, :].unsqueeze(1).broadcast_to(wide),
                                                 upto[:, :].rearrange("p (a b) -> p a b", a=E), ALU.mult))
                    then(nc.vector.tensor_reduce(tiles_upto[:, :], tiles_upto_all[:, :, :], AX.X, ALU.add))
                    wide = [P, TABLE, E]
                    then(nc.vector.tensor_tensor(gone[:, :, :], steps[:, :].unsqueeze(2).broadcast_to(wide),
                                                 tiles_upto[:, :].unsqueeze(1).broadcast_to(wide), ALU.is_ge))
                    then(nc.vector.tensor_reduce(expert_f[:, :], gone[:, :, :], AX.X, ALU.add))
                    then(nc.vector.tensor_tensor(passed_tiles[:, :, :], gone[:, :, :],
                                                 tiles_of[:, :].unsqueeze(1).broadcast_to(wide), ALU.mult))
                    then(nc.vector.tensor_reduce(step0[:, :], passed_tiles[:, :, :], AX.X, ALU.add))
                    then(nc.vector.tensor_tensor(row_a[:, :], steps[:, :], step0[:, :], ALU.subtract))
                    then(nc.vector.tensor_scalar(row_b[:, :], row_a[:, :], float(P), None, ALU.mult))
                    then(nc.vector.scalar_tensor_tensor(row_f[:, :], expert_f[:, :], float(REGION), row_b[:, :],
                                                        ALU.mult, ALU.add))
                    then(nc.vector.tensor_copy(keep["row_table"][:, :], row_f[:, :]))
                    then(nc.vector.tensor_scalar(keep["expert_table"][:, :], expert_f[:, :], float(E - 1), None, ALU.min))

                dve.wait_ge(consts_loaded.sem, 16 * MIX_CONST)
                dve.wait_ge(consts_set.sem, 9)
                dve.sem_inc(max_free.sem, 2)
                dve.sem_inc(out_free.sem, 2)
                nc.vector.tensor_copy(next_row[:, 0, :], region0[:, :]).then_inc(next_row_kept.sem, 1)
                ln_first(0)
                keys(0, None, False)
                with dve.Fori(0, NGROUPS - 1) as n:
                    group(n, False)
                group(NGROUPS - 1, True)
                step_tables()

            @block.scalar
            def _(act):
                n_weights = 0
                for e in range(E):
                    for k in range(KD):
                        act.dma_start(keep["w1"][:, k, e * DF:(e + 1) * DF],
                                      t["e_w1"][e, k * P:(k + 1) * P, :]).then_inc(weights_loaded.sem, 16)
                    act.dma_start(keep["w2"][:, e * KF * D:(e + 1) * KF * D].rearrange("p (j d) -> p j d", j=KF),
                                  t["e_w2"][e].rearrange("(j p) d -> p j d", p=P)).then_inc(weights_loaded.sem, 16)
                    n_weights += KD + 1
                act.dma_start(keep["b1"][:, :], t["e_b1"]).then_inc(weights_loaded.sem, 16)
                n_weights += 1

                def qkv(m, n, last):
                    for k in range(KD):
                        ps = work_take(act, n, f"xT{k}", last)
                        nc.scalar.activation(xT[:, k, :], ps, ACT.Copy).then_inc(xT_ready.sem, 1)
                    for tile in range(KD):
                        ps = work_take(act, n, f"q{tile}", last)
                        nc.scalar.activation(qT[:, tile, :], ps, ACT.Identity, scale=M_SCALE,
                                             bias=b_qs[:, tile:tile + 1]).then_inc(q_ready.sem, 1)

                def group(n, last):
                    ps = work_take(act, n, "shiftT", last)
                    nc.scalar.activation(shiftT[:, :], ps.bitcast(BF16)[:, 0:S], ACT.Copy).then_inc(shiftT_ready.sem, 1)
                    for c in range(TILES):
                        act.wait_ge(probs_used.sem, probs_used.count(n, c - 1))
                        act.wait_ge(exp_full.sem, exp_full.count(n, c + 1))
                        nc.scalar.activation(probs[:, c % 2, :], ps_exp[:, c % 2, :], ACT.Exp).then_inc(exp_done.sem, 1)
                    if not last:
                        qkv(n + 1, n, last)
                    for k in range(KD):
                        ps = work_take(act, n, f"yT{k}", last)
                        nc.scalar.activation(yT[:, k, :], ps, ACT.Copy).then_inc(yT_ready.sem, 1)

                act.wait_ge(consts_set.sem, 9)
                act.sem_inc(exp_done.sem, 2)
                qkv(0, None, False)
                with act.Fori(0, NGROUPS - 1) as n:
                    group(n, False)
                group(NGROUPS - 1, True)
                act.wait_ge(weights_loaded.sem, 16 * n_weights)

            @block.tensor
            def _(pe):
                def qkv(m, n, last):
                    for k in range(KD):
                        ps = work_claim(pe, n, f"xT{k}", last)
                        pe.wait_ge(ln_done.sem, ln_done.count(m, TILES))
                        for c in range(TILES):
                            mm = nc.tensor.transpose(ps[:, c * P:(c + 1) * P], xn[:, c, k * P:(k + 1) * P], identf[:, :])
                        mm.then_inc(work_full.sem, 1)
                    pe.wait_ge(xT_ready.sem, xT_ready.count(m, KD))
                    for j, name in enumerate(("q0", "q1", "k0", "k1")):
                        ps = work_claim(pe, n, name, last)
                        for k in range(KD):
                            mm = nc.tensor.matmul(ps, w_qkv[:, k, j * P:(j + 1) * P], xT[:, k, :],
                                                  start=(k == 0), stop=(k == KD - 1))
                        mm.then_inc(work_full.sem, 1)
                    for i in range(2):
                        ps = work_claim(pe, n, f"v{i}", last)
                        for c in (2 * i, 2 * i + 1):
                            for k in range(KD):
                                mm = nc.tensor.matmul(ps[:, (c % 2) * D:(c % 2 + 1) * D], xT[:, k, c * P:(c + 1) * P],
                                                      w_qkv[:, k, 2 * D:3 * D], start=(k == 0 and c % 2 == 0),
                                                      stop=(k == KD - 1), skip_group_check=True)
                        mm.then_inc(work_full.sem, 1)

                def attention(n, last):
                    def add(out, lhsT, rhs):
                        return nc.tensor.matmul(out, lhsT, rhs, start=False, stop=True, skip_group_check=True)
                    pe.wait_ge(q_ready.sem, q_ready.count(n, KD))
                    pe.wait_ge(k_ready.sem, k_ready.count(n, MH))
                    wide = mask_pos[:, :].unsqueeze(1).broadcast_to([P, MH, P])
                    for c in range(TILES):
                        pe.wait_ge(max_free.sem, max_free.count(n, c - 1))
                        ps = ps_max[:, c % 2, :]
                        nc.tensor.matmul(ps.rearrange("p (h k) -> p h k", h=MH), ident[:, :], wide, start=True, stop=False,
                                         skip_group_check=True)
                        for h in range(MH):
                            mm = add(ps[:, h * P:(h + 1) * P], qT[:, h // 2, c * P:(c + 1) * P], kT[:, h, c * P:(c + 1) * P])
                        mm.then_inc(max_full.sem, 1)
                    ps = work_claim(pe, n, "shiftT", last)
                    pe.wait_ge(shift_ready.sem, shift_ready.count(n, 1))
                    for c in range(TILES):
                        mm = nc.tensor.transpose(ps.bitcast(BF16)[:, c * P:(c + 1) * P], shift[:, c, :], ident[:, :])
                    mm.then_inc(work_full.sem, 1)
                    pe.wait_ge(v_ready.sem, v_ready.count(n, 2))

                    def shifted(c):
                        pe.wait_ge(exp_done.sem, exp_done.count(n, c - 1))
                        ps = ps_exp[:, c % 2, :]
                        nc.tensor.matmul(ps.rearrange("p (h k) -> p h k", h=MH), ident[:, :], wide, start=True, stop=False,
                                         skip_group_check=True)
                        for h in range(MH):
                            add(ps[:, h * P:(h + 1) * P], kT[:, h, c * P:(c + 1) * P], qT[:, h // 2, c * P:(c + 1) * P])
                        if c == 0:
                            pe.wait_ge(shiftT_ready.sem, shiftT_ready.count(n, 1))
                        for h in range(MH):
                            mm = add(ps[:, h * P:(h + 1) * P], sel_head[:, h, :], shiftT[:, c * P:(c + 1) * P])
                        mm.then_inc(exp_full.sem, 1)

                    def values(c):
                        pe.wait_ge(out_free.sem, out_free.count(n, c - 1))
                        pe.wait_ge(exp_done.sem, exp_done.count(n, c + 1))
                        for side in range(2):
                            for h in range(MH):
                                lo, col = MD * (h % 2), D * side + P * (h // 2)
                                mm = nc.tensor.matmul(ps_out[lo:lo + MD, c % 2, col:col + P],
                                                      v[:, c, MD * h:MD * h + MD] if side == 0 else ones64[:, :],
                                                      probs[:, c % 2, h * P:(h + 1) * P],
                                                      start=(side == 0 and h < 2), stop=True, skip_group_check=True)
                        mm.then_inc(probs_used.sem, 1)

                    shifted(0)
                    for c in range(1, TILES):
                        shifted(c)
                        values(c - 1)
                    values(TILES - 1)
                    for i in range(2):
                        ps = work_claim(pe, n, f"out{i}", last)
                        pe.wait_ge(out_free.sem, out_free.count(n, 2 * i + 2))
                        for c in (2 * i, 2 * i + 1):
                            for tile in range(KD):
                                mm = nc.tensor.matmul(ps[:, (c % 2) * D:(c % 2 + 1) * D], oT[:, tile, c * P:(c + 1) * P],
                                                      w_o[:, tile, :], start=(tile == 0 and c % 2 == 0),
                                                      stop=(tile == KD - 1), skip_group_check=True)
                        mm.then_inc(work_full.sem, 1)

                def routing(n, last):
                    for k in range(KD):
                        ps = work_claim(pe, n, f"yT{k}", last)
                        pe.wait_ge(y_ready.sem, y_ready.count(n, TILES))
                        for c in range(TILES):
                            mm = nc.tensor.transpose(ps[:, c * P:(c + 1) * P], rows[:, c, k * P:(k + 1) * P], identf[:, :])
                        mm.then_inc(work_full.sem, 1)
                    ps = work_claim(pe, n, "logits", last)
                    pe.wait_ge(yT_ready.sem, yT_ready.count(n, KD))
                    for c in range(TILES):
                        for k in range(KD):
                            mm = nc.tensor.matmul(ps[:, c * E:(c + 1) * E], yT[:, k, c * P:(c + 1) * P], w_g[:, k, :],
                                                  start=(c == 0 and k == 0), stop=(k == KD - 1), skip_group_check=True)
                    mm.then_inc(work_full.sem, 1)
                    ps = work_claim(pe, n, "ranks", last)
                    pe.wait_ge(chosen_ready.sem, chosen_ready.count(n, 1))
                    nc.tensor.matmul(ps[:, 0:TILES * E], before[:, :], chosen[:, :, :].rearrange("p c e -> p (c e)"),
                                     start=True, stop=False, skip_group_check=True)
                    for c in range(TILES - 1):
                        later = TILES - 1 - c
                        mm = nc.tensor.matmul(ps[:, (c + 1) * E:TILES * E].rearrange("p (c e) -> p c e", e=E), ones16[:, :],
                                              chosen[:, c, :].unsqueeze(1).broadcast_to([P, later, E]), start=False,
                                              stop=True, skip_group_check=True)
                    mm.then_inc(work_full.sem, 1)
                    ps = work_claim(pe, n, "totals", last)
                    for c in range(TILES):
                        mm = nc.tensor.matmul(ps[:, 0:E], ones16[:, :], chosen[:, c, :], start=(c == 0), stop=(c == TILES - 1))
                    mm.then_inc(work_full.sem, 1)

                def group(n, last):
                    attention(n, last)
                    if not last:
                        qkv(n + 1, n, last)
                    routing(n, last)

                pe.wait_ge(consts_loaded.sem, 16 * MIX_CONST)
                pe.wait_ge(consts_set.sem, 9)
                pe.sem_inc(probs_used.sem, 2)
                pe.sem_inc(next_row_ready.sem, 1)
                qkv(0, None, False)
                pe.wait_ge(v_ready.sem, 2)
                with pe.Fori(0, NGROUPS - 1) as n:
                    group(n, False)
                group(NGROUPS - 1, True)


MIX_CONST = 14 + 1 + 3 + 4


def expert_program(nc, t, mem, keep):
    ctx = ExitStack()
    with ctx:
        def sb(name, shape, dt=F32):
            return ctx.enter_context(nc.sbuf_tensor(name, shape, dt))

        def signal(name, per, ahead=0):
            return Signal(ctx, nc, name, per, ahead)

        identf = sb("e_identf", [P, P])
        passed = signal("e_waits_passed_vector", 0)
        pool_passed = signal("e_waits_passed_pool", 0)
        half = sb("e_half", [P, 1])
        eps = sb("e_eps", [P, 1])
        row = sb("e_row", [P, 2, ROW])
        yT = sb("e_yT", [P, 2, KD * P])
        yb = sb("e_yb", [P, 2, D])
        h_rows = sb("e_h_rows", [P, DF])
        hT = sb("e_hT", [P, KF, P])
        summed = sb("e_summed", [P, 2, D])
        stats = sb("e_stats", [P, 2, 6])
        moments = sb("e_moments", [P, 2, 2])
        veps = sb("e_veps", [P, 2])
        rstd = sb("e_rstd", [P, 2])
        scaled = sb("e_scaled", [P, 2, D])
        normed = sb("e_normed", [P, 2, D])
        result = sb("e_result", [P, 2, D])
        token = sb("e_token", [P, 2, 1], U32)
        ps_h, ps_hT, ps_out, ps_yT = mem["ps_a"], mem["ps_b"], mem["ps_c"], mem["ps_d"]
        b2 = sb("e_b2", [P, E * D])
        g2 = sb("e_g2", [P, D])
        be2 = sb("e_be2", [P, D])
        w1, w2, b1 = keep["w1"], keep["w2"], keep["b1"]

        consts_loaded = signal("e_consts_loaded", 0)
        consts_set = signal("e_consts_set", 0)
        row_loaded = [signal(f"e_row_loaded{u}", 16) for u in range(2)]
        yT_full = signal("e_yT_full", 1)
        yT_ready = signal("e_yT_ready", 1)
        h_full = signal("e_h_full", 2)
        h_ready = signal("e_h_ready", 2)
        hT_full = signal("e_hT_full", 2)
        hT_ready = signal("e_hT_ready", KF)
        out_full = signal("e_out_full", 1)
        yb_ready = signal("e_yb_ready", 1)
        token_ready = signal("e_token_ready", 1)
        sum_ready = signal("e_sum_ready", 1)
        stats_ready = signal("e_stats_ready", 1)
        moments_ready = signal("e_moments_ready", 1)
        veps_ready = signal("e_veps_ready", 1)
        rstd_ready = signal("e_rstd_ready", 1)
        scaled_ready = signal("e_scaled_ready", 1)
        normed_ready = signal("e_normed_ready", 1)
        result_ready = signal("e_result_ready", 1, 2)
        stored = [signal(f"e_stored{u}", 16) for u in range(2)]

        with nc.Block() as block:

            @block.sync
            def _(sp):
                sp.dma_start(identf[:, :], t["c_identity"]).then_inc(consts_loaded.sem, 16)
                for dst, src in ((b2, "e_b2"), (g2, "e_g2"), (be2, "e_be2")):
                    sp.dma_start(dst[:, :], t[src].partition_broadcast(P)).then_inc(consts_loaded.sem, 16)

                def load(i, u):
                    j = i * 2 + u
                    sp.wait_ge(result_ready.sem, result_ready.count(j, -1))
                    row0 = sp.value_load(keep["row_table"][0:1, bass.ds(j, 1)], min_val=0,
                                         max_val=E * REGION + (SPARE_TILES - 1) * P)
                    sp.dma_start(row[:, u, :], t["sorted"][bass.ds(row0, P), :]).then_inc(row_loaded[u].sem, 16)

                with sp.Fori(0, STEPS // 2) as i:
                    for u in range(2):
                        load(i, u)
                load(STEPS // 2, 0)

            @block.gpsimd
            def _(pool):
                nc.gpsimd.memset(half[:, :], -0.5).then_inc(consts_set.sem, 1)
                nc.gpsimd.memset(eps[:, :], EPS).then_inc(consts_set.sem, 1)
                pool.wait_ge(consts_set.sem, 2)
                pool.wait_ge(consts_loaded.sem, 64)
                pool.sem_inc(result_ready.sem, 2)

                def step(i, u):
                    j = i * 2 + u
                    e = pool.value_load(keep["expert_table"][0:1, bass.ds(j, 1)], min_val=0, max_val=E - 1)
                    pool.wait_ge(row_loaded[u].sem, row_loaded[u].count(i, 16))
                    nc.gpsimd.tensor_tensor(yb[:, u, :], row[:, u, 0:D], b2[:, bass.ds(e * D, D)],
                                            ALU.add).then_inc(yb_ready.sem, 1)
                    pool.wait_ge(moments_ready.sem, moments_ready.count(j, 1))
                    nc.gpsimd.tensor_tensor(veps[:, u:u + 1], moments[:, u, 1:2], eps[:, :], ALU.add).then_inc(veps_ready.sem, 1)
                    pool.wait_ge(veps_ready.sem, veps_ready.count(j, 1))
                    nc.gpsimd.tensor_tensor(rstd[:, u:u + 1], veps[:, u:u + 1], half[:, :], ALU.pow).then_inc(rstd_ready.sem, 1)
                    pool.wait_ge(normed_ready.sem, normed_ready.count(j, 1))
                    if not (isinstance(i, int) and i == 0):
                        pool.wait_ge(stored[u].sem, stored[u].count(i, 0))
                    nc.gpsimd.tensor_tensor(result[:, u, :], normed[:, u, :], row[:, u, D:2 * D],
                                            ALU.add).then_inc(result_ready.sem, 1)
                    wait_apart(pool, pool_passed, result_ready.sem, result_ready.count(j, 1))
                    wait_apart(pool, pool_passed, token_ready.sem, token_ready.count(j, 1))
                    nc.gpsimd.indirect_dma_start(
                        out=t["out"], out_offset=bass.IndirectOffsetOnAxis(ap=token[:, u, :], axis=0),
                        in_=result[:, u, :], in_offset=None, bounds_check=B * S - 1, oob_is_err=False
                        ).then_inc(stored[u].sem, 16)

                for u in range(2):
                    step(0, u)
                with pool.Fori(1, STEPS // 2) as i:
                    for u in range(2):
                        step(i, u)
                for u in range(2):
                    pool.wait_ge(stored[u].sem, 16 * (STEPS // 2))

            @block.vector
            def _(dve):
                def step(i, u):
                    j = i * 2 + u
                    e = dve.value_load(keep["expert_table"][0:1, bass.ds(j, 1)], min_val=0, max_val=E - 1)
                    dve.wait_ge(row_loaded[u].sem, row_loaded[u].count(i, 16))
                    if not (isinstance(i, int) and i == 0):
                        dve.wait_ge(stored[u].sem, stored[u].count(i, 0))
                    nc.vector.tensor_copy(token[:, u, :], row[:, u, 2 * D:2 * D + 1]).then_inc(token_ready.sem, 1)
                    for f in range(KF):
                        if f % 4 == 0:
                            dve.wait_ge(hT_full.sem, hT_full.count(j, f // 4 + 1))
                        nc.vector.tensor_scalar(hT[:, f, :], ps_hT[:, f // 4, (f % 4) * P:(f % 4 + 1) * P],
                                                b1[:, bass.ds(e * KF + f, 1)], 0.0, ALU.add, ALU.max
                                                ).then_inc(hT_ready.sem, 1)
                    dve.wait_ge(out_full.sem, out_full.count(j, 1))
                    dve.wait_ge(yb_ready.sem, yb_ready.count(j, 1))
                    nc.vector.tensor_tensor(summed[:, u, :], ps_out[:, u, 0:D], yb[:, u, :], ALU.add).then_inc(sum_ready.sem, 1)
                    dve.wait_ge(sum_ready.sem, sum_ready.count(j, 1))
                    nc.vector.bn_stats(stats[:, u, :], summed[:, u, :]).then_inc(stats_ready.sem, 1)
                    wait_apart(dve, passed, stats_ready.sem, stats_ready.count(j, 1))
                    nc.vector.bn_aggr(moments[:, u, :], stats[:, u, :]).then_inc(moments_ready.sem, 1)
                    dve.wait_ge(moments_ready.sem, moments_ready.count(j, 1))
                    nc.vector.scalar_tensor_tensor(scaled[:, u, :], summed[:, u, :], moments[:, u, 0:1], g2[:, :],
                                                   ALU.subtract, ALU.mult).then_inc(scaled_ready.sem, 1)
                    dve.wait_ge(scaled_ready.sem, scaled_ready.count(j, 1))
                    dve.wait_ge(rstd_ready.sem, rstd_ready.count(j, 1))
                    nc.vector.scalar_tensor_tensor(normed[:, u, :], scaled[:, u, :], rstd[:, u:u + 1], be2[:, :],
                                                   ALU.mult, ALU.add).then_inc(normed_ready.sem, 1)

                dve.wait_ge(consts_loaded.sem, 64)
                for u in range(2):
                    step(0, u)
                with dve.Fori(1, STEPS // 2) as i:
                    for u in range(2):
                        step(i, u)

            @block.scalar
            def _(act):
                def features(j, u):
                    act.wait_ge(yT_full.sem, yT_full.count(j, 1))
                    nc.scalar.activation(yT[:, u, :], ps_yT[:, u, 0:KD * P], ACT.Copy).then_inc(yT_ready.sem, 1)

                def hidden(j):
                    for half_ in range(2):
                        act.wait_ge(h_full.sem, h_full.count(j, half_ + 1))
                        nc.scalar.activation(h_rows[:, half_ * 512:(half_ + 1) * 512], ps_h[:, half_, :],
                                             ACT.Copy).then_inc(h_ready.sem, 1)

                features(0, 0)
                hidden(0)
                with act.Fori(0, STEPS // 2) as i:
                    for u in range(2):
                        features(i * 2 + (u + 1), 1 - u)
                        act.wait_ge(hT_full.sem, hT_full.count(i * 2 + u, 2))
                        hidden(i * 2 + (u + 1))

            @block.tensor
            def _(pe):
                def features(i, u):
                    j = i * 2 + u
                    pe.wait_ge(row_loaded[u].sem, row_loaded[u].count(i, 16))
                    for k in range(KD):
                        mm = nc.tensor.transpose(ps_yT[:, u, k * P:(k + 1) * P], row[:, u, k * P:(k + 1) * P], identf[:, :])
                    mm.then_inc(yT_full.sem, 1)

                def hidden(j, u):
                    e = pe.value_load(keep["expert_table"][0:1, bass.ds(j, 1)], min_val=0, max_val=E - 1)
                    pe.wait_ge(yT_ready.sem, yT_ready.count(j, 1))
                    for half_ in range(2):
                        for k in range(KD):
                            mm = nc.tensor.matmul(ps_h[:, half_, :], yT[:, u, k * P:(k + 1) * P],
                                                  w1[:, k, bass.ds(e * DF + half_ * 512, 512)],
                                                  start=(k == 0), stop=(k == KD - 1))
                        mm.then_inc(h_full.sem, 1)

                def transposes(j):
                    for half_ in range(2):
                        pe.wait_ge(h_ready.sem, h_ready.count(j, half_ + 1))
                        for f in range(4 * half_, 4 * half_ + 4):
                            mm = nc.tensor.transpose(ps_hT[:, half_, (f % 4) * P:(f % 4 + 1) * P],
                                                     h_rows[:, f * P:(f + 1) * P], identf[:, :])
                        mm.then_inc(hT_full.sem, 1)

                def output(j, u):
                    e = pe.value_load(keep["expert_table"][0:1, bass.ds(j, 1)], min_val=0, max_val=E - 1)
                    for f in range(KF):
                        pe.wait_ge(hT_ready.sem, hT_ready.count(j, f + 1))
                        mm = nc.tensor.matmul(ps_out[:, u, 0:D], hT[:, f, :], w2[:, bass.ds(e * KF * D + f * D, D)],
                                              start=(f == 0), stop=(f == KF - 1))
                    mm.then_inc(out_full.sem, 1)

                pe.wait_ge(consts_loaded.sem, 64)
                features(0, 0)
                hidden(0, 0)
                with pe.Fori(0, STEPS // 2) as i:
                    for u in range(2):
                        features(i + u, 1 - u)
                        transposes(i * 2 + u)
                        hidden(i * 2 + (u + 1), 1 - u)
                        output(i * 2 + u, u)


def decoder_block(nc, t):
    t["x2"] = nc.dram_tensor("x2_rows", [B, S, D], F32, kind="Internal").ap()
    t["x2_groups"] = t["x2"].rearrange("s (g p) d -> g s p d", g=NGROUPS)
    t["qk_parts"] = nc.dram_tensor("qk_parts", [2, 3, D, S], BF16, kind="Internal").ap()
    t["sorted"] = nc.dram_tensor("sorted_rows", [E * REGION + SPARE_TILES * P, ROW], F32, kind="Internal").ap()
    with ExitStack() as ctx:
        mem = {name: ctx.enter_context(nc.psum_tensor(name, [P, 2, 512], F32)) for name in ("ps_a", "ps_b", "ps_c", "ps_d")}
        attention_program(nc, t, mem)
        shapes = {"w1": [P, KD, E * DF], "w2": [P, E * KF * D], "b1": [P, E * KF]}
        keep = {name: ctx.enter_context(nc.sbuf_tensor("keep_" + name, shape, F32)) for name, shape in shapes.items()}
        for name in ("row_table", "expert_table"):
            keep[name] = ctx.enter_context(nc.sbuf_tensor("keep_" + name, [P, TABLE], I32))
        mixing_program(nc, t, mem, keep)
        expert_program(nc, t, mem, keep)


def constants():
    import numpy as np
    i = np.arange(P)
    eye = np.eye(P, dtype=np.float32)
    own = np.where(i[None, :] <= i[:, None], 0, NEG)
    previous = np.where(i[None, :] > i[:, None], 0, NEG)
    first = np.where(i[None, :] < PREFIX, 0, previous)
    sel = np.zeros((P, HEADS, P))
    for h in range(HEADS):
        sel[[h, HEADS + h], h] = 1
    sel_prefix = np.zeros((P, GROUPS, P))
    for g in range(GROUPS):
        for j, h in enumerate(group_heads(g)):
            sel_prefix[[h, HEADS + h], g, 32 * j:32 * j + 32] = 1
            sel_prefix[2 * HEADS, g, 32 * j + PREFIX:32 * j + 32] = NEG
    sel_pair = np.zeros((P, PAIRS, P))
    for h in range(HEADS):
        sel_pair[[h, HEADS + h], h // 2, CTX * (h % 2):CTX * (h % 2 + 1)] = 1
    half_cols = np.zeros((P, 2, 32))
    half_cols[:, 0, :HD] = half_cols[:, 1, HD:] = 1
    col = np.arange(D)
    odd = (col % 32) // HD
    prefix_rows = np.stack([(i[:, None] // 32 == (col // 32) % 4) & (odd == o) for o in range(2)], 1)
    sel_head = np.zeros((P, MH, P))
    for h in range(MH):
        sel_head[[h, MH + h], h] = 1
    e = np.arange(E)
    fp32 = {
        "c_identity": eye, "c_half_cols": half_cols, "c_prefix_rows": prefix_rows,
        "c_ctx_rows": i[:, None] // CTX == odd, "c_head_rows": i[:, None] // HD == np.arange(8),
        "c_head_half": i[:, None] // MD == np.arange(2),
        "c_descending": np.broadcast_to(E - e, (P, E)), "c_region0": np.broadcast_to(e * REGION, (P, E)),
        "c_token0": (i // POS * S + i % POS)[:, None] + POS * np.arange(TILES), "c_row_in_tile": i[:, None],
        "c_tile_rows": np.broadcast_to(P * np.arange(64), (P, 64)),
        "c_upto": np.broadcast_to((e[None, :] <= e[:, None]).reshape(-1), (P, E * E)),
        "c_steps": np.broadcast_to(np.arange(TABLE), (P, TABLE)),
    }
    bf16 = {
        "c_identity16": eye, "c_mask_qk": np.stack([np.concatenate([p, own], 1) for p in (first, previous)], 1),
        "c_mask_kq": np.concatenate([own.T, first.T, own.T, previous.T, own.T], 1),
        "c_sel": sel, "c_sel_prefix": sel_prefix, "c_sel_pair": sel_pair, "c_sel_head": sel_head,
        "c_mask_pos": np.where(i[:, None] % POS == i % POS, 0, NEG), "c_before": i[:, None] < i,
    }
    out = {k: np.ascontiguousarray(v, np.float32) for k, v in fp32.items()}
    out.update({k: np.ascontiguousarray(np.asarray(v, np.float32)).astype(mybir.dt.np(BF16)) for k, v in bf16.items()})
    return out


def kernel(**inputs):
    import numpy as np
    import concourse.bacc as bacc
    from concourse.bass_utils import run_bass_kernel_spmd

    def array(name):
        return np.asarray(inputs[name])

    def columns(a):
        return a.reshape(-1, P).T

    laid = {"x": array("x"), "ctx": array("ctx_1024"), "mask": array("mask_BxSxS2_if1"),
            "w_qkvT": array("L0_attn_w_qkv").T, "w_outT": array("L0_attn_w_out").T,
            "b_q2": columns(array("L0_xattn_bq")), "b_k2": columns(array("L0_xattn_bk")),
            "b_v2": array("L0_xattn_bv"), "b_o2": array("L0_xattn_bo"),
            "m_w_qkvT": array("L0_ffn_Wqkv").T, "m_w_oT": array("L0_ffn_Wo").T, "m_w_gT": array("L0_ffn_Wg").T,
            "m_b_q": columns(array("L0_ffn_bqkv")[0:D]), "m_b_k": columns(array("L0_ffn_bqkv")[D:2 * D]),
            "m_b_v": array("L0_ffn_bqkv")[2 * D:], "m_b_o": array("L0_ffn_bo"),
            "m_g1": array("L0_ffn_g1"), "m_be1": array("L0_ffn_be1"),
            "e_w1": array("L0_ffn_W1"), "e_w2": array("L0_ffn_W2"), "e_b1": columns(array("L0_ffn_b1")),
            "e_b2": array("L0_ffn_b2").reshape(-1), "e_g2": array("L0_ffn_g2"), "e_be2": array("L0_ffn_be2")}
    for a in "qkvo":
        laid[f"w_{a}2T"] = array(f"L0_xattn_W{a}").T
    laid.update(constants())

    nc = bacc.Bacc("TRN2", target_bir_lowering=False, num_devices=1)
    arrays, t = {}, {}
    for name, a in laid.items():
        a = np.ascontiguousarray(a)
        arrays["in_" + name] = a
        t[name] = nc.dram_tensor("in_" + name, a.shape, mybir.dt.from_np(a.dtype), kind="ExternalInput").ap()
    out = nc.dram_tensor("out", [B * S, D], F32, kind="ExternalOutput").ap()
    t["out"] = out
    decoder_block(nc, t)
    r = run_bass_kernel_spmd(nc, [arrays], core_ids=[0])
    return r.results[0]["out"].reshape(B, S, D)
```

```python
from contextlib import ExitStack

import concourse.bass as bass
from concourse import mybir

F32 = mybir.dt.float32
BF16 = mybir.dt.bfloat16
I32 = mybir.dt.int32
U32 = mybir.dt.uint32
ALU = mybir.AluOpType
ACT = mybir.ActivationFunctionType
AX = mybir.AxisListType

P = 128
B, S, D = 8, 512, 256
KD = D // P
TILES = S // P
HEADS, HD = 16, 16
WINDOW, PREFIX = 128, 16
CTX = 64
PAIRS = HEADS // 2
PARTS = 6
SPLIT_ROWS = PARTS * HD
Q_PARTS = (0, 0, 0, 1, 1, 2)
K_PARTS = (0, 1, 2, 0, 1, 0)
EPS = 1e-5
QK_SCALE = HD ** -0.5
GROUP = 4
GROUPS = HEADS // GROUP
HEAD_COLS = 3 * 256 + 128
GROUP_COLS = GROUP * HEAD_COLS + 256
NEG = -(2.0 ** 30)
NEG_MASK = -(2.0 ** 100)


class Signal:

    def __init__(self, ctx, nc, name, per, ahead=0):
        self.sem = ctx.enter_context(nc.semaphore(name))
        self.per, self.ahead = per, ahead

    def count(self, n, k):
        return n * self.per + (k + self.ahead)


def group_heads(g):
    return [8 * (g // 2) + 2 * j + g % 2 for j in range(GROUP)]


def wait_apart(eng, passed, sem, value):
    eng.wait_ge(sem, value)
    eng.sem_inc(passed.sem, 1)


def layernorm_statistics(nc, dve, x, stats, moments, passed, sig_stats, sig_moments, n):
    for c in range(TILES):
        nc.vector.bn_stats(stats[:, c, :], x[:, c, :]).then_inc(sig_stats.sem, 1)
    wait_apart(dve, passed, sig_stats.sem, sig_stats.count(n, TILES))
    for c in range(TILES):
        nc.vector.bn_aggr(moments[:, c, :], stats[:, c, :]).then_inc(sig_moments.sem, 1)


def layernorm_rstd(nc, pool, moments, veps, eps, half, rstd, sig_moments, sig_veps, sig_rstd, n):
    pool.wait_ge(sig_moments.sem, sig_moments.count(n, TILES))
    nc.gpsimd.tensor_tensor(veps[:, :], moments[:, :, 1], eps, ALU.add).then_inc(sig_veps.sem, 1)
    pool.wait_ge(sig_veps.sem, sig_veps.count(n, 1))
    nc.gpsimd.tensor_tensor(rstd[:, :], veps[:, :], half, ALU.pow).then_inc(sig_rstd.sem, 1)


def layernorm_apply(nc, dve, x, out, moments, rstd, sig_rstd, sig_done, n):
    dve.wait_ge(sig_rstd.sem, sig_rstd.count(n, 1))
    for c in range(TILES):
        nc.vector.tensor_scalar(out[:, c, :], x[:, c, :], moments[:, c, 0:1], rstd[:, c:c + 1],
                                ALU.subtract, ALU.mult).then_inc(sig_done.sem, 1)


CROSS_FILLS = ["out0", "out1", "xT2_0", "xT2_1", "q2_0", "q2_1", "shiftT2", "out2_0", "out2_1"]
FILLS = ["xT0", "xT1", "q0", "q1", "out0", "out1", "k0", "k1", "v0", "v1", "vg", "xT2_0", "xT2_1", "q2_0", "q2_1",
         "shiftT2", "shiftT", "out2_0", "out2_1", "ctxT", "k2", "v2"]
WINDOW_FILLS = [f for f in FILLS if f not in CROSS_FILLS]
CROSS_MAX, WINDOW_MAX = 2 * TILES, 30
CROSS_EXP, WINDOW_EXP = PAIRS, 9 * GROUPS
CROSS_SUMS, WINDOW_SUMS = KD, GROUPS


def attention_program(nc, t, mem, later_loads):
    ctx = ExitStack()
    with ctx:
        def sb(name, shape, dt=F32):
            return ctx.enter_context(nc.sbuf_tensor(name, shape, dt))

        def signal(name, per, ahead=0):
            return Signal(ctx, nc, name, per, ahead)

        def cross_signal(name, per, ahead=0):
            return Signal(ctx, nc, name, per, ahead - per)

        identf = sb("identf", [P, P])
        ident = sb("ident", [P, P], BF16)
        mask_qk = sb("mask_qk", [P, 2, 256], BF16)
        mask_kq = sb("mask_kq", [P, 640], BF16)
        sel = sb("sel", [P, HEADS, P], BF16)
        sel_prefix = sb("sel_prefix", [P, GROUPS, P], BF16)
        sel_pair = sb("sel_pair", [P, PAIRS, P], BF16)
        half_cols = sb("half_cols", [P, 2, 32])
        prefix_rows = sb("prefix_rows", [P, 2, D])
        ctx_rows = sb("ctx_rows", [P, D])
        head_rows = sb("head_rows", [P, 8])
        w_qkv = sb("w_qkv", [P, KD, 3 * D])
        w_out = sb("w_out", [P, KD, D])
        w_q2 = sb("w_q2", [P, KD, D])
        w_k2 = sb("w_k2", [P, KD, D])
        w_v2 = sb("w_v2", [P, KD, D])
        w_o2 = sb("w_o2", [P, KD, D])
        b_q2 = sb("b_q2", [P, KD])
        b_q2s = sb("b_q2s", [P, KD])
        b_k2 = sb("b_k2", [P, KD])
        b_v2 = sb("b_v2", [P, D])
        b_o2 = sb("b_o2", [P, D])
        half = sb("half", [P, TILES])
        eps = sb("eps", [P, TILES])
        x_in = sb("x_in", [P, TILES, D])
        x_res = sb("x_res", [P, TILES, D])
        stats = sb("stats", [P, TILES, 6])
        moments = sb("moments", [P, TILES, 2])
        veps = sb("veps", [P, TILES])
        rstd = sb("rstd", [P, TILES])
        stats2 = sb("stats2", [P, TILES, 6])
        moments2 = sb("moments2", [P, TILES, 2])
        veps2 = sb("veps2", [P, TILES])
        rstd2 = sb("rstd2", [P, TILES])
        xn = sb("xn", [P, TILES, D])
        xn2 = sb("xn2", [P, TILES, D])
        xT = sb("xT", [P, KD, S])
        xT2 = sb("xT2", [P, KD, S])
        parts = sb("parts", [P, 3, 4, S], BF16)
        rest = sb("rest", [P, 4, S])
        q_rows = sb("q_rows", [SPLIT_ROWS, HEADS, S], BF16)
        k_rows = sb("k_rows", [SPLIT_ROWS, HEADS, S], BF16)
        v_half = sb("v_half", [P, 2, TILES, D])
        v_prefix = sb("v_prefix", [P, 2, D])
        top = sb("top", [P, TILES, HEADS])
        top_prefix = sb("top_prefix", [P, 2, HEADS])
        top2 = sb("top2", [P, TILES, HEADS])
        shift = sb("shift", [P, TILES, P], BF16)
        shiftT = sb("shiftT", [P, S], BF16)
        shift2 = sb("shift2", [P, TILES, P], BF16)
        shiftT2 = sb("shiftT2", [P, S], BF16)
        probs = sb("probs", [P, 2, GROUP_COLS])
        rden = sb("rden", [P, S])
        oT = sb("oT", [P, KD, S])
        oT2 = sb("oT2", [P, KD, S])
        x1 = sb("x1", [P, TILES, D])
        x1b = sb("x1b", [P, TILES, D])
        ctx_in = sb("ctx_in", [2 * CTX, D])
        mask_in = sb("mask_in", [P, TILES, CTX], I32)
        mask_add = sb("mask_add", [P, TILES, 2, CTX], BF16)
        ctxT = sb("ctxT", [P, KD, 2, CTX])
        k2 = sb("k2", [P, KD, 8, CTX])
        v2 = sb("v2", [P, D])
        v2pair = sb("v2pair", [P, D])
        q2T = sb("q2T", [P, KD, S])
        x2 = sb("x2", [P, TILES, D])
        ps_max = mem["ps_a"]
        ps_exp = mem["ps_b"]
        ps_out = mem["ps_c"]
        ps_work = mem["ps_d"]

        consts_loaded = signal("consts_loaded", 0)
        consts_set = signal("consts_set", 0)
        later_loaded = signal("later_loaded", 0)
        x_loaded = signal("x_loaded", 16)
        xres_loaded = signal("xres_loaded", 16)
        ctx_loaded = signal("ctx_loaded", 32)
        mask_loaded = signal("mask_loaded", 16)
        ln_stats = signal("ln_stats", TILES)
        ln_moments = signal("ln_moments", TILES)
        ln_veps = signal("ln_veps", 1)
        ln_rstd = signal("ln_rstd", 1)
        ln_done = signal("ln_done", TILES)
        ln2_stats = cross_signal("ln2_stats", TILES)
        ln2_moments = cross_signal("ln2_moments", TILES)
        ln2_veps = cross_signal("ln2_veps", 1)
        ln2_rstd = cross_signal("ln2_rstd", 1)
        ln2_done = cross_signal("ln2_done", TILES)
        work_full = signal("work_full", len(FILLS), -len(CROSS_FILLS))
        xT_ready = signal("xT_ready", KD)
        xT2_ready = cross_signal("xT2_ready", KD)
        part_hi = signal("part_hi", 4)
        part_rest = signal("part_rest", 4)
        part_mid = signal("part_mid", 4)
        part_lo = signal("part_lo", 4)
        q_stored = signal("q_stored", 16 * 6)
        k_stored = signal("k_stored", 16 * 6)
        rows_loaded = signal("rows_loaded", 16 * 12)
        v_ready = signal("v_ready", 4)
        vprefix_ready = signal("vprefix_ready", 2)
        max_full = signal("max_full", CROSS_MAX + WINDOW_MAX, -CROSS_MAX)
        max_free = signal("max_free", CROSS_MAX + WINDOW_MAX, 2 - CROSS_MAX)
        top_joined = signal("top_joined", 1)
        shift_hi = signal("shift_hi", 1)
        shift_ready = signal("shift_ready", 1)
        shiftT_ready = signal("shiftT_ready", 1)
        shift2_hi = cross_signal("shift2_hi", 1)
        shift2_ready = cross_signal("shift2_ready", 1)
        shiftT2_ready = cross_signal("shiftT2_ready", 1)
        exp_full = signal("exp_full", CROSS_EXP + WINDOW_EXP, -CROSS_EXP)
        exp_done = signal("exp_done", CROSS_EXP + WINDOW_EXP, 2 - CROSS_EXP)
        probs_used = signal("probs_used", CROSS_SUMS + WINDOW_SUMS, 2 - CROSS_SUMS)
        out_recip = signal("out_recip", 2 * KD, -KD)
        out_free = signal("out_free", 2 * KD, 1 - KD)
        ctxT_ready = signal("ctxT_ready", 1)
        k2_ready = signal("k2_ready", 2)
        v2_biased = signal("v2_biased", 1)
        v2_ready = signal("v2_ready", 1)
        mask_ready = cross_signal("mask_ready", 1)
        q2_ready = cross_signal("q2_ready", 2)
        x1_ready = cross_signal("x1_ready", 2)
        x1b_ready = cross_signal("x1b_ready", 1)
        x2_ready = cross_signal("x2_ready", 2)
        x2_stored = cross_signal("x2_stored", 16, 16)
        passed = signal("waits_passed_vector", 0)
        pool_passed = signal("waits_passed_pool", 0)
        sp_passed = signal("waits_passed_sync", 0)

        def released(n, name):
            kind, k = name.rstrip("01"), int(name[-1]) if name[-1] in "01" else 0
            sig, count = {
                "xT": (xT_ready, k + 1), "q": (part_rest, k + 1), "k": (part_rest, k + 3), "v": (v_ready, 2 * k + 2),
                "vg": (vprefix_ready, 2), "shiftT": (shiftT_ready, 1), "ctxT": (ctxT_ready, 1), "k2": (k2_ready, 2),
                "v2": (v2_biased, 1), "out": (x1_ready, k + 1), "xT2_": (xT2_ready, k + 1), "q2_": (q2_ready, k + 1),
                "shiftT2": (shiftT2_ready, 1), "out2_": (x2_ready, k + 1),
            }[kind]
            return sig.sem, sig.count(n, count)

        def work_place(n, name):
            if isinstance(n, int) and n == 0:
                j = WINDOW_FILLS.index(name)
                return WINDOW_FILLS, j, j % 2
            order = CROSS_FILLS if isinstance(n, int) and n == B else FILLS
            j = order.index(name)
            return order, j, (j + len(WINDOW_FILLS)) % 2

        def work_claim(pe, n, name):
            order, j, bank = work_place(n, name)
            if j >= 2:
                pe.wait_ge(*released(n, order[j - 2]))
            elif order is not WINDOW_FILLS:
                pe.wait_ge(*released(n - 1, FILLS[j - 2]))
            return ps_work[:, bank, :]

        def work_take(eng, n, name):
            order, j, bank = work_place(n, name)
            eng.wait_ge(work_full.sem, j + 1 if order is WINDOW_FILLS else work_full.count(n, j + 1))
            return ps_work[:, bank, :]

        with nc.Block() as block:

            @block.sync
            def _(sp):
                n_const = 0

                def const(dst, src):
                    nonlocal n_const
                    sp.dma_start(dst, src).then_inc(consts_loaded.sem, 16)
                    n_const += 1

                def load_x(m):
                    sp.dma_start(x_in[:, :, :], t["x"][m].rearrange("(c p) d -> p c d", p=P)).then_inc(x_loaded.sem, 16)

                load_x(0)
                const(identf[:, :], t["c_identity"])
                for k in range(KD):
                    const(w_qkv[:, k, :], t["w_qkvT"][k * P:(k + 1) * P, :])
                const(ident[:, :], t["c_identity16"])
                const(mask_qk[:, :, :], t["c_mask_qk"])
                const(mask_kq[:, :], t["c_mask_kq"])
                const(sel[:, :, :], t["c_sel"])
                const(sel_prefix[:, :, :], t["c_sel_prefix"])
                const(sel_pair[:, :, :], t["c_sel_pair"])
                const(half_cols[:, :, :], t["c_half_cols"])
                const(prefix_rows[:, :, :], t["c_prefix_rows"])
                const(ctx_rows[:, :], t["c_ctx_rows"])
                const(head_rows[:, :], t["c_head_rows"])
                for dst, src in ((w_out, "w_outT"), (w_q2, "w_q2T"), (w_k2, "w_k2T"), (w_v2, "w_v2T"), (w_o2, "w_o2T")):
                    const(dst[:, :, :], t[src].rearrange("(k p) n -> p k n", p=P))
                const(b_q2[:, :], t["b_q2"])
                const(b_k2[:, :], t["b_k2"])
                const(b_v2[:, :], t["b_v2"].partition_broadcast(P))
                const(b_o2[:, :], t["b_o2"].partition_broadcast(P))
                assert n_const == N_CONST

                def split_side(n, side, stored):
                    for tile in range(KD):
                        for part, sig in enumerate((part_hi, part_mid, part_lo)):
                            sp.wait_ge(sig.sem, sig.count(n, KD * side + tile + 1))
                            sp.dma_start(t["qk_parts"][side, part, tile * P:(tile + 1) * P, :],
                                         parts[:, part, KD * side + tile, :]).then_inc(stored.sem, 16)
                    sp.wait_ge(stored.sem, stored.count(n, 16 * 6))
                    dst, order = ((q_rows, Q_PARTS), (k_rows, K_PARTS))[side]
                    for block_, part in enumerate(order):
                        sp.dma_start(dst[block_ * HD:(block_ + 1) * HD, :, :],
                                     t["qk_parts"][side, part].rearrange("(h r) s -> r h s", r=HD)
                                     ).then_inc(rows_loaded.sem, 16)

                def tiles_of(src):
                    return src.rearrange("(c p) d -> p c d", p=P)

                def iteration(n, last):
                    first = isinstance(n, int) and n == 0
                    if not first:
                        sp.wait_ge(ctxT_ready.sem, ctxT_ready.count(n, 0))
                    for rep in range(2):
                        sp.dma_start(ctx_in[rep * CTX:(rep + 1) * CTX, :], t["ctx"][n]).then_inc(ctx_loaded.sem, 16)
                    if not last:
                        sp.wait_ge(ln_done.sem, ln_done.count(n, TILES))
                        load_x(n + 1)
                    if not first:
                        wait_apart(sp, sp_passed, exp_full.sem, exp_full.count(n, 0))
                    split_side(n, 0, q_stored)
                    split_side(n, 1, k_stored)
                    if not first:
                        sp.wait_ge(x1_ready.sem, x1_ready.count(n, 2))
                    sp.dma_start(x_res[:, :, :], tiles_of(t["x"][n])).then_inc(xres_loaded.sem, 16)
                    if not first:
                        sp.wait_ge(mask_ready.sem, mask_ready.count(n, 1))
                    sp.dma_start(mask_in[:, :, :], tiles_of(t["mask"][n])).then_inc(mask_loaded.sem, 16)
                    if not first:
                        store_x2(n)

                def store_x2(n):
                    sp.wait_ge(x2_ready.sem, x2_ready.count(n, 2))
                    sp.dma_start(tiles_of(t["x2"][n - 1]), x2[:, :, :]).then_inc(x2_stored.sem, 16)

                iteration(0, False)
                for dst, src in later_loads:
                    sp.dma_start(dst, src).then_inc(later_loaded.sem, 16)
                with sp.Fori(1, B - 1) as n:
                    iteration(n, False)
                iteration(B - 1, True)
                store_x2(B)
                sp.wait_ge(later_loaded.sem, 16 * len(later_loads))
                sp.wait_ge(x2_stored.sem, x2_stored.count(B, 16))

            @block.gpsimd
            def _(pool):
                nc.gpsimd.memset(half[:, :], -0.5).then_inc(consts_set.sem, 1)
                nc.gpsimd.memset(eps[:, :], EPS).then_inc(consts_set.sem, 1)
                nc.gpsimd.memset(v_half[:, :, :, :], 0.0).then_inc(consts_set.sem, 1)
                nc.gpsimd.memset(shift[:, :, :], 0.0).then_inc(consts_set.sem, 1)
                nc.gpsimd.memset(shift2[:, :, :], 0.0).then_inc(consts_set.sem, 1)
                pool.wait_ge(consts_set.sem, 4)
                nc.gpsimd.memset(shift[:, :, 2 * HEADS:2 * HEADS + 1], 1.0).then_inc(consts_set.sem, 1)
                pool.wait_ge(consts_loaded.sem, 16 * N_CONST)
                nc.gpsimd.tensor_scalar(b_q2s[:, :], b_q2[:, :], QK_SCALE, None, ALU.mult).then_inc(consts_set.sem, 1)

                def low_parts(n, tiles):
                    for j in tiles:
                        pool.wait_ge(part_mid.sem, part_mid.count(n, j + 1))
                        nc.gpsimd.tensor_tensor(parts[:, 2, j, :], rest[:, j, :], parts[:, 1, j, :],
                                                ALU.subtract).then_inc(part_lo.sem, 1)

                def ln_first(m):
                    layernorm_rstd(nc, pool, moments, veps, eps[:, :], half[:, :], rstd, ln_moments, ln_veps, ln_rstd, m)

                def iteration(n, window=True, cross=True, last=False):
                    if window:
                        low_parts(n, (0, 1))
                    if cross:
                        layernorm_rstd(nc, pool, moments2, veps2, eps[:, :], half[:, :], rstd2, ln2_moments, ln2_veps, ln2_rstd, n)
                    if window:
                        low_parts(n, (2, 3))
                    if cross:
                        nc.gpsimd.tensor_tensor(x1b[:, :, :], x1[:, :, :],
                                                b_o2[:, :].unsqueeze(1).broadcast_to([P, TILES, D]),
                                                ALU.add).then_inc(x1b_ready.sem, 1)
                    if window and not last:
                        ln_first(n + 1)

                pool.wait_ge(consts_set.sem, 6)
                ln_first(0)
                iteration(0, cross=False)
                with pool.Fori(1, B - 1) as n:
                    iteration(n)
                iteration(B - 1, last=True)
                iteration(B, window=False)

            @block.vector
            def _(dve):
                def ln_first(m):
                    dve.wait_ge(x_loaded.sem, x_loaded.count(m, 16))
                    layernorm_statistics(nc, dve, x_in, stats, moments, passed, ln_stats, ln_moments, m)
                    layernorm_apply(nc, dve, x_in, xn, moments, rstd, ln_rstd, ln_done, m)

                def split_rest(n, tiles):
                    for j in tiles:
                        ps = work_take(dve, n, ("q0", "q1", "k0", "k1")[j])
                        dve.wait_ge(part_hi.sem, part_hi.count(n, j + 1))
                        nc.vector.scalar_tensor_tensor(rest[:, j, :], ps, QK_SCALE if j < 2 else 1.0, parts[:, 0, j, :],
                                                       ALU.mult, ALU.subtract).then_inc(part_rest.sem, 1)

                def prefix_values(n):
                    ps = work_take(dve, n, "vg")
                    for odd in range(2):
                        nc.vector.tensor_tensor(v_prefix[:, odd, :], ps[:, 0:D], prefix_rows[:, odd, :],
                                                ALU.mult).then_inc(vprefix_ready.sem, 1)

                def maxima(n, first, count, out_of):
                    for f in range(first, first + count):
                        dve.wait_ge(max_full.sem, max_full.count(n, f + 1))
                        out, src = out_of(f - first, ps_max[:, f % 2, :])
                        nc.vector.tensor_reduce(out, src, AX.X, ALU.max).then_inc(max_free.sem, 1)

                def window_fill(f, ps):
                    if f < 4:
                        return top[:, 0, 4 * f:4 * f + 4], ps.rearrange("p (h k) -> p h k", h=4)
                    f -= 4
                    if f < 8:
                        c, j = 1, f
                    else:
                        c, j = 2 + (f - 8) // 9, (f - 8) % 9
                    if j == 8:
                        return top_prefix[:, c - 2, :], ps[:, 0:HEADS * PREFIX].rearrange("p (h k) -> p h k", h=HEADS)
                    return top[:, c, 2 * j:2 * j + 2], ps.rearrange("p (h k) -> p h k", h=2)

                def context_fill(f, ps):
                    c, tile = f // 2, f % 2
                    return top2[:, c, 8 * tile:8 * tile + 8], ps.rearrange("p (h k) -> p h k", h=8)

                def shift_parts(n, tops, out, hi, ready):
                    nc.vector.tensor_scalar(out[:, :, 0:HEADS], tops[:, :, :], -1.0, None,
                                            ALU.mult).then_inc(hi.sem, 1)
                    dve.wait_ge(hi.sem, hi.count(n, 1))
                    nc.vector.scalar_tensor_tensor(out[:, :, HEADS:2 * HEADS], tops[:, :, :], -1.0,
                                                   out[:, :, 0:HEADS], ALU.mult, ALU.subtract
                                                   ).then_inc(ready.sem, 1)

                def normalise(n, k, out):
                    used = k + 1 if k < KD else CROSS_SUMS + 2 * (k - KD) + 2
                    dve.wait_ge(probs_used.sem, probs_used.count(n, used))
                    nc.vector.reciprocal(rden[:, :], ps_out[:, 1, :]).then_inc(out_recip.sem, 1)
                    dve.wait_ge(out_recip.sem, out_recip.count(n, k + 1))
                    nc.vector.tensor_tensor(out[:, k % KD, :], ps_out[:, 0, :], rden[:, :],
                                            ALU.mult).then_inc(out_free.sem, 1)

                def residual(n, names, base, out, sig):
                    for i, name in enumerate(names):
                        ps = work_take(dve, n, name)
                        nc.vector.tensor_tensor(out[:, 2 * i:2 * i + 2, :], ps.rearrange("p (c d) -> p c d", c=2),
                                                base[:, 2 * i:2 * i + 2, :], ALU.add).then_inc(sig.sem, 1)

                def context_keys(n):
                    ps = work_take(dve, n, "k2")
                    for tile in range(KD):
                        nc.vector.scalar_tensor_tensor(
                            k2[:, tile, :, :], ps[:, tile * CTX:(tile + 1) * CTX].unsqueeze(1).broadcast_to([P, 8, CTX]),
                            b_k2[:, tile:tile + 1], head_rows[:, :].unsqueeze(2).broadcast_to([P, 8, CTX]),
                            ALU.add, ALU.mult).then_inc(k2_ready.sem, 1)
                    ps = work_take(dve, n, "v2")
                    nc.vector.tensor_tensor(v2[:, :], ps[:, 0:D], b_v2[:, :], ALU.add).then_inc(v2_biased.sem, 1)
                    dve.wait_ge(v2_biased.sem, v2_biased.count(n, 1))
                    nc.vector.tensor_tensor(v2pair[:, :], v2[:, :], ctx_rows[:, :], ALU.mult).then_inc(v2_ready.sem, 1)

                def iteration(n, window=True, cross=True, last=False):
                    if window:
                        split_rest(n, (0, 1))
                    if cross:
                        dve.wait_ge(xres_loaded.sem, xres_loaded.count(n, 0))
                        residual(n, ("out0", "out1"), x_res, x1, x1_ready)
                        dve.wait_ge(x1_ready.sem, x1_ready.count(n, 2))
                        layernorm_statistics(nc, dve, x1, stats2, moments2, passed, ln2_stats, ln2_moments, n)
                    if window:
                        split_rest(n, (2, 3))
                    if cross:
                        layernorm_apply(nc, dve, x1, xn2, moments2, rstd2, ln2_rstd, ln2_done, n)
                    if window:
                        prefix_values(n)
                    if cross:
                        dve.wait_ge(mask_loaded.sem, mask_loaded.count(n, 0))
                        nc.vector.tensor_scalar(mask_add[:, :, :, :],
                                                mask_in[:, :, :].unsqueeze(2).broadcast_to([P, TILES, 2, CTX]), 0, NEG_MASK,
                                                ALU.is_equal, ALU.mult).then_inc(mask_ready.sem, 1)
                        maxima(n, 0, CROSS_MAX, context_fill)
                        dve.wait_ge(max_free.sem, max_free.count(n, CROSS_MAX))
                        shift_parts(n, top2, shift2, shift2_hi, shift2_ready)
                    if window:
                        maxima(n, CROSS_MAX, WINDOW_MAX, window_fill)
                        dve.wait_ge(max_free.sem, max_free.count(n, CROSS_MAX + WINDOW_MAX))
                        nc.vector.tensor_tensor(top[:, 2:4, :], top[:, 2:4, :], top_prefix[:, :, :],
                                                ALU.max).then_inc(top_joined.sem, 1)
                        dve.wait_ge(top_joined.sem, top_joined.count(n, 1))
                        shift_parts(n, top, shift, shift_hi, shift_ready)
                    if cross:
                        for tile in range(KD):
                            normalise(n, tile, oT2)
                        dve.wait_ge(x1b_ready.sem, x1b_ready.count(n, 1))
                        dve.wait_ge(x2_stored.sem, x2_stored.count(n, 0))
                        residual(n, ("out2_0", "out2_1"), x1b, x2, x2_ready)
                    if window:
                        normalise(n, KD, oT)
                        if not last:
                            ln_first(n + 1)
                        context_keys(n)
                        normalise(n, KD + 1, oT)

                dve.wait_ge(consts_loaded.sem, 16 * N_CONST)
                dve.wait_ge(consts_set.sem, 6)
                dve.sem_inc(max_free.sem, 2)
                dve.sem_inc(out_free.sem, 1)
                dve.sem_inc(x2_stored.sem, 16)
                ln_first(0)
                iteration(0, cross=False)
                with dve.Fori(1, B - 1) as n:
                    iteration(n)
                iteration(B - 1, last=True)
                iteration(B, window=False)

            @block.scalar
            def _(act):
                def copy_out(n, name, sig, pieces):
                    ps = work_take(act, n, name)
                    for out, src in pieces(ps):
                        nc.scalar.activation(out, src, ACT.Copy).then_inc(sig.sem, 1)

                def high_parts(n, tiles):
                    for j in tiles:
                        ps = work_take(act, n, ("q0", "q1", "k0", "k1")[j])
                        nc.scalar.activation(parts[:, 0, j, :], ps, ACT.Copy,
                                             scale=QK_SCALE if j < 2 else 1.0).then_inc(part_hi.sem, 1)
                    for j in tiles:
                        act.wait_ge(part_rest.sem, part_rest.count(n, j + 1))
                        nc.scalar.activation(parts[:, 1, j, :], rest[:, j, :], ACT.Copy).then_inc(part_mid.sem, 1)

                def shift_rows(n, name, out, sig):
                    ps = work_take(act, n, name)
                    nc.scalar.activation(out[:, :], ps.bitcast(BF16)[:, 0:S], ACT.Copy).then_inc(sig.sem, 1)

                def exps(n, user, fills):
                    act.wait_ge(probs_used.sem, probs_used.count(n, user - 1))
                    for f, (lo, width) in fills:
                        act.wait_ge(exp_full.sem, exp_full.count(n, f + 1))
                        nc.scalar.activation(probs[:, user % 2, lo:lo + width], ps_exp[:, f % 2, 0:width],
                                             ACT.Exp).then_inc(exp_done.sem, 1)

                def iteration(n, window=True, cross=True):
                    if window:
                        for k in range(KD):
                            copy_out(n, f"xT{k}", xT_ready, lambda ps: [(xT[:, k, :], ps)])
                        high_parts(n, (0, 1))
                        high_parts(n, (2, 3))
                        for i in range(2):
                            copy_out(n, f"v{i}", v_ready, lambda ps: [
                                (v_half[:, odd, 2 * i:2 * i + 2, :].rearrange("p c (i w) -> p c i w", w=32)[:, :, :, HD * odd:HD * odd + HD],
                                 ps.rearrange("p (c i w) -> p c i w", c=2, w=32)[:, :, :, HD * odd:HD * odd + HD])
                                for odd in range(2)])
                    if cross:
                        for k in range(KD):
                            copy_out(n, f"xT2_{k}", xT2_ready, lambda ps: [(xT2[:, k, :], ps)])
                        for tile in range(KD):
                            ps = work_take(act, n, f"q2_{tile}")
                            nc.scalar.activation(q2T[:, tile, :], ps, ACT.Identity, scale=QK_SCALE,
                                                 bias=b_q2s[:, tile:tile + 1]).then_inc(q2_ready.sem, 1)
                        shift_rows(n, "shiftT2", shiftT2, shiftT2_ready)
                        for tile in range(KD):
                            exps(n, tile, [(4 * tile + j, (512 * j, 512)) for j in range(4)])
                    if window:
                        shift_rows(n, "shiftT", shiftT, shiftT_ready)
                        for g in range(GROUPS):
                            cols = [(HEAD_COLS * j + o, w) for j in range(GROUP) for o, w in ((0, 512), (512, 384))]
                            exps(n, CROSS_SUMS + g, list(enumerate(cols + [(GROUP * HEAD_COLS, 256)], CROSS_EXP + 9 * g)))
                            if g == 1:
                                copy_out(n, "ctxT", ctxT_ready, lambda ps: [
                                    (ctxT[:, :, :, :].rearrange("p k r c -> p (k r c)"), ps[:, 0:KD * P])])

                act.wait_ge(consts_set.sem, 6)
                act.wait_ge(consts_loaded.sem, 16 * N_CONST)
                act.sem_inc(exp_done.sem, 2)
                iteration(0, cross=False)
                with act.Fori(1, B) as n:
                    iteration(n)
                iteration(B, window=False)

            @block.tensor
            def _(pe):
                def features(n):
                    for k in range(KD):
                        ps = work_claim(pe, n, f"xT{k}")
                        pe.wait_ge(ln_done.sem, ln_done.count(n, TILES))
                        for c in range(TILES):
                            mm = nc.tensor.transpose(ps[:, c * P:(c + 1) * P], xn[:, c, k * P:(k + 1) * P], identf[:, :])
                        mm.then_inc(work_full.sem, 1)

                def queries_or_keys(n, tiles):
                    pe.wait_ge(xT_ready.sem, xT_ready.count(n, KD))
                    for j in tiles:
                        ps = work_claim(pe, n, ("q0", "q1", "k0", "k1")[j])
                        for k in range(KD):
                            mm = nc.tensor.matmul(ps, w_qkv[:, k, j * P:(j + 1) * P], xT[:, k, :],
                                                  start=(k == 0), stop=(k == KD - 1))
                        mm.then_inc(work_full.sem, 1)

                def values(n):
                    for i in range(2):
                        ps = work_claim(pe, n, f"v{i}")
                        for c in (2 * i, 2 * i + 1):
                            for k in range(KD):
                                mm = nc.tensor.matmul(ps[:, (c % 2) * D:(c % 2 + 1) * D], xT[:, k, c * P:(c + 1) * P],
                                                      w_qkv[:, k, 2 * D:3 * D], start=(k == 0 and c % 2 == 0),
                                                      stop=(k == KD - 1), skip_group_check=True)
                        mm.then_inc(work_full.sem, 1)
                    ps = work_claim(pe, n, "vg")
                    for r in range(GROUP):
                        for k in range(KD):
                            mm = nc.tensor.matmul(ps[32 * r:32 * r + 32, 0:D], xT[:, k, 0:32], w_qkv[:, k, 2 * D:3 * D],
                                                  start=(k == 0), stop=(k == KD - 1), skip_group_check=True)
                    mm.then_inc(work_full.sem, 1)

                def max_claim(n, f):
                    pe.wait_ge(max_free.sem, max_free.count(n, f - 1))
                    return ps_max[:, f % 2, :]

                def window_scores(n, f):
                    if f < 4:
                        c, j, heads, width, mask = 0, f, 4, P, mask_qk[:, 1, P:2 * P]
                    else:
                        c = 1 if f < 12 else 2 + (f - 12) // 9
                        j = f - 4 if f < 12 else (f - 12) % 9
                        heads, width, mask = 2, 2 * P, mask_qk[:, min(c, 2) - 1, :]
                    q0 = c * P
                    ps = max_claim(n, CROSS_MAX + f)
                    if j < HEADS // heads:
                        nc.tensor.matmul(ps.rearrange("p (h k) -> p h k", h=heads), ident[:, :],
                                         mask.unsqueeze(1).broadcast_to([P, heads, width]),
                                         start=True, stop=False, skip_group_check=True)
                        for i in range(heads):
                            h = heads * j + i
                            mm = nc.tensor.matmul(ps[:, i * width:(i + 1) * width], q_rows[:, h, q0:q0 + P],
                                                  k_rows[:, h, q0 + P - width:q0 + P], start=False,
                                                  stop=True, skip_group_check=True)
                    else:
                        for h in range(HEADS):
                            mm = nc.tensor.matmul(ps[:, h * PREFIX:(h + 1) * PREFIX], q_rows[:, h, q0:q0 + P],
                                                  k_rows[:, h, 0:PREFIX], start=(h == 0), stop=True,
                                                  skip_group_check=True)
                    mm.then_inc(max_full.sem, 1)

                def shift_transposes(n, name, src, ready):
                    ps = work_claim(pe, n, name)
                    pe.wait_ge(ready.sem, ready.count(n, 1))
                    for c in range(TILES):
                        mm = nc.tensor.transpose(ps.bitcast(BF16)[:, c * P:(c + 1) * P], src[:, c, :], ident[:, :])
                    mm.then_inc(work_full.sem, 1)

                def exp_claim(n, f):
                    pe.wait_ge(exp_done.sem, exp_done.count(n, f - 1))
                    return ps_exp[:, f % 2, :]

                def window_shifted(n, g):
                    def add(ps, col, lhsT, rhs):
                        width = rhs.shape[-1]
                        return nc.tensor.matmul(ps[:, col:col + width], lhsT, rhs, start=False, stop=True,
                                                skip_group_check=True)
                    f = CROSS_EXP + 9 * g
                    for h in group_heads(g):
                        for tiles, lo, width in (((0, 1), 0, 512), ((2, 3), 256, 384)):
                            ps = exp_claim(n, f)
                            nc.tensor.matmul(ps[:, 0:width], ident[:, :], mask_kq[:, lo:lo + width] if lo == 0 else mask_kq[:, 256:640],
                                             start=True, stop=False, skip_group_check=True)
                            for i, kt in enumerate(tiles):
                                q0, q1 = kt * P, min(kt + 2, TILES) * P
                                add(ps, 256 * i, sel[:, h, :], shiftT[:, q0:q1])
                                mm = add(ps, 256 * i, k_rows[:, h, kt * P:(kt + 1) * P], q_rows[:, h, q0:q1])
                            mm.then_inc(exp_full.sem, 1)
                            f += 1
                    ps = exp_claim(n, f)
                    nc.tensor.matmul(ps[:, 0:256], sel_prefix[:, g, :], shiftT[:, 256:512], start=True, stop=False,
                                     skip_group_check=True)
                    for j, h in enumerate(group_heads(g)):
                        mm = nc.tensor.matmul(ps[32 * j:32 * j + 32, 0:256], k_rows[:, h, 0:32], q_rows[:, h, 256:512],
                                              start=False, stop=True, skip_group_check=True)
                    mm.then_inc(exp_full.sem, 1)

                def out_claim(n, k):
                    pe.wait_ge(out_free.sem, out_free.count(n, k))

                def window_values(n, g):
                    tile, odd = g // 2, g % 2
                    pr = probs[:, g % 2, :]
                    if odd == 0:
                        out_claim(n, KD + tile)
                    pe.wait_ge(exp_done.sem, exp_done.count(n, CROSS_EXP + 9 * g + 9))
                    if g == 0:
                        pe.wait_ge(v_ready.sem, v_ready.count(n, 4))
                        pe.wait_ge(vprefix_ready.sem, vprefix_ready.count(n, 2))
                    for kt in range(TILES + 1):
                        for side in range(2):
                            for j in range(GROUP):
                                w = slice(32 * (4 * tile + j), 32 * (4 * tile + j) + 32)
                                if kt < TILES:
                                    q0, q1 = kt * P, min(kt + 2, TILES) * P
                                    lhsT = v_half[:, odd, kt, w] if side == 0 else half_cols[:, odd, :]
                                    rhs = pr[:, HEAD_COLS * j + 256 * kt:HEAD_COLS * j + 256 * kt + q1 - q0]
                                else:
                                    q0, q1 = 256, 512
                                    lhsT = v_prefix[:, odd, w] if side == 0 else prefix_rows[:, odd, 32 * j:32 * j + 32]
                                    rhs = pr[:, GROUP * HEAD_COLS:GROUP * HEAD_COLS + 256]
                                mm = nc.tensor.matmul(ps_out[32 * j:32 * j + 32, side, q0:q1], lhsT, rhs,
                                                      start=(kt == 0 and odd == 0), stop=True, skip_group_check=True)
                    mm.then_inc(probs_used.sem, 1)

                def output(n, names, src, w, k):
                    pe.wait_ge(out_free.sem, out_free.count(n, k))
                    for i, name in enumerate(names):
                        ps = work_claim(pe, n, name)
                        for c in (2 * i, 2 * i + 1):
                            for tile in range(KD):
                                mm = nc.tensor.matmul(ps[:, (c % 2) * D:(c % 2 + 1) * D], src[:, tile, c * P:(c + 1) * P],
                                                      w[:, tile, :], start=(tile == 0 and c % 2 == 0),
                                                      stop=(tile == KD - 1), skip_group_check=True)
                        mm.then_inc(work_full.sem, 1)

                def context_features(n):
                    ps = work_claim(pe, n, "ctxT")
                    pe.wait_ge(ctx_loaded.sem, ctx_loaded.count(n, 32))
                    for k in range(KD):
                        mm = nc.tensor.transpose(ps[:, k * P:(k + 1) * P], ctx_in[:, k * P:(k + 1) * P], identf[:, :])
                    mm.then_inc(work_full.sem, 1)

                def context_kv(n):
                    ps = work_claim(pe, n, "k2")
                    pe.wait_ge(ctxT_ready.sem, ctxT_ready.count(n, 1))
                    for tile in range(KD):
                        for k in range(KD):
                            mm = nc.tensor.matmul(ps[:, tile * CTX:(tile + 1) * CTX], w_k2[:, k, tile * P:(tile + 1) * P],
                                                  ctxT[:, k, 0, :], start=(tile == 0 and k == 0), stop=(k == KD - 1),
                                                  skip_group_check=True)
                    mm.then_inc(work_full.sem, 1)
                    ps = work_claim(pe, n, "v2")
                    for k in range(KD):
                        mm = nc.tensor.matmul(ps[:, 0:D], ctxT[:, k, :, :].rearrange("p r c -> p (r c)"), w_v2[:, k, :],
                                              start=(k == 0), stop=(k == KD - 1))
                    mm.then_inc(work_full.sem, 1)

                def context_queries(n):
                    for k in range(KD):
                        ps = work_claim(pe, n, f"xT2_{k}")
                        pe.wait_ge(ln2_done.sem, ln2_done.count(n, TILES))
                        for c in range(TILES):
                            mm = nc.tensor.transpose(ps[:, c * P:(c + 1) * P], xn2[:, c, k * P:(k + 1) * P], identf[:, :])
                        mm.then_inc(work_full.sem, 1)
                    pe.wait_ge(xT2_ready.sem, xT2_ready.count(n, KD))
                    for tile in range(KD):
                        ps = work_claim(pe, n, f"q2_{tile}")
                        for k in range(KD):
                            mm = nc.tensor.matmul(ps, w_q2[:, k, tile * P:(tile + 1) * P], xT2[:, k, :],
                                                  start=(k == 0), stop=(k == KD - 1))
                        mm.then_inc(work_full.sem, 1)

                def context_scores(n):
                    pe.wait_ge(mask_ready.sem, mask_ready.count(n, 1))
                    pe.wait_ge(k2_ready.sem, k2_ready.count(n, 0))
                    pe.wait_ge(q2_ready.sem, q2_ready.count(n, 2))
                    for c in range(TILES):
                        for tile in range(KD):
                            ps = max_claim(n, 2 * c + tile)
                            nc.tensor.matmul(ps.rearrange("p (h k) -> p h k", h=8), ident[:, :],
                                             mask_add[:, c, 0, :].unsqueeze(1).broadcast_to([P, 8, CTX]),
                                             start=True, stop=False, skip_group_check=True)
                            nc.tensor.matmul(ps, q2T[:, tile, c * P:(c + 1) * P],
                                             k2[:, tile, :, :].rearrange("p h k -> p (h k)"),
                                             start=False, stop=True, skip_group_check=True).then_inc(max_full.sem, 1)

                def context_shifted(n, i):
                    tile = i // 4
                    ps = exp_claim(n, i)
                    for c in range(TILES):
                        nc.tensor.matmul(ps[:, c * P:(c + 1) * P], mask_add[:, c, :, :].rearrange("p r k -> p (r k)"),
                                         ident[:, :], start=(c == 0), stop=False, skip_group_check=True)
                    nc.tensor.matmul(ps, k2[:, tile, 2 * (i % 4):2 * (i % 4) + 2, :].rearrange("p h k -> p (h k)"),
                                     q2T[:, tile, :], start=False, stop=False, skip_group_check=True)
                    if i == 0:
                        pe.wait_ge(shiftT2_ready.sem, shiftT2_ready.count(n, 1))
                    nc.tensor.matmul(ps, sel_pair[:, i, :], shiftT2[:, :], start=False, stop=True,
                                     skip_group_check=True).then_inc(exp_full.sem, 1)

                def context_values(n, tile):
                    if tile == 0:
                        pe.wait_ge(v2_ready.sem, v2_ready.count(n, 0))
                    out_claim(n, tile)
                    pe.wait_ge(exp_done.sem, exp_done.count(n, 4 * tile + 4))
                    for side in range(2):
                        for j in range(GROUP):
                            w = slice(32 * (4 * tile + j), 32 * (4 * tile + j) + 32)
                            mm = nc.tensor.matmul(ps_out[32 * j:32 * j + 32, side, :],
                                                  v2pair[:, w] if side == 0 else ctx_rows[:, 0:32],
                                                  probs[:, tile, 512 * j:512 * j + 512],
                                                  start=True, stop=True, skip_group_check=True)
                    mm.then_inc(probs_used.sem, 1)

                def iteration(n, window=True, cross=True):
                    if window:
                        features(n)
                        queries_or_keys(n, (0, 1))
                    if cross:
                        output(n, ("out0", "out1"), oT, w_out, 0)
                    if window:
                        queries_or_keys(n, (2, 3))
                        values(n)
                    if cross:
                        context_queries(n)
                        context_scores(n)
                    ahead = WINDOW_MAX - 3 * PAIRS
                    if window:
                        pe.wait_ge(rows_loaded.sem, rows_loaded.count(n, 16 * 12))
                        for f in range(ahead):
                            window_scores(n, f)
                    if cross:
                        shift_transposes(n, "shiftT2", shift2, shift2_ready)
                    for i in range(PAIRS):
                        if cross:
                            context_shifted(n, i)
                        if window:
                            for f in range(ahead + 3 * i, ahead + 3 * i + 3):
                                window_scores(n, f)
                    if cross:
                        context_values(n, 0)
                    if window:
                        shift_transposes(n, "shiftT", shift, shift_ready)
                        pe.wait_ge(shiftT_ready.sem, shiftT_ready.count(n, 1))
                        window_shifted(n, 0)
                    if cross:
                        context_values(n, 1)
                    if window:
                        window_shifted(n, 1)
                        window_values(n, 0)
                    if cross:
                        output(n, ("out2_0", "out2_1"), oT2, w_o2, KD)
                    if window:
                        context_features(n)
                        window_shifted(n, 2)
                        window_values(n, 1)
                        window_shifted(n, 3)
                        window_values(n, 2)
                        context_kv(n)
                        window_values(n, 3)

                pe.wait_ge(consts_loaded.sem, 16 * N_CONST)
                pe.sem_inc(probs_used.sem, 2)
                iteration(0, cross=False)
                with pe.Fori(1, B) as n:
                    iteration(n)
                iteration(B, window=False)


N_CONST = 1 + KD + 10 + 5 + 4
REGION = B * S + P
SPARE_TILES = 10
ROW = 2 * D + 4
NO_TOKEN = float(1 << 20)
E, DF = 8, 1024
KF = DF // P
MH, MD = 4, 64
M_SCALE = MD ** -0.5
POS = 16
NGROUPS = S // (TILES * POS)
STEPS = B * S // P + E
TABLE = STEPS + 2

ROUTE_FILLS = ["out0", "out1", "yT0", "yT1", "logits", "ranks", "totals"]
MIX_FILLS = ["xT0", "xT1", "q0", "q1", "out0", "out1", "k0", "k1", "v0", "v1", "yT0", "yT1", "logits", "ranks",
             "totals", "shiftT"]
MIX_WORK = [f for f in MIX_FILLS if f not in ROUTE_FILLS]


def mixing_constants(ctx, nc, t):
    shapes = {
        "identf": ([P, P], F32, "c_identity"), "ident": ([P, P], BF16, "c_identity16"),
        "mask_pos": ([P, P], BF16, "c_mask_pos"),
        "sel_head": ([P, MH, P], BF16, "c_sel_head"),
        "before": ([P, P], BF16, "c_before"),
        "head_half": ([P, 2], F32, "c_head_half"),
        "descending": ([P, E], F32, "c_descending"),
        "region0": ([P, E], F32, "c_region0"),
        "token0": ([P, TILES], F32, "c_token0"),
        "tile_rows": ([P, 64], F32, "c_tile_rows"),
        "upto": ([P, E * E], F32, "c_upto"),
        "steps": ([P, TABLE], F32, "c_steps"),
        "w_qkv": ([P, KD, 3 * D], F32, "m_w_qkvT"), "w_o": ([P, KD, D], F32, "m_w_oT"), "w_g": ([P, KD, E], F32, "m_w_gT"),
        "b_q": ([P, KD], F32, "m_b_q"), "b_k": ([P, KD], F32, "m_b_k"), "b_v": ([P, D], F32, "m_b_v"),
        "b_o": ([P, D], F32, "m_b_o"), "g1": ([P, D], F32, "m_g1"), "be1": ([P, D], F32, "m_be1"),
    }
    consts, loads = {}, []
    for name, (shape, dt, src) in shapes.items():
        tensor = consts[name] = ctx.enter_context(nc.sbuf_tensor("m_" + name, shape, dt))
        if name.startswith("w_"):
            loads.append((tensor[:, :, :], t[src].rearrange("(k p) n -> p k n", p=P)))
        elif name in ("b_v", "b_o", "g1", "be1"):
            loads.append((tensor[:, :], t[src].partition_broadcast(P)))
        elif len(shape) == 3:
            loads.append((tensor[:, :, :], t[src]))
        else:
            loads.append((tensor[:, :], t[src]))
    return consts, loads


def mixing_program(nc, t, mem, consts, keep):
    ctx = ExitStack()
    with ctx:
        def sb(name, shape, dt=F32):
            return ctx.enter_context(nc.sbuf_tensor(name, shape, dt))

        def signal(name, per, ahead=0):
            return Signal(ctx, nc, name, per, ahead)

        def route_signal(name, per, ahead=0):
            return Signal(ctx, nc, name, per, ahead - per)

        (identf, ident, mask_pos, sel_head, before, head_half, descending, region0, token0, tile_rows, upto, steps,
         w_qkv, w_o, w_g, b_q, b_k, b_v, b_o, g1, be1) = consts.values()
        ones16 = sb("ones16", [P, P], BF16)
        ones64 = sb("ones64", [P, MD])
        b_qs = sb("m_b_qs", [P, KD])
        half = sb("m_half", [P, TILES])
        eps = sb("m_eps", [P, TILES])
        x_in = sb("m_x_in", [P, TILES, D])
        stats = sb("m_stats", [P, TILES, 6])
        moments = sb("m_moments", [P, TILES, 2])
        veps = sb("m_veps", [P, TILES])
        rstd = sb("m_rstd", [P, TILES])
        stats1 = sb("m_stats1", [P, TILES, 6])
        moments1 = sb("m_moments1", [P, TILES, 2])
        veps1 = sb("m_veps1", [P, TILES])
        rstd1 = sb("m_rstd1", [P, TILES])
        xn = sb("m_xn", [P, TILES, D])
        xnb = sb("m_xnb", [P, TILES, D])
        xT = sb("m_xT", [P, KD, S])
        qT = sb("m_qT", [P, KD, S])
        kT = sb("m_kT", [P, MH, S])
        v = sb("m_v", [P, TILES, D])
        top = sb("m_top", [P, TILES, MH])
        shift = sb("m_shift", [P, TILES, P], BF16)
        shiftT = sb("m_shiftT", [P, S], BF16)
        probs = sb("m_probs", [P, 2, MH * P])
        rden = sb("m_rden", [P, 2, D])
        oT = sb("m_oT", [P, KD, S])
        mixed = sb("m_mixed", [P, TILES, D])
        rows = sb("m_rows", [P, TILES, ROW])
        yT = oT
        best = sb("m_best", [P, TILES])
        is_best = sb("m_is_best", [P, TILES, E])
        order = sb("m_order", [P, TILES, E])
        first = sb("m_first", [P, TILES])
        chosen = sb("m_chosen", [P, TILES, E], BF16)
        place = sb("m_place", [P, TILES, E])
        own_place = sb("m_own_place", [P, TILES, E])
        slot_f = sb("m_slot_f", [P, TILES])
        slot = sb("m_slot", [P, TILES], U32)
        next_row = sb("m_next_row", [P, 2, E])
        token = sb("m_token", [P, TILES])
        filler = sb("m_filler", [P, ROW])
        filler_row = sb("m_filler_row", [P, E], I32)
        counts = sb("m_counts", [P, E])
        tiles_of = sb("m_tiles_of", [P, E])
        tiles_upto_all = sb("m_tiles_upto_all", [P, E, E])
        tiles_upto = sb("m_tiles_upto", [P, E])
        expert_f = sb("m_expert_f", [P, TABLE])
        step0 = sb("m_step0", [P, TABLE])
        row_a = sb("m_row_a", [P, TABLE])
        row_b = sb("m_row_b", [P, TABLE])
        row_f = sb("m_row_f", [P, TABLE])
        tile_need = probs[:, 0, :].rearrange("p (e k) -> p e k", e=E)
        gone = probs[:, 1, 0:TABLE * E].rearrange("p (j e) -> p j e", e=E)
        passed_tiles = qT[:, 0, 0:TABLE * E].rearrange("p (j e) -> p j e", e=E)
        ps_max, ps_exp, ps_out, ps_work = mem["ps_a"], mem["ps_b"], mem["ps_c"], mem["ps_d"]

        consts_set = signal("m_consts_set", 0)
        x_loaded = signal("m_x_loaded", 16 * B)
        rows_loaded = signal("m_rows_loaded", 16 * B)
        ln_stats = signal("m_ln_stats", TILES)
        ln_moments = signal("m_ln_moments", TILES)
        ln_veps = signal("m_ln_veps", 1)
        ln_rstd = signal("m_ln_rstd", 1)
        ln_done = signal("m_ln_done", TILES)
        xnb_ready = signal("m_xnb_ready", 1)
        ln1_stats = route_signal("m_ln1_stats", TILES)
        ln1_moments = route_signal("m_ln1_moments", TILES)
        ln1_veps = route_signal("m_ln1_veps", 1)
        ln1_rstd = route_signal("m_ln1_rstd", 1)
        ln1_scaled = route_signal("m_ln1_scaled", TILES)
        y_ready = route_signal("m_y_ready", TILES)
        work_full = signal("m_work_full", len(MIX_FILLS), -len(ROUTE_FILLS))
        xT_ready = signal("m_xT_ready", KD)
        q_ready = signal("m_q_ready", KD)
        k_ready = signal("m_k_ready", MH)
        v_ready = signal("m_v_ready", 2)
        max_full = signal("m_max_full", TILES)
        max_free = signal("m_max_free", TILES, 2)
        shift_hi = signal("m_shift_hi", 1)
        shift_ready = signal("m_shift_ready", 1)
        shiftT_ready = signal("m_shiftT_ready", 1)
        exp_full = signal("m_exp_full", TILES)
        exp_done = signal("m_exp_done", TILES, 2)
        probs_used = signal("m_probs_used", TILES, 2)
        recip_done = signal("m_recip_done", TILES)
        out_free = signal("m_out_free", TILES, 2)
        mixed_ready = route_signal("m_mixed_ready", 2)
        yT_ready = route_signal("m_yT_ready", KD)
        best_ready = route_signal("m_best_ready", 1)
        is_best_ready = route_signal("m_is_best_ready", 1)
        order_ready = route_signal("m_order_ready", 1)
        first_ready = route_signal("m_first_ready", 1)
        chosen_ready = route_signal("m_chosen_ready", 1)
        place_ready = route_signal("m_place_ready", 1)
        own_place_ready = route_signal("m_own_place_ready", 1)
        slot_f_ready = route_signal("m_slot_f_ready", 1)
        slot_ready = route_signal("m_slot_ready", 1)
        next_row_ready = route_signal("m_next_row_ready", 1, 1)
        next_row_kept = route_signal("m_next_row_kept", 1, 1)
        token_written = route_signal("m_token_written", 1)
        token_next = route_signal("m_token_next", 1, 1)
        rows_sent = route_signal("m_rows_sent", 16 * TILES, 16)
        filler_sent = signal("m_filler_sent", 0)
        tables = signal("m_tables", 0)
        weights_loaded = signal("m_weights_loaded", 0)
        passed = signal("m_waits_passed_vector", 0)
        pool_passed = signal("m_waits_passed_pool", 0)
        sp_passed = signal("m_waits_passed_sync", 0)

        def released(n, name):
            kind, k = name.rstrip("01"), int(name[-1]) if name[-1] in "01" else 0
            sig, count = {
                "xT": (xT_ready, k + 1), "q": (q_ready, k + 1), "k": (k_ready, 2 * k + 2), "v": (v_ready, k + 1),
                "shiftT": (shiftT_ready, 1), "out": (mixed_ready, k + 1), "yT": (yT_ready, k + 1),
                "logits": (is_best_ready, 1), "ranks": (place_ready, 1), "totals": (next_row_ready, 1),
            }[kind]
            return sig.sem, sig.count(n, count)

        def work_place(n, name):
            if isinstance(n, int) and n == 0:
                j = MIX_WORK.index(name)
                return MIX_WORK, j, j % 2
            order = ROUTE_FILLS if isinstance(n, int) and n == NGROUPS else MIX_FILLS
            j = order.index(name)
            return order, j, (j + len(MIX_WORK)) % 2

        def work_claim(pe, n, name):
            order, j, bank = work_place(n, name)
            if j >= 2:
                pe.wait_ge(*released(n, order[j - 2]))
            elif order is not MIX_WORK:
                pe.wait_ge(*released(n - 1, MIX_FILLS[j - 2]))
            return ps_work[:, bank, :]

        def work_take(eng, n, name):
            order, j, bank = work_place(n, name)
            eng.wait_ge(work_full.sem, j + 1 if order is MIX_WORK else work_full.count(n, j + 1))
            return ps_work[:, bank, :]

        with nc.Block() as block:

            @block.sync
            def _(sp):
                def load_x(m):
                    for s in range(B):
                        sp.dma_start(x_in[s * POS:(s + 1) * POS, :, :],
                                     t["x2_groups"][m, s].rearrange("(c i) d -> i c d", i=POS)).then_inc(x_loaded.sem, 16)

                def load_rows(m):
                    for s in range(B):
                        sp.dma_start(rows[s * POS:(s + 1) * POS, :, D:2 * D],
                                     t["x2_groups"][m, s].rearrange("(c i) d -> i c d", i=POS)).then_inc(rows_loaded.sem, 16)

                def load_expert(e):
                    for k in range(KD):
                        sp.dma_start(keep["w1"][:, k, bass.ds(e * DF, DF)],
                                     t["e_w1"][e, k * P:(k + 1) * P, :]).then_inc(weights_loaded.sem, 16)
                    sp.dma_start(keep["w2"][:, bass.ds(e * KF * D, KF * D)].rearrange("p (j d) -> p j d", j=KF),
                                 t["e_w2"][e].rearrange("(j p) d -> p j d", p=P)).then_inc(weights_loaded.sem, 16)

                def iteration(n, last):
                    if not last:
                        sp.wait_ge(ln_done.sem, ln_done.count(n, TILES))
                        load_x(n + 1)
                    load_expert(n)
                    if not (isinstance(n, int) and n == 0):
                        sp.wait_ge(rows_sent.sem, rows_sent.count(n, 16 * TILES))
                    load_rows(n)

                load_x(0)
                sp.dma_start(keep["b1"][:, :], t["e_b1"]).then_inc(weights_loaded.sem, 16)
                iteration(0, False)
                sp.wait_ge(consts_set.sem, 8)
                for i in range(1, SPARE_TILES):
                    sp.dma_start(t["sorted"][E * REGION + i * P:E * REGION + (i + 1) * P, :],
                                 filler[:, :]).then_inc(filler_sent.sem, 16)
                with sp.Fori(1, NGROUPS - 1) as n:
                    iteration(n, False)
                iteration(NGROUPS - 1, True)
                sp.wait_ge(tables.sem, 1)
                for e in range(E):
                    row0 = sp.value_load(filler_row[0:1, e:e + 1], min_val=0, max_val=E * REGION - P)
                    sp.dma_start(t["sorted"][bass.ds(row0, P), :], filler[:, :]).then_inc(filler_sent.sem, 16)
                sp.wait_ge(weights_loaded.sem, 16 * (1 + E * (KD + 1)))
                sp.wait_ge(filler_sent.sem, 16 * (SPARE_TILES - 1 + E))

            @block.gpsimd
            def _(pool):
                nc.gpsimd.memset(half[:, :], -0.5).then_inc(consts_set.sem, 1)
                nc.gpsimd.memset(eps[:, :], EPS).then_inc(consts_set.sem, 1)
                nc.gpsimd.memset(shift[:, :, :], 0.0).then_inc(consts_set.sem, 1)
                nc.gpsimd.memset(ones16[:, :], 1.0).then_inc(consts_set.sem, 1)
                nc.gpsimd.memset(ones64[:, :], 1.0).then_inc(consts_set.sem, 1)
                nc.gpsimd.memset(rows[:, :, 2 * D:ROW], 0.0).then_inc(consts_set.sem, 1)
                nc.gpsimd.memset(filler[:, :], 0.0).then_inc(consts_set.sem, 1)
                pool.wait_ge(consts_set.sem, 7)
                nc.gpsimd.memset(filler[:, 2 * D:2 * D + 1], NO_TOKEN).then_inc(consts_set.sem, 1)
                nc.gpsimd.tensor_scalar(b_qs[:, :], b_q[:, :], M_SCALE, None, ALU.mult).then_inc(consts_set.sem, 1)
                nc.gpsimd.tensor_copy(token[:, :], token0[:, :]).then_inc(token_next.sem, 1)
                pool.wait_ge(consts_set.sem, 9)
                pool.dma_start(t["sorted"][E * REGION:E * REGION + P, :], filler[:, :]).then_inc(rows_sent.sem, 16)

                def ln_first(m):
                    layernorm_rstd(nc, pool, moments, veps, eps[:, :], half[:, :], rstd, ln_moments, ln_veps, ln_rstd, m)

                def bias(n):
                    pool.wait_ge(ln_done.sem, ln_done.count(n, TILES))
                    nc.gpsimd.tensor_tensor(xnb[:, :, :], xn[:, :, :], b_o[:, :].unsqueeze(1).broadcast_to([P, TILES, D]),
                                            ALU.add).then_inc(xnb_ready.sem, 1)

                def iteration(n, work=True, route=True, last=False):
                    if route:
                        wait_apart(pool, pool_passed, rows_sent.sem, rows_sent.count(n, 0))
                        wait_apart(pool, pool_passed, token_next.sem, token_next.count(n, 0))
                        nc.gpsimd.tensor_copy(rows[:, :, 2 * D], token[:, :]).then_inc(token_written.sem, 1)
                        wait_apart(pool, pool_passed, token_written.sem, token_written.count(n, 1))
                        nc.gpsimd.tensor_scalar(token[:, :], token[:, :], float(TILES * POS), None,
                                                ALU.add).then_inc(token_next.sem, 1)
                        layernorm_rstd(nc, pool, moments1, veps1, eps[:, :], half[:, :], rstd1, ln1_moments, ln1_veps, ln1_rstd, n)
                        if work:
                            pool.wait_ge(mixed_ready.sem, mixed_ready.count(n, 2))
                    if work:
                        bias(n)
                    if route:
                        wait_apart(pool, pool_passed, rows_loaded.sem, rows_loaded.count(n, 0))
                        wait_apart(pool, pool_passed, y_ready.sem, y_ready.count(n, TILES))
                        wait_apart(pool, pool_passed, slot_ready.sem, slot_ready.count(n, 1))
                        for c in range(TILES):
                            nc.gpsimd.indirect_dma_start(
                                out=t["sorted"], out_offset=bass.IndirectOffsetOnAxis(ap=slot[:, c:c + 1], axis=0),
                                in_=rows[:, c, :], in_offset=None).then_inc(rows_sent.sem, 16)
                    if work and not last:
                        ln_first(n + 1)

                ln_first(0)
                iteration(0, route=False)
                with pool.Fori(1, NGROUPS - 1) as n:
                    iteration(n)
                iteration(NGROUPS - 1, last=True)
                iteration(NGROUPS, work=False)
                pool.wait_ge(rows_sent.sem, rows_sent.count(NGROUPS, 16 * TILES))

            @block.vector
            def _(dve):
                def ln_statistics(m):
                    dve.wait_ge(x_loaded.sem, x_loaded.count(m, 16 * B))
                    layernorm_statistics(nc, dve, x_in, stats, moments, passed, ln_stats, ln_moments, m)

                def ln_apply(m):
                    if not (isinstance(m, int) and m == 0):
                        dve.wait_ge(xnb_ready.sem, xnb_ready.count(m, 0))
                    layernorm_apply(nc, dve, x_in, xn, moments, rstd, ln_rstd, ln_done, m)

                def keys(n):
                    for tile in range(KD):
                        ps = work_take(dve, n, f"k{tile}")
                        for odd in range(2):
                            nc.vector.tensor_scalar(kT[:, 2 * tile + odd, :], ps, b_k[:, tile:tile + 1],
                                                    head_half[:, odd:odd + 1], ALU.add, ALU.mult).then_inc(k_ready.sem, 1)

                def values(n):
                    for i in range(2):
                        ps = work_take(dve, n, f"v{i}")
                        nc.vector.tensor_tensor(v[:, 2 * i:2 * i + 2, :], ps.rearrange("p (c d) -> p c d", c=2),
                                                b_v[:, :].unsqueeze(1).broadcast_to([P, 2, D]),
                                                ALU.add).then_inc(v_ready.sem, 1)

                def maxima(n, tiles):
                    for c in tiles:
                        dve.wait_ge(max_full.sem, max_full.count(n, c + 1))
                        nc.vector.tensor_reduce(top[:, c, :], ps_max[:, c % 2, :].rearrange("p (h k) -> p h k", h=MH),
                                                AX.X, ALU.max).then_inc(max_free.sem, 1)

                def shift_parts(n):
                    dve.wait_ge(max_free.sem, max_free.count(n, TILES))
                    nc.vector.tensor_scalar(shift[:, :, 0:MH], top[:, :, :], -1.0, None, ALU.mult).then_inc(shift_hi.sem, 1)
                    dve.wait_ge(shift_hi.sem, shift_hi.count(n, 1))
                    nc.vector.scalar_tensor_tensor(shift[:, :, MH:2 * MH], top[:, :, :], -1.0, shift[:, :, 0:MH],
                                                   ALU.mult, ALU.subtract).then_inc(shift_ready.sem, 1)

                def normalise(n, c):
                    dve.wait_ge(probs_used.sem, probs_used.count(n, c + 1))
                    nc.vector.reciprocal(rden[:, c % 2, :], ps_out[:, c % 2, D:2 * D]).then_inc(recip_done.sem, 1)
                    dve.wait_ge(recip_done.sem, recip_done.count(n, c + 1))
                    nc.vector.tensor_tensor(oT[:, :, c * P:(c + 1) * P],
                                            ps_out[:, c % 2, 0:D].rearrange("p (t q) -> p t q", t=KD),
                                            rden[:, c % 2, :].rearrange("p (t q) -> p t q", t=KD),
                                            ALU.mult).then_inc(out_free.sem, 1)

                def post_norm_statistics(n):
                    dve.wait_ge(xnb_ready.sem, xnb_ready.count(n, 0))
                    for i in range(2):
                        ps = work_take(dve, n, f"out{i}")
                        nc.vector.tensor_tensor(mixed[:, 2 * i:2 * i + 2, :], ps.rearrange("p (c d) -> p c d", c=2),
                                                xnb[:, 2 * i:2 * i + 2, :], ALU.add).then_inc(mixed_ready.sem, 1)
                    dve.wait_ge(mixed_ready.sem, mixed_ready.count(n, 2))
                    layernorm_statistics(nc, dve, mixed, stats1, moments1, passed, ln1_stats, ln1_moments, n)
                    dve.wait_ge(ln1_moments.sem, ln1_moments.count(n, TILES))
                    for c in range(TILES):
                        nc.vector.scalar_tensor_tensor(mixed[:, c, :], mixed[:, c, :], moments1[:, c, 0:1], g1[:, :],
                                                       ALU.subtract, ALU.mult).then_inc(ln1_scaled.sem, 1)

                def post_norm_apply(n):
                    dve.wait_ge(ln1_rstd.sem, ln1_rstd.count(n, 1))
                    dve.wait_ge(ln1_scaled.sem, ln1_scaled.count(n, TILES))
                    dve.wait_ge(rows_sent.sem, rows_sent.count(n, 0))
                    for c in range(TILES):
                        nc.vector.scalar_tensor_tensor(rows[:, c, 0:D], mixed[:, c, :], rstd1[:, c:c + 1], be1[:, :],
                                                       ALU.mult, ALU.add).then_inc(y_ready.sem, 1)

                def choose(n):
                    wide = [P, TILES, E]
                    ps = work_take(dve, n, "logits")[:, 0:TILES * E].rearrange("p (c e) -> p c e", c=TILES)
                    nc.vector.tensor_reduce(best[:, :], ps, AX.X, ALU.max).then_inc(best_ready.sem, 1)
                    dve.wait_ge(best_ready.sem, best_ready.count(n, 1))
                    nc.vector.tensor_tensor(is_best[:, :, :], ps, best[:, :].unsqueeze(2).broadcast_to(wide),
                                            ALU.is_equal).then_inc(is_best_ready.sem, 1)
                    dve.wait_ge(is_best_ready.sem, is_best_ready.count(n, 1))
                    nc.vector.tensor_tensor(order[:, :, :], is_best[:, :, :], descending[:, :].unsqueeze(1).broadcast_to(wide),
                                            ALU.mult).then_inc(order_ready.sem, 1)
                    dve.wait_ge(order_ready.sem, order_ready.count(n, 1))
                    nc.vector.tensor_reduce(first[:, :], order[:, :, :], AX.X, ALU.max).then_inc(first_ready.sem, 1)
                    dve.wait_ge(first_ready.sem, first_ready.count(n, 1))
                    nc.vector.tensor_tensor(chosen[:, :, :], order[:, :, :], first[:, :].unsqueeze(2).broadcast_to(wide),
                                            ALU.is_equal).then_inc(chosen_ready.sem, 1)

                def slots(n):
                    wide = [P, TILES, E]
                    ps = work_take(dve, n, "ranks")[:, 0:TILES * E].rearrange("p (c e) -> p c e", c=TILES)
                    dve.wait_ge(next_row_kept.sem, next_row_kept.count(n, 0))
                    nc.vector.tensor_tensor(place[:, :, :], ps, next_row[:, 0, :].unsqueeze(1).broadcast_to(wide),
                                            ALU.add).then_inc(place_ready.sem, 1)
                    ps = work_take(dve, n, "totals")[:, 0:E]
                    nc.vector.tensor_tensor(next_row[:, 1, :], ps, next_row[:, 0, :], ALU.add).then_inc(next_row_ready.sem, 1)
                    dve.wait_ge(place_ready.sem, place_ready.count(n, 1))
                    nc.vector.tensor_tensor(own_place[:, :, :], place[:, :, :], chosen[:, :, :],
                                            ALU.mult).then_inc(own_place_ready.sem, 1)
                    dve.wait_ge(own_place_ready.sem, own_place_ready.count(n, 1))
                    nc.vector.tensor_reduce(slot_f[:, :], own_place[:, :, :], AX.X, ALU.add).then_inc(slot_f_ready.sem, 1)
                    dve.wait_ge(slot_f_ready.sem, slot_f_ready.count(n, 1))
                    nc.vector.tensor_copy(slot[:, :], slot_f[:, :]).then_inc(slot_ready.sem, 1)
                    dve.wait_ge(next_row_ready.sem, next_row_ready.count(n, 1))
                    nc.vector.tensor_copy(next_row[:, 0, :], next_row[:, 1, :]).then_inc(next_row_kept.sem, 1)

                def iteration(n, work=True, route=True, last=False):
                    if route:
                        post_norm_statistics(n)
                    if work:
                        keys(n)
                    if route:
                        post_norm_apply(n)
                    if work:
                        values(n)
                    if route:
                        choose(n)
                    if work:
                        maxima(n, (0, 1))
                    if route:
                        slots(n)
                    if work:
                        maxima(n, (2, 3))
                        shift_parts(n)
                        normalise(n, 0)
                        if not last:
                            ln_statistics(n + 1)
                        normalise(n, 1)
                        if not last:
                            ln_apply(n + 1)
                        normalise(n, 2)
                        normalise(n, 3)

                def step_tables():
                    done = 1

                    def then(instruction):
                        nonlocal done
                        done += 1
                        instruction.then_inc(tables.sem, 1)
                        dve.wait_ge(tables.sem, done)

                    dve.wait_ge(next_row_kept.sem, NGROUPS + 1)
                    nc.vector.tensor_copy(filler_row[:, :], next_row[:, 0, :]).then_inc(tables.sem, 1)
                    then(nc.vector.tensor_tensor(counts[:, :], next_row[:, 0, :], region0[:, :], ALU.subtract))
                    wide = [P, E, 64]
                    then(nc.vector.tensor_tensor(tile_need[:, :, :], counts[:, :].unsqueeze(2).broadcast_to(wide),
                                                 tile_rows[:, :].unsqueeze(1).broadcast_to(wide), ALU.is_gt))
                    then(nc.vector.tensor_reduce(tiles_of[:, :], tile_need[:, :, :], AX.X, ALU.add))
                    wide = [P, E, E]
                    then(nc.vector.tensor_tensor(tiles_upto_all[:, :, :], tiles_of[:, :].unsqueeze(1).broadcast_to(wide),
                                                 upto[:, :].rearrange("p (a b) -> p a b", a=E), ALU.mult))
                    then(nc.vector.tensor_reduce(tiles_upto[:, :], tiles_upto_all[:, :, :], AX.X, ALU.add))
                    wide = [P, TABLE, E]
                    then(nc.vector.tensor_tensor(gone[:, :, :], steps[:, :].unsqueeze(2).broadcast_to(wide),
                                                 tiles_upto[:, :].unsqueeze(1).broadcast_to(wide), ALU.is_ge))
                    then(nc.vector.tensor_reduce(expert_f[:, :], gone[:, :, :], AX.X, ALU.add))
                    then(nc.vector.tensor_tensor(passed_tiles[:, :, :], gone[:, :, :],
                                                 tiles_of[:, :].unsqueeze(1).broadcast_to(wide), ALU.mult))
                    then(nc.vector.tensor_reduce(step0[:, :], passed_tiles[:, :, :], AX.X, ALU.add))
                    then(nc.vector.tensor_tensor(row_a[:, :], steps[:, :], step0[:, :], ALU.subtract))
                    then(nc.vector.tensor_scalar(row_b[:, :], row_a[:, :], float(P), None, ALU.mult))
                    then(nc.vector.scalar_tensor_tensor(row_f[:, :], expert_f[:, :], float(REGION), row_b[:, :],
                                                        ALU.mult, ALU.add))
                    then(nc.vector.tensor_copy(keep["row_table"][:, :], row_f[:, :]))
                    then(nc.vector.tensor_scalar(keep["expert_table"][:, :], expert_f[:, :], float(E - 1), None, ALU.min))

                dve.wait_ge(consts_set.sem, 9)
                dve.sem_inc(max_free.sem, 2)
                dve.sem_inc(out_free.sem, 2)
                nc.vector.tensor_copy(next_row[:, 0, :], region0[:, :]).then_inc(next_row_kept.sem, 1)
                ln_statistics(0)
                ln_apply(0)
                iteration(0, route=False)
                with dve.Fori(1, NGROUPS - 1) as n:
                    iteration(n)
                iteration(NGROUPS - 1, last=True)
                iteration(NGROUPS, work=False)
                step_tables()

            @block.scalar
            def _(act):
                def iteration(n, work=True, route=True):
                    if work:
                        for k in range(KD):
                            ps = work_take(act, n, f"xT{k}")
                            nc.scalar.activation(xT[:, k, :], ps, ACT.Copy).then_inc(xT_ready.sem, 1)
                        for tile in range(KD):
                            ps = work_take(act, n, f"q{tile}")
                            nc.scalar.activation(qT[:, tile, :], ps, ACT.Identity, scale=M_SCALE,
                                                 bias=b_qs[:, tile:tile + 1]).then_inc(q_ready.sem, 1)
                    if route:
                        for k in range(KD):
                            ps = work_take(act, n, f"yT{k}")
                            nc.scalar.activation(yT[:, k, :], ps, ACT.Copy).then_inc(yT_ready.sem, 1)
                    if work:
                        ps = work_take(act, n, "shiftT")
                        nc.scalar.activation(shiftT[:, :], ps.bitcast(BF16)[:, 0:S], ACT.Copy).then_inc(shiftT_ready.sem, 1)
                        for c in range(TILES):
                            act.wait_ge(probs_used.sem, probs_used.count(n, c - 1))
                            act.wait_ge(exp_full.sem, exp_full.count(n, c + 1))
                            nc.scalar.activation(probs[:, c % 2, :], ps_exp[:, c % 2, :], ACT.Exp).then_inc(exp_done.sem, 1)

                act.wait_ge(consts_set.sem, 9)
                act.sem_inc(exp_done.sem, 2)
                iteration(0, route=False)
                with act.Fori(1, NGROUPS) as n:
                    iteration(n)
                iteration(NGROUPS, work=False)

            @block.tensor
            def _(pe):
                def features(n):
                    for k in range(KD):
                        ps = work_claim(pe, n, f"xT{k}")
                        pe.wait_ge(ln_done.sem, ln_done.count(n, TILES))
                        for c in range(TILES):
                            mm = nc.tensor.transpose(ps[:, c * P:(c + 1) * P], xn[:, c, k * P:(k + 1) * P], identf[:, :])
                        mm.then_inc(work_full.sem, 1)

                def queries_or_keys(n, tiles):
                    pe.wait_ge(xT_ready.sem, xT_ready.count(n, KD))
                    for j in tiles:
                        ps = work_claim(pe, n, ("q0", "q1", "k0", "k1")[j])
                        for k in range(KD):
                            mm = nc.tensor.matmul(ps, w_qkv[:, k, j * P:(j + 1) * P], xT[:, k, :],
                                                  start=(k == 0), stop=(k == KD - 1))
                        mm.then_inc(work_full.sem, 1)

                def all_values(n):
                    for i in range(2):
                        ps = work_claim(pe, n, f"v{i}")
                        for c in (2 * i, 2 * i + 1):
                            for k in range(KD):
                                mm = nc.tensor.matmul(ps[:, (c % 2) * D:(c % 2 + 1) * D], xT[:, k, c * P:(c + 1) * P],
                                                      w_qkv[:, k, 2 * D:3 * D], start=(k == 0 and c % 2 == 0),
                                                      stop=(k == KD - 1), skip_group_check=True)
                        mm.then_inc(work_full.sem, 1)

                wide = mask_pos[:, :].unsqueeze(1).broadcast_to([P, MH, P])

                def add(out, lhsT, rhs):
                    return nc.tensor.matmul(out, lhsT, rhs, start=False, stop=True, skip_group_check=True)

                def scores(n, tiles):
                    pe.wait_ge(q_ready.sem, q_ready.count(n, KD))
                    pe.wait_ge(k_ready.sem, k_ready.count(n, MH))
                    for c in tiles:
                        pe.wait_ge(max_free.sem, max_free.count(n, c - 1))
                        ps = ps_max[:, c % 2, :]
                        nc.tensor.matmul(ps.rearrange("p (h k) -> p h k", h=MH), ident[:, :], wide, start=True, stop=False,
                                         skip_group_check=True)
                        for h in range(MH):
                            mm = add(ps[:, h * P:(h + 1) * P], qT[:, h // 2, c * P:(c + 1) * P], kT[:, h, c * P:(c + 1) * P])
                        mm.then_inc(max_full.sem, 1)

                def attention(n):
                    ps = work_claim(pe, n, "shiftT")
                    pe.wait_ge(shift_ready.sem, shift_ready.count(n, 1))
                    for c in range(TILES):
                        mm = nc.tensor.transpose(ps.bitcast(BF16)[:, c * P:(c + 1) * P], shift[:, c, :], ident[:, :])
                    mm.then_inc(work_full.sem, 1)
                    pe.wait_ge(v_ready.sem, v_ready.count(n, 2))

                    def shifted(c):
                        pe.wait_ge(exp_done.sem, exp_done.count(n, c - 1))
                        ps = ps_exp[:, c % 2, :]
                        nc.tensor.matmul(ps.rearrange("p (h k) -> p h k", h=MH), ident[:, :], wide, start=True, stop=False,
                                         skip_group_check=True)
                        for h in range(MH):
                            add(ps[:, h * P:(h + 1) * P], kT[:, h, c * P:(c + 1) * P], qT[:, h // 2, c * P:(c + 1) * P])
                        if c == 0:
                            pe.wait_ge(shiftT_ready.sem, shiftT_ready.count(n, 1))
                        for h in range(MH):
                            mm = add(ps[:, h * P:(h + 1) * P], sel_head[:, h, :], shiftT[:, c * P:(c + 1) * P])
                        mm.then_inc(exp_full.sem, 1)

                    def values(c):
                        pe.wait_ge(out_free.sem, out_free.count(n, c - 1))
                        pe.wait_ge(exp_done.sem, exp_done.count(n, c + 1))
                        for side in range(2):
                            for h in range(MH):
                                lo, col = MD * (h % 2), D * side + P * (h // 2)
                                mm = nc.tensor.matmul(ps_out[lo:lo + MD, c % 2, col:col + P],
                                                      v[:, c, MD * h:MD * h + MD] if side == 0 else ones64[:, :],
                                                      probs[:, c % 2, h * P:(h + 1) * P],
                                                      start=(side == 0 and h < 2), stop=True, skip_group_check=True)
                        mm.then_inc(probs_used.sem, 1)

                    shifted(0)
                    for c in range(1, TILES):
                        shifted(c)
                        values(c - 1)
                    values(TILES - 1)

                def output(n):
                    for i in range(2):
                        ps = work_claim(pe, n, f"out{i}")
                        pe.wait_ge(out_free.sem, out_free.count(n, 2 * i + 2 - TILES))
                        for c in (2 * i, 2 * i + 1):
                            for tile in range(KD):
                                mm = nc.tensor.matmul(ps[:, (c % 2) * D:(c % 2 + 1) * D], oT[:, tile, c * P:(c + 1) * P],
                                                      w_o[:, tile, :], start=(tile == 0 and c % 2 == 0),
                                                      stop=(tile == KD - 1), skip_group_check=True)
                        mm.then_inc(work_full.sem, 1)

                def logits(n):
                    for k in range(KD):
                        ps = work_claim(pe, n, f"yT{k}")
                        pe.wait_ge(y_ready.sem, y_ready.count(n, TILES))
                        for c in range(TILES):
                            mm = nc.tensor.transpose(ps[:, c * P:(c + 1) * P], rows[:, c, k * P:(k + 1) * P], identf[:, :])
                        mm.then_inc(work_full.sem, 1)
                    ps = work_claim(pe, n, "logits")
                    pe.wait_ge(yT_ready.sem, yT_ready.count(n, KD))
                    for c in range(TILES):
                        for k in range(KD):
                            mm = nc.tensor.matmul(ps[:, c * E:(c + 1) * E], yT[:, k, c * P:(c + 1) * P], w_g[:, k, :],
                                                  start=(c == 0 and k == 0), stop=(k == KD - 1), skip_group_check=True)
                    mm.then_inc(work_full.sem, 1)

                def ranks(n):
                    ps = work_claim(pe, n, "ranks")
                    pe.wait_ge(chosen_ready.sem, chosen_ready.count(n, 1))
                    nc.tensor.matmul(ps[:, 0:TILES * E], before[:, :], chosen[:, :, :].rearrange("p c e -> p (c e)"),
                                     start=True, stop=False, skip_group_check=True)
                    for c in range(TILES - 1):
                        later = TILES - 1 - c
                        mm = nc.tensor.matmul(ps[:, (c + 1) * E:TILES * E].rearrange("p (c e) -> p c e", e=E), ones16[:, :],
                                              chosen[:, c, :].unsqueeze(1).broadcast_to([P, later, E]), start=False,
                                              stop=True, skip_group_check=True)
                    mm.then_inc(work_full.sem, 1)
                    ps = work_claim(pe, n, "totals")
                    for c in range(TILES):
                        mm = nc.tensor.matmul(ps[:, 0:E], ones16[:, :], chosen[:, c, :], start=(c == 0), stop=(c == TILES - 1))
                    mm.then_inc(work_full.sem, 1)

                def iteration(n, work=True, route=True):
                    if work:
                        features(n)
                        queries_or_keys(n, (0, 1))
                    if route:
                        output(n)
                    if work:
                        queries_or_keys(n, (2, 3))
                        all_values(n)
                    if route:
                        logits(n)
                    if work:
                        scores(n, (0, 1))
                    if route:
                        ranks(n)
                    if work:
                        scores(n, (2, 3))
                        attention(n)

                pe.wait_ge(consts_set.sem, 9)
                pe.sem_inc(probs_used.sem, 2)
                pe.sem_inc(next_row_ready.sem, 1)
                iteration(0, route=False)
                with pe.Fori(1, NGROUPS) as n:
                    iteration(n)
                iteration(NGROUPS, work=False)


UNROLL = 4
ROUNDS = STEPS // UNROLL


def expert_program(nc, t, mem, identf, keep):
    ctx = ExitStack()
    with ctx:
        def sb(name, shape, dt=F32):
            return ctx.enter_context(nc.sbuf_tensor(name, shape, dt))

        def signal(name, per, ahead=0):
            return Signal(ctx, nc, name, per, ahead)

        b2 = sb("e_b2", [P, E * D])
        g2 = sb("e_g2", [P, D])
        be2 = sb("e_be2", [P, D])
        half = sb("e_half", [P, 1])
        eps = sb("e_eps", [P, 1])
        row = sb("e_row", [P, UNROLL, ROW])
        token = sb("e_token", [P, UNROLL, 1], U32)
        yT = sb("e_yT", [P, 2, KD * P])
        w1_now = sb("e_w1_now", [P, 2, KD, DF])
        hT = sb("e_hT", [P, 2, KF, P])
        yb = sb("e_yb", [P, 2, D])
        xb = sb("e_xb", [P, 2, D])
        summed = sb("e_summed", [P, 2, D])
        stats = sb("e_stats", [P, 2, 6])
        moments = sb("e_moments", [P, 2, 2])
        veps = sb("e_veps", [P, 2])
        rstd = sb("e_rstd", [P, 2])
        scaled = sb("e_scaled", [P, 2, D])
        result = sb("e_result", [P, 2, D])
        ps_h = [mem["ps_a"], mem["ps_b"]]
        ps_out, ps_yT = mem["ps_c"], mem["ps_d"]
        w1, w2, b1 = keep["w1"], keep["w2"], keep["b1"]

        consts_loaded = signal("e_consts_loaded", 0)
        consts_set = signal("e_consts_set", 0)
        row_loaded = [signal(f"e_row_loaded{u}", 16) for u in range(UNROLL)]
        yT_full = signal("e_yT_full", 1)
        yT_ready = signal("e_yT_ready", 1)
        w1_ready = signal("e_w1_ready", KD)
        h_full = signal("e_h_full", KF // 4)
        hT_ready = signal("e_hT_ready", KF)
        out_full = signal("e_out_full", 1)
        yb_ready = signal("e_yb_ready", 1)
        xb_ready = signal("e_xb_ready", 1)
        token_ready = signal("e_token_ready", 1)
        sum_ready = signal("e_sum_ready", 1)
        stats_ready = signal("e_stats_ready", 1)
        moments_ready = signal("e_moments_ready", 1)
        veps_ready = signal("e_veps_ready", 1)
        rstd_ready = signal("e_rstd_ready", 1)
        scaled_ready = signal("e_scaled_ready", 1)
        result_ready = signal("e_result_ready", 1)
        stored = [signal(f"e_stored{u}", 16) for u in range(2)]
        passed = signal("e_waits_passed_vector", 0)
        pool_passed = signal("e_waits_passed_pool", 0)

        def expert_of(eng, j):
            return eng.value_load(keep["expert_table"][0:1, bass.ds(j, 1)], min_val=0, max_val=E - 1)

        def rounds(eng, step):
            for u in range(UNROLL):
                step(0, u)
            with eng.Fori(1, ROUNDS - 1) as i:
                for u in range(UNROLL):
                    step(i, u)
            for u in range(UNROLL):
                step(ROUNDS - 1, u)

        def is_step(i, u):
            return not (isinstance(i, int) and i * UNROLL + u >= STEPS)

        def await_row(eng, i, u):
            sig = row_loaded[u % UNROLL]
            eng.wait_ge(sig.sem, sig.count(i + u // UNROLL, 16))

        with nc.Block() as block:

            @block.sync
            def _(sp):
                def load(i, u):
                    j = i * UNROLL + u
                    if not isinstance(i, int):
                        sp.wait_ge(xb_ready.sem, xb_ready.count(j - UNROLL, 1))
                        sp.wait_ge(token_ready.sem, token_ready.count(j - UNROLL, 1))
                        sp.wait_ge(yT_full.sem, yT_full.count(j - UNROLL, 1))
                    row0 = sp.value_load(keep["row_table"][0:1, bass.ds(j, 1)], min_val=0,
                                         max_val=E * REGION + (SPARE_TILES - 1) * P)
                    sp.dma_start(row[:, u, :], t["sorted"][bass.ds(row0, P), :]).then_inc(row_loaded[u].sem, 16)

                for u in range(UNROLL):
                    load(0, u)
                for dst, src in ((b2, "e_b2"), (g2, "e_g2"), (be2, "e_be2")):
                    sp.dma_start(dst[:, :], t[src].partition_broadcast(P)).then_inc(consts_loaded.sem, 16)
                with sp.Fori(1, ROUNDS) as i:
                    for u in range(UNROLL):
                        load(i, u)

            @block.gpsimd
            def _(pool):
                nc.gpsimd.memset(half[:, :], -0.5).then_inc(consts_set.sem, 1)
                nc.gpsimd.memset(eps[:, :], EPS).then_inc(consts_set.sem, 1)
                pool.wait_ge(consts_set.sem, 2)
                pool.wait_ge(consts_loaded.sem, 48)

                def residuals(i, u):
                    j = i * UNROLL + u
                    e = expert_of(pool, j)
                    await_row(pool, i, u)
                    nc.gpsimd.tensor_tensor(yb[:, u % 2, :], row[:, u % UNROLL, 0:D], b2[:, bass.ds(e * D, D)],
                                            ALU.add).then_inc(yb_ready.sem, 1)
                    nc.gpsimd.tensor_tensor(xb[:, u % 2, :], row[:, u % UNROLL, D:2 * D], be2[:, :],
                                            ALU.add).then_inc(xb_ready.sem, 1)

                def step(i, u):
                    j, s = i * UNROLL + u, u % 2
                    if is_step(i, u + 1):
                        residuals(i, u + 1)
                    pool.wait_ge(moments_ready.sem, moments_ready.count(j, 1))
                    nc.gpsimd.tensor_tensor(veps[:, s:s + 1], moments[:, s, 1:2], eps[:, :], ALU.add).then_inc(veps_ready.sem, 1)
                    pool.wait_ge(veps_ready.sem, veps_ready.count(j, 1))
                    nc.gpsimd.tensor_tensor(rstd[:, s:s + 1], veps[:, s:s + 1], half[:, :], ALU.pow).then_inc(rstd_ready.sem, 1)
                    wait_apart(pool, pool_passed, result_ready.sem, result_ready.count(j, 1))
                    nc.gpsimd.indirect_dma_start(
                        out=t["out"], out_offset=bass.IndirectOffsetOnAxis(ap=token[:, u, :], axis=0),
                        in_=result[:, s, :], in_offset=None, bounds_check=B * S - 1, oob_is_err=False
                        ).then_inc(stored[s].sem, 16)

                residuals(0, 0)
                rounds(pool, step)
                for s in range(2):
                    pool.wait_ge(stored[s].sem, 16 * (STEPS // 2))

            @block.vector
            def _(dve):
                def hidden(i, u):
                    j, s = i * UNROLL + u, u % 2
                    e = expert_of(dve, j)
                    await_row(dve, i, u)
                    nc.vector.tensor_copy(token[:, u % UNROLL, :], row[:, u % UNROLL, 2 * D:2 * D + 1]).then_inc(token_ready.sem, 1)
                    for f in range(KF):
                        if f % 4 == 0:
                            dve.wait_ge(h_full.sem, h_full.count(j, f // 4 + 1))
                        nc.vector.tensor_scalar(hT[:, s, f, :], ps_h[s][:, f // 4, (f % 4) * P:(f % 4 + 1) * P],
                                                b1[:, bass.ds(e * KF + f, 1)], 0.0, ALU.add, ALU.max
                                                ).then_inc(hT_ready.sem, 1)

                def step(i, u):
                    j, s = i * UNROLL + u, u % 2
                    if is_step(i, u + 1):
                        hidden(i, u + 1)
                    dve.wait_ge(out_full.sem, out_full.count(j, 1))
                    dve.wait_ge(yb_ready.sem, yb_ready.count(j, 1))
                    nc.vector.tensor_tensor(summed[:, s, :], ps_out[:, s, 0:D], yb[:, s, :], ALU.add).then_inc(sum_ready.sem, 1)
                    dve.wait_ge(sum_ready.sem, sum_ready.count(j, 1))
                    nc.vector.bn_stats(stats[:, s, :], summed[:, s, :]).then_inc(stats_ready.sem, 1)
                    wait_apart(dve, passed, stats_ready.sem, stats_ready.count(j, 1))
                    nc.vector.bn_aggr(moments[:, s, :], stats[:, s, :]).then_inc(moments_ready.sem, 1)
                    dve.wait_ge(moments_ready.sem, moments_ready.count(j, 1))
                    nc.vector.scalar_tensor_tensor(scaled[:, s, :], summed[:, s, :], moments[:, s, 0:1], g2[:, :],
                                                   ALU.subtract, ALU.mult).then_inc(scaled_ready.sem, 1)
                    dve.wait_ge(scaled_ready.sem, scaled_ready.count(j, 1))
                    dve.wait_ge(rstd_ready.sem, rstd_ready.count(j, 1))
                    dve.wait_ge(xb_ready.sem, xb_ready.count(j, 1))
                    if not (isinstance(i, int) and i == 0 and u < 2):
                        stores = stored[s].count(i * 2 + u // 2, 0)
                        dve.wait_ge(stored[s].sem, stores)
                    nc.vector.scalar_tensor_tensor(result[:, s, :], scaled[:, s, :], rstd[:, s:s + 1], xb[:, s, :],
                                                   ALU.mult, ALU.add).then_inc(result_ready.sem, 1)

                dve.wait_ge(consts_loaded.sem, 48)
                hidden(0, 0)
                rounds(dve, step)

            @block.scalar
            def _(act):
                def weights(j, s):
                    e = expert_of(act, j)
                    for k in range(KD):
                        nc.scalar.activation(w1_now[:, s, k, :], w1[:, k, bass.ds(e * DF, DF)], ACT.Copy).then_inc(w1_ready.sem, 1)

                def features(j, s):
                    act.wait_ge(yT_full.sem, yT_full.count(j, 1))
                    nc.scalar.activation(yT[:, s, :], ps_yT[:, s, 0:KD * P], ACT.Copy).then_inc(yT_ready.sem, 1)

                def step(i, u):
                    if is_step(i, u + 2):
                        features(i * UNROLL + (u + 2), u % 2)
                        weights(i * UNROLL + (u + 2), u % 2)

                for j in range(2):
                    weights(j, j)
                    features(j, j)
                rounds(act, step)

            @block.tensor
            def _(pe):
                def features(i, u):
                    await_row(pe, i, u)
                    for k in range(KD):
                        mm = nc.tensor.transpose(ps_yT[:, u % 2, k * P:(k + 1) * P], row[:, u % UNROLL, k * P:(k + 1) * P],
                                                 identf[:, :])
                    mm.then_inc(yT_full.sem, 1)

                def hidden(i, u):
                    j, s = i * UNROLL + u, u % 2
                    pe.wait_ge(yT_ready.sem, yT_ready.count(j, 1))
                    pe.wait_ge(w1_ready.sem, w1_ready.count(j, KD))
                    for f in range(KF):
                        for k in range(KD):
                            mm = nc.tensor.matmul(ps_h[s][:, f // 4, (f % 4) * P:(f % 4 + 1) * P],
                                                  w1_now[:, s, k, f * P:(f + 1) * P], yT[:, s, k * P:(k + 1) * P],
                                                  start=(f % 4 == 0 and k == 0), stop=(k == KD - 1), skip_group_check=True)
                        if f % 4 == 3:
                            mm.then_inc(h_full.sem, 1)

                def output(i, u):
                    j, s = i * UNROLL + u, u % 2
                    e = expert_of(pe, j)
                    pe.wait_ge(hT_ready.sem, hT_ready.count(j, KF))
                    for f in range(KF):
                        mm = nc.tensor.matmul(ps_out[:, s, 0:D], hT[:, s, f, :], w2[:, bass.ds(e * KF * D + f * D, D)],
                                              start=(f == 0), stop=(f == KF - 1))
                    mm.then_inc(out_full.sem, 1)

                def step(i, u):
                    if is_step(i, u + 2):
                        features(i, u + 2)
                    if is_step(i, u + 1):
                        hidden(i, u + 1)
                    output(i, u)

                features(0, 0)
                features(0, 1)
                hidden(0, 0)
                rounds(pe, step)


def decoder_block(nc, t):
    t["x2"] = nc.dram_tensor("x2_rows", [B, S, D], F32, kind="Internal").ap()
    t["x2_groups"] = t["x2"].rearrange("s (g p) d -> g s p d", g=NGROUPS)
    t["qk_parts"] = nc.dram_tensor("qk_parts", [2, 3, D, S], BF16, kind="Internal").ap()
    t["sorted"] = nc.dram_tensor("sorted_rows", [E * REGION + SPARE_TILES * P, ROW], F32, kind="Internal").ap()
    with ExitStack() as ctx:
        mem = {name: ctx.enter_context(nc.psum_tensor(name, [P, 2, 512], F32)) for name in ("ps_a", "ps_b", "ps_c", "ps_d")}
        consts, loads = mixing_constants(ctx, nc, t)
        attention_program(nc, t, mem, loads)
        shapes = {"w1": [P, KD, E * DF], "w2": [P, E * KF * D], "b1": [P, E * KF]}
        keep = {name: ctx.enter_context(nc.sbuf_tensor("keep_" + name, shape, F32)) for name, shape in shapes.items()}
        for name in ("row_table", "expert_table"):
            keep[name] = ctx.enter_context(nc.sbuf_tensor("keep_" + name, [P, TABLE], I32))
        mixing_program(nc, t, mem, consts, keep)
        expert_program(nc, t, mem, consts["identf"], keep)


def constants():
    import numpy as np
    i = np.arange(P)
    eye = np.eye(P, dtype=np.float32)
    own = np.where(i[None, :] <= i[:, None], 0, NEG)
    previous = np.where(i[None, :] > i[:, None], 0, NEG)
    first = np.where(i[None, :] < PREFIX, 0, previous)
    sel = np.zeros((P, HEADS, P))
    for h in range(HEADS):
        sel[[h, HEADS + h], h] = 1
    sel_prefix = np.zeros((P, GROUPS, P))
    for g in range(GROUPS):
        for j, h in enumerate(group_heads(g)):
            sel_prefix[[h, HEADS + h], g, 32 * j:32 * j + 32] = 1
            sel_prefix[2 * HEADS, g, 32 * j + PREFIX:32 * j + 32] = NEG
    sel_pair = np.zeros((P, PAIRS, P))
    for h in range(HEADS):
        sel_pair[[h, HEADS + h], h // 2, CTX * (h % 2):CTX * (h % 2 + 1)] = 1
    half_cols = np.zeros((P, 2, 32))
    half_cols[:, 0, :HD] = half_cols[:, 1, HD:] = 1
    col = np.arange(D)
    odd = (col % 32) // HD
    prefix_rows = np.stack([(i[:, None] // 32 == (col // 32) % 4) & (odd == o) for o in range(2)], 1)
    sel_head = np.zeros((P, MH, P))
    for h in range(MH):
        sel_head[[h, MH + h], h] = 1
    e = np.arange(E)
    fp32 = {
        "c_identity": eye, "c_half_cols": half_cols, "c_prefix_rows": prefix_rows,
        "c_ctx_rows": i[:, None] // CTX == odd, "c_head_rows": i[:, None] // HD == np.arange(8),
        "c_head_half": i[:, None] // MD == np.arange(2),
        "c_descending": np.broadcast_to(E - e, (P, E)), "c_region0": np.broadcast_to(e * REGION, (P, E)),
        "c_token0": (i // POS * S + i % POS)[:, None] + POS * np.arange(TILES),
        "c_tile_rows": np.broadcast_to(P * np.arange(64), (P, 64)),
        "c_upto": np.broadcast_to((e[None, :] <= e[:, None]).reshape(-1), (P, E * E)),
        "c_steps": np.broadcast_to(np.arange(TABLE), (P, TABLE)),
    }
    bf16 = {
        "c_identity16": eye, "c_mask_qk": np.stack([np.concatenate([p, own], 1) for p in (first, previous)], 1),
        "c_mask_kq": np.concatenate([own.T, first.T, own.T, previous.T, own.T], 1),
        "c_sel": sel, "c_sel_prefix": sel_prefix, "c_sel_pair": sel_pair, "c_sel_head": sel_head,
        "c_mask_pos": np.where(i[:, None] % POS == i % POS, 0, NEG), "c_before": i[:, None] < i,
    }
    out = {k: np.ascontiguousarray(v, np.float32) for k, v in fp32.items()}
    out.update({k: np.ascontiguousarray(np.asarray(v, np.float32)).astype(mybir.dt.np(BF16)) for k, v in bf16.items()})
    return out


def kernel(**inputs):
    import numpy as np
    import concourse.bacc as bacc
    from concourse.bass_utils import run_bass_kernel_spmd

    def array(name):
        return np.asarray(inputs[name])

    def columns(a):
        return a.reshape(-1, P).T

    laid = {"x": array("x"), "ctx": array("ctx_1024"), "mask": array("mask_BxSxS2_if1"),
            "w_qkvT": array("L0_attn_w_qkv").T, "w_outT": array("L0_attn_w_out").T,
            "b_q2": columns(array("L0_xattn_bq")), "b_k2": columns(array("L0_xattn_bk")),
            "b_v2": array("L0_xattn_bv"), "b_o2": array("L0_xattn_bo"),
            "m_w_qkvT": array("L0_ffn_Wqkv").T, "m_w_oT": array("L0_ffn_Wo").T, "m_w_gT": array("L0_ffn_Wg").T,
            "m_b_q": columns(array("L0_ffn_bqkv")[0:D]), "m_b_k": columns(array("L0_ffn_bqkv")[D:2 * D]),
            "m_b_v": array("L0_ffn_bqkv")[2 * D:], "m_b_o": array("L0_ffn_bo"),
            "m_g1": array("L0_ffn_g1"), "m_be1": array("L0_ffn_be1"),
            "e_w1": array("L0_ffn_W1"), "e_w2": array("L0_ffn_W2"), "e_b1": columns(array("L0_ffn_b1")),
            "e_b2": array("L0_ffn_b2").reshape(-1), "e_g2": array("L0_ffn_g2"), "e_be2": array("L0_ffn_be2")}
    for a in "qkvo":
        laid[f"w_{a}2T"] = array(f"L0_xattn_W{a}").T
    laid.update(constants())

    nc = bacc.Bacc("TRN2", target_bir_lowering=False, num_devices=1)
    arrays, t = {}, {}
    for name, a in laid.items():
        a = np.ascontiguousarray(a)
        arrays["in_" + name] = a
        t[name] = nc.dram_tensor("in_" + name, a.shape, mybir.dt.from_np(a.dtype), kind="ExternalInput").ap()
    out = nc.dram_tensor("out", [B * S, D], F32, kind="ExternalOutput").ap()
    t["out"] = out
    decoder_block(nc, t)
    r = run_bass_kernel_spmd(nc, [arrays], core_ids=[0])
    return r.results[0]["out"].reshape(B, S, D)
```

```python
from contextlib import ExitStack
from itertools import islice

import concourse.bass as bass
from concourse import mybir

F32 = mybir.dt.float32
BF16 = mybir.dt.bfloat16
I32 = mybir.dt.int32
U32 = mybir.dt.uint32
ALU = mybir.AluOpType
ACT = mybir.ActivationFunctionType
AX = mybir.AxisListType

P = 128
B, S, D = 8, 512, 256
KD = D // P
TILES = S // P
HEADS, HD = 16, 16
WINDOW, PREFIX = 128, 16
CTX = 64
PAIRS = HEADS // 2
PARTS = 6
SPLIT_ROWS = PARTS * HD
SHIFT_ROWS = SPLIT_ROWS + 2
STACKS = ((0, 0, 3), (3, 1, 2), (5, 2, 1))
EPS = 1e-5
QK_SCALE = HD ** -0.5
GROUP = 4
GROUPS = HEADS // GROUP
HEAD_COLS = 3 * 256 + 128
GROUP_COLS = GROUP * HEAD_COLS + 256
NEG = -(2.0 ** 30)
NEG_MASK = -(2.0 ** 100)


class Signal:

    def __init__(self, ctx, nc, name, per, ahead=0):
        self.sem = ctx.enter_context(nc.semaphore(name))
        self.per, self.ahead = per, ahead

    def count(self, n, k):
        return n * self.per + (k + self.ahead)

    def next(self, n, k):
        return self.count(n, self.per + k)


def group_heads(g):
    return range(GROUP * g, GROUP * g + GROUP)


def wait_apart(eng, passed, sem, value):
    eng.wait_ge(sem, value)
    eng.sem_inc(passed.sem, 1)


def layernorm_statistics(nc, dve, x, stats, moments, passed, sig_stats, sig_moments, n):
    for c in range(TILES):
        nc.vector.bn_stats(stats[:, c, :], x[:, c, :]).then_inc(sig_stats.sem, 1)
    wait_apart(dve, passed, sig_stats.sem, sig_stats.count(n, TILES))
    for c in range(TILES):
        nc.vector.bn_aggr(moments[:, c, :], stats[:, c, :]).then_inc(sig_moments.sem, 1)


def layernorm_rstd(nc, pool, moments, veps, eps, half, rstd, sig_moments, sig_veps, sig_rstd, n):
    pool.wait_ge(sig_moments.sem, sig_moments.count(n, TILES))
    nc.gpsimd.tensor_tensor(veps[:, :], moments[:, :, 1], eps, ALU.add).then_inc(sig_veps.sem, 1)
    pool.wait_ge(sig_veps.sem, sig_veps.count(n, 1))
    nc.gpsimd.tensor_tensor(rstd[:, :], veps[:, :], half, ALU.pow).then_inc(sig_rstd.sem, 1)


def layernorm_apply(nc, dve, x, out, moments, rstd, sig_rstd, sig_done, n):
    dve.wait_ge(sig_rstd.sem, sig_rstd.count(n, 1))
    for c in range(TILES):
        nc.vector.tensor_scalar(out[:, c, :], x[:, c, :], moments[:, c, 0:1], rstd[:, c:c + 1],
                                ALU.subtract, ALU.mult).then_inc(sig_done.sem, 1)


CROSS_FILLS = ["s3", "oT0", "oT1", "out0", "out1", "xT2_0", "xT2_1", "q2_0", "q2_1", "shiftT2", "out2_0", "out2_1"]
FRONT_FILLS = ["xT0", "xT1", "q0", "k0", "q1", "k1"]
FILLS = ["s3", "oT0", "oT1", "out0", "out1", "v0", "v1", "xT2_0", "xT2_1", "q2_0", "q2_1", "vg", "shiftT", "ctxT",
         "k2", "shiftT2", "xT0", "xT1", "q0", "k0", "q1", "s0", "k1", "v2", "out2_0", "out2_1", "s1", "s2"]
FIRST_FILLS = [f for f in FILLS if f not in CROSS_FILLS]
LAST_FILLS = [f for f in FILLS if f not in FRONT_FILLS]
CROSS_MAX, WINDOW_MAX = 2 * TILES, 30
EARLY_MAX = 4
EARLY_BEFORE_S2 = min(EARLY_MAX, 1)
SCORE_MAX = CROSS_MAX + WINDOW_MAX
BEFORE_S3, BEFORE_HEADS, BEFORE_OUT0, BEFORE_OUT1, BEFORE_V0, BEFORE_V1, BEFORE_Q0, BEFORE_Q1, BEFORE_VG = 6, 8, 10, 12, 14, 16, 18, 20, 22
CROSS_EXP, WINDOW_EXP = PAIRS, 9 * GROUPS
CROSS_SUMS, WINDOW_SUMS = KD, GROUPS
WINDOW_ORDER = [(c, j) for half in range(2) for c in range(TILES) for j in range(8) if j // (2 if c == 0 else 4) == half]
HALF_FILLS = len(WINDOW_ORDER) // 2
WINDOW_ORDER[-2:-2] = [(2, 8), (3, 8)]
PROJECTIONS = ("q0", "k0", "q1", "k1")


def attention_program(nc, t, mem, later_loads):
    ctx = ExitStack()
    with ctx:
        def sb(name, shape, dt=F32):
            return ctx.enter_context(nc.sbuf_tensor(name, shape, dt))

        def signal(name, per, ahead=0):
            return Signal(ctx, nc, name, per, ahead)

        def cross_signal(name, per, ahead=0):
            return Signal(ctx, nc, name, per, ahead - per)

        identf = sb("identf", [P, P])
        ident = sb("ident", [P, P], BF16)
        mask_qk = sb("mask_qk", [P, 2, 256], BF16)
        mask_kq = sb("mask_kq", [P, 640], BF16)
        mask_prefix = sb("mask_prefix", [P, 256], BF16)
        prefix_rows = sb("prefix_rows", [P, HEADS])
        ctx_rows = sb("ctx_rows", [P, D])
        w_qkv = sb("w_qkv", [P, KD, 3 * D])
        w_out = sb("w_out", [P, KD, D])
        w_q2 = sb("w_q2", [P, KD, D])
        w_k2 = sb("w_k2", [P, KD, D])
        w_v2 = sb("w_v2", [P, KD, D])
        w_o2 = sb("w_o2", [P, KD, D])
        b_q2 = sb("b_q2", [P, KD])
        b_q2s = sb("b_q2s", [P, KD])
        b_k2 = sb("b_k2", [P, KD])
        b_v2 = sb("b_v2", [P, D])
        b_o2 = sb("b_o2", [P, D])
        half = sb("half", [P, TILES])
        eps = sb("eps", [P, TILES])
        x_in = sb("x_in", [P, TILES, D])
        x_res = sb("x_res", [P, TILES, D])
        stats = sb("stats", [P, TILES, 6])
        moments = sb("moments", [P, TILES, 2])
        veps = sb("veps", [P, TILES])
        rstd = sb("rstd", [P, TILES])
        stats2 = sb("stats2", [P, TILES, 6])
        moments2 = sb("moments2", [P, TILES, 2])
        veps2 = sb("veps2", [P, TILES])
        rstd2 = sb("rstd2", [P, TILES])
        xn = sb("xn", [P, TILES, D])
        xT = sb("xT", [P, KD, S])
        parts = sb("parts", [P, 3, 4, S], BF16)
        rest = sb("rest", [P, 4, S])
        q_rows = sb("q_rows", [SHIFT_ROWS, HEADS, S], BF16)
        k_rows = sb("k_rows", [SHIFT_ROWS, HEADS, S], BF16)
        v_ones = sb("v_ones", [P, TILES, HEADS, 32])
        v_prefix = sb("v_prefix", [P, HEADS, 32])
        top = sb("top", [P, TILES, HEADS])
        top_prefix = sb("top_prefix", [P, 2, HEADS])
        top2 = sb("top2", [P, TILES, HEADS])
        shift = sb("shift", [P, TILES, P], BF16)
        shiftT = sb("shiftT", [P, S], BF16)
        shift2, shiftT2 = shift, shiftT
        probs = sb("probs", [P, 2, GROUP_COLS])
        rden = sb("rden", [P, S])
        sums = sb("sums", [P, 2, S])
        rsum = sb("rsum", [P, 2, TILES, GROUP, 1])
        heads_out = sb("heads_out", [P, TILES, D])
        xn2 = heads_out
        oT = sb("oT", [P, KD, S])
        oT2 = sb("oT2", [P, KD, S])
        xT2 = oT2
        x1 = sb("x1", [P, TILES, D])
        ctx_in = sb("ctx_in", [2 * CTX, D])
        mask_in = sb("mask_in", [P, TILES, CTX], I32)
        mask_add = sb("mask_add", [P, TILES, 2, CTX], BF16)
        ctxT = sb("ctxT", [P, KD, 2, CTX])
        k2_parts = sb("k2_parts", [P, 3, KD, CTX], BF16)
        k2_rest = sb("k2_rest", [P, KD, CTX])
        k2_rows = sb("k2_rows", [SHIFT_ROWS, HEADS, CTX], BF16)
        v2 = sb("v2", [P, D])
        v2pair = sb("v2pair", [P, D])
        q2_parts = sb("q2_parts", [P, 3, KD, S], BF16)
        q2_rest = sb("q2_rest", [P, KD, S])
        q2_rows = sb("q2_rows", [SHIFT_ROWS, HEADS, S], BF16)
        ps_max = mem["ps_a"]
        ps_exp = mem["ps_b"]
        ps_out = mem["ps_c"]
        ps_work = mem["ps_d"]

        first_loaded = signal("first_loaded", 0)
        consts_loaded = signal("consts_loaded", 0)
        consts_set = signal("consts_set", 0)
        later_loaded = signal("later_loaded", 0)
        x_loaded = signal("x_loaded", 16)
        xres_loaded = signal("xres_loaded", 16)
        ctx_loaded = signal("ctx_loaded", 32)
        mask_loaded = signal("mask_loaded", 16)
        ln_stats = signal("ln_stats", TILES)
        ln_moments = signal("ln_moments", TILES)
        ln_veps = signal("ln_veps", 1)
        ln_rstd = signal("ln_rstd", 1)
        ln_done = signal("ln_done", TILES)
        ln2_stats = cross_signal("ln2_stats", TILES)
        ln2_moments = cross_signal("ln2_moments", TILES)
        ln2_veps = cross_signal("ln2_veps", 1)
        ln2_rstd = cross_signal("ln2_rstd", 1)
        ln2_done = cross_signal("ln2_done", TILES)
        work_full = signal("work_full", len(FILLS), len(FRONT_FILLS) - len(CROSS_FILLS))
        xT_ready = signal("xT_ready", KD)
        xT2_ready = cross_signal("xT2_ready", KD)
        part_hi = signal("part_hi", 4)
        part_rest = signal("part_rest", 4)
        part_mid = signal("part_mid", 4)
        part_lo = signal("part_lo", 4)
        qk_stored = [signal(f"qk_stored_{tile}", 16 * 6) for tile in range(KD)]
        rows_loaded = [signal(f"rows_loaded_{tile}", 16 * 2 * len(STACKS)) for tile in range(KD)]
        v_ready = signal("v_ready", 2)
        vprefix_ready = signal("vprefix_ready", 1)
        max_full = signal("max_full", SCORE_MAX, EARLY_MAX - CROSS_MAX)
        max_free = signal("max_free", SCORE_MAX, 2 + EARLY_MAX - CROSS_MAX)
        top_joined = signal("top_joined", 1)
        shift_hi = signal("shift_hi", 1)
        shift_ready = signal("shift_ready", 1)
        shiftT_ready = signal("shiftT_ready", 1)
        shift_stacked = signal("shift_stacked", 32)
        shift2_hi = cross_signal("shift2_hi", 1)
        shift2_ready = cross_signal("shift2_ready", 1)
        shiftT2_ready = cross_signal("shiftT2_ready", 1)
        exp_full = signal("exp_full", CROSS_EXP + WINDOW_EXP, -CROSS_EXP)
        exp_done = signal("exp_done", CROSS_EXP + WINDOW_EXP, 2 - CROSS_EXP)
        probs_used = signal("probs_used", CROSS_SUMS + WINDOW_SUMS, 2 - CROSS_SUMS)
        sums_ready = signal("sums_ready", GROUPS)
        sums_recip = signal("sums_recip", GROUPS)
        heads_ready = signal("heads_ready", GROUPS)
        oT_ready = cross_signal("oT_ready", KD)
        out2_recip = cross_signal("out2_recip", KD)
        oT2_ready = cross_signal("oT2_ready", KD)
        ctxT_ready = signal("ctxT_ready", 1)
        k2_hi = signal("k2_hi", KD)
        k2_left = signal("k2_left", KD)
        k2_mid = signal("k2_mid", 1)
        k2_lo = signal("k2_lo", 1)
        k2_stored = signal("k2_stored", 16 * 3 * KD)
        k2_loaded = signal("k2_loaded", 16 * len(STACKS))
        v2_biased = signal("v2_biased", 1)
        v2_ready = signal("v2_ready", 1)
        mask_ready = cross_signal("mask_ready", 1)
        q2_hi = cross_signal("q2_hi", KD)
        q2_left = cross_signal("q2_left", KD)
        q2_mid = cross_signal("q2_mid", KD)
        q2_lo = cross_signal("q2_lo", KD)
        q2_stored = [cross_signal(f"q2_stored_{tile}", 16 * 3) for tile in range(KD)]
        q2_loaded = [cross_signal(f"q2_loaded_{tile}", 16 * len(STACKS)) for tile in range(KD)]
        shift2_stacked = cross_signal("shift2_stacked", 32)
        x1_ready = cross_signal("x1_ready", 2)
        x1b_ready = cross_signal("x1b_ready", 1)
        x2_ready = cross_signal("x2_ready", 2)
        x2_stored = cross_signal("x2_stored", 16, 16)
        passed = signal("waits_passed_vector", 0)
        pool_passed = signal("waits_passed_pool", 0)
        sp_passed = signal("waits_passed_sync", 0)

        def released(n, name):
            by_name = {"vg": (vprefix_ready, 1), "shiftT": (shiftT_ready, 1), "shiftT2": (shiftT2_ready, 1),
                       "ctxT": (ctxT_ready, 1), "k2": (k2_left, 2), "v2": (v2_biased, 1),
                       "s0": (heads_ready, 1), "s1": (heads_ready, 2), "s2": (heads_ready, 3),
                       "s3": (heads_ready, 0)}
            for k in range(KD):
                by_name.update({f"xT{k}": (xT_ready, KD + k + 1),
                                f"q{k}": (part_rest, 4 + 2 * k + 1), f"k{k}": (part_rest, 4 + 2 * k + 2),
                                f"v{k}": (v_ready, k + 1), f"oT{k}": (oT_ready, k + 1), f"out{k}": (x1_ready, k + 1),
                                f"xT2_{k}": (xT2_ready, k + 1), f"q2_{k}": (q2_left, k + 1), f"out2_{k}": (x2_ready, k + 1)})
            sig, count = by_name[name]
            return sig.sem, sig.count(n, count)

        def early_max(n, f):
            lacking = CROSS_MAX if isinstance(n, int) and n == -1 else 0
            return SCORE_MAX - EARLY_MAX + f + lacking

        def window_max(n, f):
            late = f - EARLY_MAX
            if isinstance(n, int) and n == 0:
                return CROSS_MAX + late
            return late

        def cross_max(n, f):
            return (0 if isinstance(n, int) and n == B else WINDOW_MAX) - EARLY_MAX + f

        def exp_window(n, g):
            first = isinstance(n, int) and n == 0
            return 9 * g + (CROSS_EXP if first or g >= GROUPS // 2 else 0)

        def exp_cross(n, i):
            return i + (0 if isinstance(n, int) and n == B else 9 * GROUPS // 2)

        def user_window(n, g):
            first = isinstance(n, int) and n == 0
            return g + (CROSS_SUMS if first or g >= GROUPS // 2 else 0)

        def user_cross(n, tile):
            return tile + (0 if isinstance(n, int) and n == B else GROUPS // 2)

        def work_place(n, name):
            special = {-1: FRONT_FILLS, 0: FIRST_FILLS, B - 1: LAST_FILLS, B: CROSS_FILLS}
            order = special.get(n, FILLS) if isinstance(n, int) else FILLS
            return order, order.index(name)

        def work_claim(pe, n, name):
            order, j = work_place(n, name)
            if j >= 2:
                pe.wait_ge(*released(n, order[j - 2]))
            elif order is FIRST_FILLS:
                pe.wait_ge(*released(-1, FRONT_FILLS[j - 2]))
            elif order is not FRONT_FILLS:
                pe.wait_ge(*released(n - 1, FILLS[j - 2]))
            return ps_work[:, j % 2, :]

        def work_take(eng, n, name):
            order, j = work_place(n, name)
            if order is FRONT_FILLS:
                filled = j + 1
            elif order is FIRST_FILLS:
                filled = len(FRONT_FILLS) + j + 1
            elif order is CROSS_FILLS:
                filled = work_full.count(n, j + 1 - len(FRONT_FILLS))
            else:
                filled = work_full.count(n, j + 1)
            eng.wait_ge(work_full.sem, filled)
            return ps_work[:, j % 2, :]

        with nc.Block() as block:

            @block.sync
            def _(sp):
                n_const = 0

                def const(dst, src):
                    nonlocal n_const
                    sp.dma_start(dst, src).then_inc(consts_loaded.sem, 16)
                    n_const += 1

                def load_x(m):
                    sp.dma_start(x_in[:, :, :], t["x"][m].rearrange("(c p) d -> p c d", p=P)).then_inc(x_loaded.sem, 16)

                load_x(0)
                sp.dma_start(identf[:, :], t["c_identity"]).then_inc(first_loaded.sem, 16)
                for k in range(KD):
                    sp.dma_start(w_qkv[:, k, :], t["w_qkvT"][k * P:(k + 1) * P, :]).then_inc(first_loaded.sem, 16)
                const(ident[:, :], t["c_identity16"])
                const(mask_qk[:, :, :], t["c_mask_qk"])
                const(mask_kq[:, :], t["c_mask_kq"])
                const(mask_prefix[:, :], t["c_mask_prefix"])
                const(prefix_rows[:, :], t["c_prefix_rows"])
                const(v_prefix[:, :, :], t["c_prefix_ones"])
                const(ctx_rows[:, :], t["c_ctx_rows"])
                for dst, src in ((w_out, "w_outT"), (w_q2, "w_q2T"), (w_k2, "w_k2T"), (w_v2, "w_v2T"), (w_o2, "w_o2T")):
                    const(dst[:, :, :], t[src].rearrange("(k p) n -> p k n", p=P))
                const(b_q2[:, :], t["b_q2"])
                const(b_k2[:, :], t["b_k2"])
                const(b_v2[:, :], t["b_v2"].partition_broadcast(P))
                const(b_o2[:, :], t["b_o2"].partition_broadcast(P))
                assert n_const == N_CONST

                def store_part(dst, src, stored):
                    sp.dma_start(dst.rearrange("r h s -> h r s"), src).then_inc(stored.sem, 16)

                def stack_rows(dst, src, repeat, loaded):
                    dst = dst.rearrange("p h s -> p (h s)")
                    for block_, part, count in STACKS:
                        if repeat:
                            run = src[part:part + 1].rearrange("x r h s -> x r (h s)").broadcast_to([count, HD, dst.shape[-1]])
                        else:
                            run = src[0:count].rearrange("x r h s -> (x r) (h s)")
                        sp.dma_start(dst[block_ * HD:(block_ + count) * HD, :], run).then_inc(loaded.sem, 16)

                def split_front(n, tile):
                    heads = slice(8 * tile, 8 * tile + 8)
                    for part, sig in enumerate((part_hi, part_mid, part_lo)):
                        for side in range(2):
                            sp.wait_ge(sig.sem, sig.next(n, 2 * tile + side + 1))
                            store_part(t["qk_parts"][side, part, :, heads, :], parts[:, part, 2 * tile + side, :],
                                       qk_stored[tile])
                    if not (isinstance(n, int) and n == -1):
                        wait_apart(sp, sp_passed, exp_full.sem, exp_full.count(n, exp_window(n, GROUPS // KD * (tile + 1) - 1) + 9))
                    sp.wait_ge(qk_stored[tile].sem, qk_stored[tile].next(n, 16 * 6))
                    stack_rows(q_rows[:, heads, :], t["qk_parts"][0, :, :, heads, :], True, rows_loaded[tile])
                    stack_rows(k_rows[:, heads, :], t["qk_parts"][1, :, :, heads, :], False, rows_loaded[tile])

                def split_context_queries(n):
                    for tile in range(KD):
                        heads = slice(8 * tile, 8 * tile + 8)
                        for part, sig in enumerate((q2_hi, q2_mid, q2_lo)):
                            sp.wait_ge(sig.sem, sig.count(n, tile + 1))
                            store_part(t["ctx_q_parts"][part, :, heads, :], q2_parts[:, part, tile, :], q2_stored[tile])
                    for tile in range(KD):
                        heads = slice(8 * tile, 8 * tile + 8)
                        sp.wait_ge(q2_stored[tile].sem, q2_stored[tile].count(n, 16 * 3))
                        stack_rows(q2_rows[:, heads, :], t["ctx_q_parts"][:, :, heads, :], True, q2_loaded[tile])

                def stack_shift2(n):
                    sp.wait_ge(shiftT2_ready.sem, shiftT2_ready.count(n, 1))
                    for part in range(2):
                        sp.dma_start(q2_rows[SPLIT_ROWS + part:SPLIT_ROWS + part + 1, :, :],
                                     shiftT2[part * HEADS:(part + 1) * HEADS, :]).then_inc(shift2_stacked.sem, 16)

                def split_context_keys(n):
                    for part, (sig, count) in enumerate(((k2_hi, KD), (k2_mid, 1), (k2_lo, 1))):
                        sp.wait_ge(sig.sem, sig.count(n, count))
                        for tile in range(KD):
                            store_part(t["ctx_k_parts"][part, :, 8 * tile:8 * tile + 8, :], k2_parts[:, part, tile, :], k2_stored)
                    wait_apart(sp, sp_passed, exp_full.sem, exp_full.count(n, exp_window(n, GROUPS // 2)))
                    sp.wait_ge(k2_stored.sem, k2_stored.count(n, 16 * 3 * KD))
                    stack_rows(k2_rows[:, :, :], t["ctx_k_parts"], False, k2_loaded)

                def tiles_of(src):
                    return src.rearrange("(c p) d -> p c d", p=P)

                def iteration(n, last):
                    first = isinstance(n, int) and n == 0
                    if not first:
                        sp.wait_ge(ctxT_ready.sem, ctxT_ready.count(n, 0))
                    for rep in range(2):
                        sp.dma_start(ctx_in[rep * CTX:(rep + 1) * CTX, :], t["ctx"][n]).then_inc(ctx_loaded.sem, 16)
                    if not last:
                        sp.wait_ge(ln_done.sem, ln_done.count(n, TILES))
                        load_x(n + 1)
                    if not first:
                        split_context_queries(n)
                        sp.wait_ge(x1_ready.sem, x1_ready.count(n, 2))
                    sp.dma_start(x_res[:, :, :], tiles_of(t["x"][n])).then_inc(xres_loaded.sem, 16)
                    if not first:
                        sp.wait_ge(mask_ready.sem, mask_ready.count(n, 1))
                    sp.dma_start(mask_in[:, :, :], tiles_of(t["mask"][n])).then_inc(mask_loaded.sem, 16)
                    sp.wait_ge(shiftT_ready.sem, shiftT_ready.count(n, 1))
                    for part in range(2):
                        sp.dma_start(q_rows[SPLIT_ROWS + part:SPLIT_ROWS + part + 1, :, :],
                                     shiftT[part * HEADS:(part + 1) * HEADS, :]).then_inc(shift_stacked.sem, 16)
                    if not first:
                        stack_shift2(n)
                    if not last:
                        split_front(n, 0)
                    if not first:
                        store_x2(n)
                    if not last:
                        split_front(n, 1)
                    split_context_keys(n)

                def store_x2(n):
                    sp.wait_ge(x2_ready.sem, x2_ready.count(n, 2))
                    sp.dma_start(tiles_of(t["x2"][n - 1]), x1[:, :, :]).then_inc(x2_stored.sem, 16)

                for tile in range(KD):
                    split_front(-1, tile)
                iteration(0, False)
                for dst, src in later_loads:
                    sp.dma_start(dst, src).then_inc(later_loaded.sem, 16)
                with sp.Fori(1, B - 1) as n:
                    iteration(n, False)
                iteration(B - 1, True)
                split_context_queries(B)
                stack_shift2(B)
                store_x2(B)
                sp.wait_ge(later_loaded.sem, 16 * len(later_loads))
                sp.wait_ge(x2_stored.sem, x2_stored.count(B, 16))

            @block.gpsimd
            def _(pool):
                nc.gpsimd.memset(half[:, :], -0.5).then_inc(consts_set.sem, 1)
                nc.gpsimd.memset(eps[:, :], EPS).then_inc(consts_set.sem, 1)
                def low_parts(n, tiles):
                    for j in tiles:
                        pool.wait_ge(part_mid.sem, part_mid.next(n, j + 1))
                        nc.gpsimd.tensor_tensor(parts[:, 2, j, :], rest[:, j, :], parts[:, 1, j, :],
                                                ALU.subtract).then_inc(part_lo.sem, 1)

                def ln_first(m):
                    layernorm_rstd(nc, pool, moments, veps, eps[:, :], half[:, :], rstd, ln_moments, ln_veps, ln_rstd, m)

                def iteration(n, window=True, cross=True, last=False):
                    if cross:
                        layernorm_rstd(nc, pool, moments2, veps2, eps[:, :], half[:, :], rstd2, ln2_moments, ln2_veps, ln2_rstd, n)
                        pool.wait_ge(ln2_done.sem, ln2_done.count(n, TILES))
                        nc.gpsimd.tensor_tensor(x1[:, :, :], x1[:, :, :],
                                                b_o2[:, :].unsqueeze(1).broadcast_to([P, TILES, D]),
                                                ALU.add).then_inc(x1b_ready.sem, 1)
                        for tile in range(KD):
                            pool.wait_ge(q2_mid.sem, q2_mid.count(n, tile + 1))
                            nc.gpsimd.tensor_tensor(q2_parts[:, 2, tile, :], q2_rest[:, tile, :], q2_parts[:, 1, tile, :],
                                                    ALU.subtract).then_inc(q2_lo.sem, 1)
                    if window and not last:
                        ln_first(n + 1)
                    if window:
                        pool.wait_ge(k2_mid.sem, k2_mid.count(n, 1))
                        nc.gpsimd.tensor_tensor(k2_parts[:, 2, :, :], k2_rest[:, :, :], k2_parts[:, 1, :, :],
                                                ALU.subtract).then_inc(k2_lo.sem, 1)
                    if window and not last:
                        low_parts(n, range(4))

                pool.wait_ge(consts_set.sem, 2)
                ln_first(0)
                nc.gpsimd.memset(v_ones[:, :, :, HD:HD + 1], 1.0).then_inc(consts_set.sem, 1)
                nc.gpsimd.memset(v_ones[:, :, :, HD + 1:32], 0.0).then_inc(consts_set.sem, 1)
                nc.gpsimd.memset(shift[:, :, :], 0.0).then_inc(consts_set.sem, 1)
                pool.wait_ge(consts_set.sem, 5)
                nc.gpsimd.memset(k_rows[SPLIT_ROWS:SHIFT_ROWS, :, :], 1.0).then_inc(consts_set.sem, 1)
                pool.wait_ge(consts_set.sem, 6)
                nc.gpsimd.memset(k2_rows[SPLIT_ROWS:SHIFT_ROWS, :, :], 1.0).then_inc(consts_set.sem, 1)
                pool.wait_ge(consts_set.sem, 7)
                pool.wait_ge(consts_loaded.sem, 16 * N_CONST)
                nc.gpsimd.tensor_scalar(b_q2s[:, :], b_q2[:, :], QK_SCALE, None, ALU.mult).then_inc(consts_set.sem, 1)
                nc.gpsimd.tensor_scalar(w_q2[:, :, :], w_q2[:, :, :], QK_SCALE, None, ALU.mult).then_inc(consts_set.sem, 1)
                low_parts(-1, range(4))
                iteration(0, cross=False)
                with pool.Fori(1, B - 1) as n:
                    iteration(n)
                iteration(B - 1, last=True)
                iteration(B, window=False)

            @block.vector
            def _(dve):
                def ln_first(m):
                    dve.wait_ge(x_loaded.sem, x_loaded.count(m, 16))
                    layernorm_statistics(nc, dve, x_in, stats, moments, passed, ln_stats, ln_moments, m)
                    layernorm_apply(nc, dve, x_in, xn, moments, rstd, ln_rstd, ln_done, m)

                def split_rest(n, tiles):
                    for j in tiles:
                        ps = work_take(dve, n, PROJECTIONS[j])
                        dve.wait_ge(part_hi.sem, part_hi.next(n, j + 1))
                        nc.vector.scalar_tensor_tensor(rest[:, j, :], ps, QK_SCALE if j % 2 == 0 else 1.0, parts[:, 0, j, :],
                                                       ALU.mult, ALU.subtract).then_inc(part_rest.sem, 1)

                def prefix_values(n):
                    ps = work_take(dve, n, "vg")
                    nc.vector.tensor_tensor(v_prefix[:, :, 0:HD], ps[:, 0:D].rearrange("p (h w) -> p h w", w=HD),
                                            prefix_rows[:, :].unsqueeze(2).broadcast_to([P, HEADS, HD]),
                                            ALU.mult).then_inc(vprefix_ready.sem, 1)

                def maximum(n, place, out_of, f):
                    dve.wait_ge(max_full.sem, max_full.count(n, place + 1))
                    out, src = out_of(f, ps_max[:, place % 2, :])
                    nc.vector.tensor_reduce(out, src, AX.X, ALU.max).then_inc(max_free.sem, 1)

                def early_maxima(n, fills):
                    for f in fills:
                        maximum(n, early_max(n, f), window_fill, f)

                def window_maxima(n, fills):
                    for f in fills:
                        if f >= EARLY_MAX:
                            maximum(n, window_max(n, f), window_fill, f)

                def context_maxima(n):
                    for f in range(CROSS_MAX):
                        maximum(n, cross_max(n, f), context_fill, f)
                    dve.wait_ge(max_free.sem, max_free.count(n, cross_max(n, CROSS_MAX)))
                    shift_parts(n, top2, shift2, shift2_hi, shift2_ready)

                def window_fill(f, ps):
                    c, j = WINDOW_ORDER[f]
                    if j == 8:
                        return top_prefix[:, c - 2, :], ps[:, 0:HEADS * PREFIX].rearrange("p (h k) -> p h k", h=HEADS)
                    heads = 4 if c == 0 else 2
                    return top[:, c, heads * j:heads * (j + 1)], ps.rearrange("p (h k) -> p h k", h=heads)

                def context_fill(f, ps):
                    c, tile = f % TILES, f // TILES
                    return top2[:, c, 8 * tile:8 * tile + 8], ps.rearrange("p (h k) -> p h k", h=8)

                def shift_parts(n, tops, out, hi, ready):
                    nc.vector.tensor_scalar(out[:, :, 0:HEADS], tops[:, :, :], -1.0, None,
                                            ALU.mult).then_inc(hi.sem, 1)
                    dve.wait_ge(hi.sem, hi.count(n, 1))
                    nc.vector.scalar_tensor_tensor(out[:, :, HEADS:2 * HEADS], tops[:, :, :], -1.0,
                                                   out[:, :, 0:HEADS], ALU.mult, ALU.subtract
                                                   ).then_inc(ready.sem, 1)

                def normalise_heads(n, g):
                    ps = work_take(dve, n, f"s{g}").rearrange("p (c j w) -> p c j w", c=TILES, w=32)
                    k = g + 1 if g < GROUPS - 1 else 0
                    nc.vector.reciprocal(rsum[:, g % 2, :, :, :], ps[:, :, :, HD:HD + 1]).then_inc(sums_recip.sem, 1)
                    dve.wait_ge(sums_recip.sem, sums_recip.count(n, k))
                    cols = slice(GROUP * HD * g, GROUP * HD * (g + 1))
                    nc.vector.tensor_tensor(heads_out[:, :, cols].rearrange("p c (j w) -> p c j w", w=HD), ps[:, :, :, 0:HD],
                                            rsum[:, g % 2, :, :, :].broadcast_to([P, TILES, GROUP, HD]),
                                            ALU.mult).then_inc(heads_ready.sem, 1)

                def normalise_cross(n, tile):
                    dve.wait_ge(probs_used.sem, probs_used.count(n, user_cross(n, tile) + 1))
                    nc.vector.reciprocal(rden[:, :], ps_out[:, 1, :]).then_inc(out2_recip.sem, 1)
                    dve.wait_ge(out2_recip.sem, out2_recip.count(n, tile + 1))
                    nc.vector.tensor_tensor(oT2[:, tile, :], ps_out[:, 0, :], rden[:, :],
                                            ALU.mult).then_inc(oT2_ready.sem, 1)

                def residual(n, names, base, out, sig):
                    for i, name in enumerate(names):
                        ps = work_take(dve, n, name)
                        nc.vector.tensor_tensor(out[:, 2 * i:2 * i + 2, :], ps.rearrange("p (c d) -> p c d", c=2),
                                                base[:, 2 * i:2 * i + 2, :], ALU.add).then_inc(sig.sem, 1)

                def context_query_rest(n, tile):
                    ps = work_take(dve, n, f"q2_{tile}")
                    dve.wait_ge(q2_hi.sem, q2_hi.count(n, tile + 1))
                    nc.vector.scalar_tensor_tensor(q2_rest[:, tile, :], ps, b_q2s[:, tile:tile + 1], q2_parts[:, 0, tile, :],
                                                   ALU.add, ALU.subtract).then_inc(q2_left.sem, 1)

                def context_key_rest(n):
                    ps = work_take(dve, n, "k2")
                    dve.wait_ge(k2_hi.sem, k2_hi.count(n, KD))
                    for tile in range(KD):
                        nc.vector.scalar_tensor_tensor(k2_rest[:, tile, :], ps[:, tile * CTX:(tile + 1) * CTX],
                                                       b_k2[:, tile:tile + 1], k2_parts[:, 0, tile, :],
                                                       ALU.add, ALU.subtract).then_inc(k2_left.sem, 1)

                def context_values(n):
                    ps = work_take(dve, n, "v2")
                    nc.vector.tensor_tensor(v2[:, :], ps[:, 0:D], b_v2[:, :], ALU.add).then_inc(v2_biased.sem, 1)
                    dve.wait_ge(v2_biased.sem, v2_biased.count(n, 1))
                    nc.vector.tensor_tensor(v2pair[:, :], v2[:, :], ctx_rows[:, :], ALU.mult).then_inc(v2_ready.sem, 1)

                def iteration(n, window=True, cross=True, last=False):
                    if window:
                        window_maxima(n, range(BEFORE_S3))
                    if cross:
                        normalise_heads(n, GROUPS - 1)
                    if window:
                        window_maxima(n, range(BEFORE_S3, BEFORE_OUT1))
                    if cross:
                        dve.wait_ge(xres_loaded.sem, xres_loaded.count(n, 0))
                        dve.wait_ge(x2_stored.sem, x2_stored.count(n, 0))
                        residual(n, ("out0", "out1"), x_res, x1, x1_ready)
                        dve.wait_ge(x1_ready.sem, x1_ready.count(n, 2))
                        layernorm_statistics(nc, dve, x1, stats2, moments2, passed, ln2_stats, ln2_moments, n)
                    if window:
                        window_maxima(n, range(BEFORE_OUT1, BEFORE_V0))
                    if cross:
                        layernorm_apply(nc, dve, x1, xn2, moments2, rstd2, ln2_rstd, ln2_done, n)
                        dve.wait_ge(mask_loaded.sem, mask_loaded.count(n, 0))
                        nc.vector.tensor_scalar(mask_add[:, :, :, :],
                                                mask_in[:, :, :].unsqueeze(2).broadcast_to([P, TILES, 2, CTX]), 0, NEG_MASK,
                                                ALU.is_equal, ALU.mult).then_inc(mask_ready.sem, 1)
                    if window:
                        window_maxima(n, range(BEFORE_V0, BEFORE_Q0))
                    if cross:
                        context_query_rest(n, 0)
                    if window:
                        window_maxima(n, range(BEFORE_Q0, BEFORE_Q1))
                    if cross:
                        context_query_rest(n, 1)
                    if window:
                        window_maxima(n, range(BEFORE_Q1, BEFORE_VG))
                        if isinstance(n, int) and n == 0:
                            dve.wait_ge(consts_loaded.sem, 16 * N_CONST)
                        prefix_values(n)
                        window_maxima(n, range(BEFORE_VG, WINDOW_MAX))
                        dve.wait_ge(max_free.sem, max_free.count(n, window_max(n, WINDOW_MAX)))
                        nc.vector.tensor_tensor(top[:, 2:4, :], top[:, 2:4, :], top_prefix[:, :, :],
                                                ALU.max).then_inc(top_joined.sem, 1)
                        dve.wait_ge(top_joined.sem, top_joined.count(n, 1))
                        shift_parts(n, top, shift, shift_hi, shift_ready)
                    if cross:
                        context_maxima(n)
                    if window:
                        context_key_rest(n)
                        if not last:
                            ln_first(n + 1)
                            split_rest(n, (0, 1))
                    if cross:
                        normalise_cross(n, 0)
                    if window:
                        if not last:
                            split_rest(n, (2,))
                        normalise_heads(n, 0)
                    if cross:
                        normalise_cross(n, 1)
                    if window:
                        if not last:
                            split_rest(n, (3,))
                        context_values(n)
                    if cross:
                        dve.wait_ge(x1b_ready.sem, x1b_ready.count(n, 1))
                        residual(n, ("out2_0", "out2_1"), x1, x1, x2_ready)
                    if window:
                        normalise_heads(n, 1)
                        if not last:
                            early_maxima(n, range(EARLY_BEFORE_S2))
                        normalise_heads(n, 2)
                        if not last:
                            early_maxima(n, range(EARLY_BEFORE_S2, EARLY_MAX))

                dve.sem_inc(max_free.sem, 2)
                dve.sem_inc(x2_stored.sem, 16)
                ln_first(0)
                split_rest(-1, range(4))
                dve.wait_ge(consts_set.sem, 7)
                early_maxima(-1, range(EARLY_MAX))
                iteration(0, cross=False)
                with dve.Fori(1, B - 1) as n:
                    iteration(n)
                iteration(B - 1, last=True)
                iteration(B, window=False)

            @block.scalar
            def _(act):
                def copy_out(n, name, sig, pieces):
                    ps = work_take(act, n, name)
                    for out, src in pieces(ps):
                        nc.scalar.activation(out, src, ACT.Copy).then_inc(sig.sem, 1)

                def features(n, k):
                    copy_out(n, f"xT{k}", xT_ready, lambda ps: [(xT[:, k, :], ps)])

                def high_part(n, j):
                    ps = work_take(act, n, PROJECTIONS[j])
                    nc.scalar.activation(parts[:, 0, j, :], ps, ACT.Copy,
                                         scale=QK_SCALE if j % 2 == 0 else 1.0).then_inc(part_hi.sem, 1)

                def middle_part(n, j):
                    act.wait_ge(part_rest.sem, part_rest.next(n, j + 1))
                    nc.scalar.activation(parts[:, 1, j, :], rest[:, j, :], ACT.Copy).then_inc(part_mid.sem, 1)

                def shift_rows(n, name, out, sig):
                    ps = work_take(act, n, name)
                    nc.scalar.activation(out[:, :], ps.bitcast(BF16)[:, 0:S], ACT.Copy).then_inc(sig.sem, 1)

                def exps(n, user, fills):
                    for f, (lo, width) in fills:
                        act.wait_ge(exp_full.sem, exp_full.count(n, f + 1))
                        nc.scalar.activation(probs[:, user % 2, lo:lo + width], ps_exp[:, f % 2, 0:width],
                                             ACT.Exp).then_inc(exp_done.sem, 1)

                def probs_claim(n, user):
                    act.wait_ge(probs_used.sem, probs_used.count(n, user - 1))

                def head_exps(n, g, j):
                    cols = [(HEAD_COLS * j, 512), (HEAD_COLS * j + 512, 384)] if j < GROUP else [(GROUP * HEAD_COLS, 256)]
                    exps(n, user_window(n, g), list(enumerate(cols, exp_window(n, g) + 2 * j)))

                def group_sums(n, g):
                    act.wait_ge(probs_used.sem, probs_used.count(n, user_window(n, g) + 1))
                    if not (isinstance(n, int) and n == 0 and g < 2):
                        act.wait_ge(heads_ready.sem, heads_ready.count(n, g - 1))
                    nc.scalar.activation(sums[:, g % 2, :], ps_out[:, g % 2, :], ACT.Copy).then_inc(sums_ready.sem, 1)

                def values(n, i):
                    copy_out(n, f"v{i}", v_ready, lambda ps: [
                        (v_ones[:, 2 * i:2 * i + 2, :, 0:HD], ps.rearrange("p (c h w) -> p c h w", c=2, w=HD))])

                def cross_exp(n, i):
                    if i % 4 == 0:
                        probs_claim(n, user_cross(n, i // 4))
                    exps(n, user_cross(n, i // 4), [(exp_cross(n, i), (512 * (i % 4), 512))])

                def iteration(n, window=True, cross=True, last=False):
                    if cross:
                        for k in range(KD):
                            copy_out(n, f"oT{k}", oT_ready, lambda ps: [(oT[:, k, :], ps)])
                    if window:
                        values(n, 0)
                        values(n, 1)
                    if cross:
                        for k in range(KD):
                            copy_out(n, f"xT2_{k}", xT2_ready, lambda ps: [(xT2[:, k, :], ps)])
                        for tile in range(KD):
                            ps = work_take(act, n, f"q2_{tile}")
                            nc.scalar.activation(q2_parts[:, 0, tile, :], ps, ACT.Identity,
                                                 bias=b_q2s[:, tile:tile + 1]).then_inc(q2_hi.sem, 1)
                            act.wait_ge(q2_left.sem, q2_left.count(n, tile + 1))
                            nc.scalar.activation(q2_parts[:, 1, tile, :], q2_rest[:, tile, :], ACT.Copy).then_inc(q2_mid.sem, 1)
                    if window:
                        shift_rows(n, "shiftT", shiftT, shiftT_ready)
                    front = window and not last
                    if window:
                        probs_claim(n, user_window(n, 0))
                    for j in range(GROUP + 1):
                        if window:
                            head_exps(n, 0, j)
                        if j == 1 and window:
                            copy_out(n, "ctxT", ctxT_ready, lambda ps: [
                                (ctxT[:, :, :, :].rearrange("p k r c -> p (k r c)"), ps[:, 0:KD * P])])
                        if j == 3 and window:
                            ps = work_take(act, n, "k2")
                            for tile in range(KD):
                                nc.scalar.activation(k2_parts[:, 0, tile, :], ps[:, tile * CTX:(tile + 1) * CTX], ACT.Identity,
                                                     bias=b_k2[:, tile:tile + 1]).then_inc(k2_hi.sem, 1)
                    if cross:
                        shift_rows(n, "shiftT2", shiftT2, shiftT2_ready)
                    if window:
                        probs_claim(n, user_window(n, 1))
                        for j in range(GROUP + 1):
                            head_exps(n, 1, j)
                            if j in (3, 4) and front:
                                features(n, j - 3)
                        act.wait_ge(k2_left.sem, k2_left.count(n, KD))
                        nc.scalar.activation(k2_parts[:, 1, :, :], k2_rest[:, :, :], ACT.Copy).then_inc(k2_mid.sem, 1)
                        group_sums(n, 0)
                    for i in range(4):
                        if cross:
                            cross_exp(n, i)
                        if i == 2 and front:
                            high_part(n, 0)
                    if window:
                        group_sums(n, 1)
                    if front:
                        middle_part(n, 0)
                        high_part(n, 1)
                    for i in range(4, PAIRS):
                        if cross:
                            cross_exp(n, i)
                        if i == 5 and front:
                            middle_part(n, 1)
                            high_part(n, 2)
                    if front:
                        middle_part(n, 2)
                    if window:
                        for g in (2, 3):
                            probs_claim(n, user_window(n, g))
                            for j in range(GROUP + 1):
                                head_exps(n, g, j)
                                if (g, j) == (2, 0) and front:
                                    high_part(n, 3)
                                if (g, j) == (3, 0) and front:
                                    middle_part(n, 3)
                            if g == 3:
                                group_sums(n, 2)
                        group_sums(n, 3)

                act.sem_inc(exp_done.sem, 2)
                for k in range(KD):
                    features(-1, k)
                for tile in range(KD):
                    for side in range(2):
                        high_part(-1, 2 * tile + side)
                    for side in range(2):
                        middle_part(-1, 2 * tile + side)
                act.wait_ge(consts_set.sem, 7)
                iteration(0, cross=False)
                act.wait_ge(consts_set.sem, 9)
                with act.Fori(1, B - 1) as n:
                    iteration(n)
                iteration(B - 1, last=True)
                iteration(B, window=False)

            @block.tensor
            def _(pe):
                def features(n, k):
                    ps = work_claim(pe, n, f"xT{k}")
                    pe.wait_ge(ln_done.sem, ln_done.next(n, TILES))
                    for c in range(TILES):
                        mm = nc.tensor.transpose(ps[:, c * P:(c + 1) * P], xn[:, c, k * P:(k + 1) * P], identf[:, :])
                    mm.then_inc(work_full.sem, 1)

                def queries_or_keys(n, j):
                    if j == 0:
                        pe.wait_ge(xT_ready.sem, xT_ready.next(n, KD))
                    ps = work_claim(pe, n, PROJECTIONS[j])
                    col = (j % 2) * D + (j // 2) * P
                    for k in range(KD):
                        mm = nc.tensor.matmul(ps, w_qkv[:, k, col:col + P], xT[:, k, :],
                                              start=(k == 0), stop=(k == KD - 1))
                    mm.then_inc(work_full.sem, 1)

                def values(n, i):
                    ps = work_claim(pe, n, f"v{i}")
                    for c in (2 * i, 2 * i + 1):
                        for k in range(KD):
                            mm = nc.tensor.matmul(ps[:, (c % 2) * D:(c % 2 + 1) * D], xT[:, k, c * P:(c + 1) * P],
                                                  w_qkv[:, k, 2 * D:3 * D], start=(k == 0 and c % 2 == 0),
                                                  stop=(k == KD - 1), skip_group_check=True)
                    mm.then_inc(work_full.sem, 1)

                def prefix_values(n):
                    ps = work_claim(pe, n, "vg")
                    for r in range(GROUP):
                        for k in range(KD):
                            mm = nc.tensor.matmul(ps[32 * r:32 * r + 32, 0:D], xT[:, k, 0:32], w_qkv[:, k, 2 * D:3 * D],
                                                  start=(k == 0), stop=(k == KD - 1), skip_group_check=True)
                    mm.then_inc(work_full.sem, 1)

                def max_claim(n, f):
                    pe.wait_ge(max_free.sem, max_free.count(n, f - 1))
                    return ps_max[:, f % 2, :]

                def window_scores(n, f, early=False):
                    c, j = WINDOW_ORDER[f]
                    if c == 0:
                        heads, width, mask = 4, P, mask_qk[:, 1, P:2 * P]
                    else:
                        heads, width, mask = 2, 2 * P, mask_qk[:, min(c, 2) - 1, :]
                    if f % HALF_FILLS == 0 and f < 2 * HALF_FILLS:
                        loaded = rows_loaded[f // HALF_FILLS]
                        count = loaded.next if early else loaded.count
                        pe.wait_ge(loaded.sem, count(n, 16 * 2 * len(STACKS)))
                    q0 = c * P
                    ps = max_claim(n, early_max(n, f) if early else window_max(n, f))
                    if j < 8:
                        nc.tensor.matmul(ps.rearrange("p (h k) -> p h k", h=heads), ident[:, :],
                                         mask.unsqueeze(1).broadcast_to([P, heads, width]),
                                         start=True, stop=False, skip_group_check=True)
                        for i in range(heads):
                            h = heads * j + i
                            mm = nc.tensor.matmul(ps[:, i * width:(i + 1) * width], q_rows[0:SPLIT_ROWS, h, q0:q0 + P],
                                                  k_rows[0:SPLIT_ROWS, h, q0 + P - width:q0 + P], start=False,
                                                  stop=True, skip_group_check=True)
                    else:
                        for h in range(HEADS):
                            mm = nc.tensor.matmul(ps[:, h * PREFIX:(h + 1) * PREFIX], q_rows[0:SPLIT_ROWS, h, q0:q0 + P],
                                                  k_rows[0:SPLIT_ROWS, h, 0:PREFIX], start=(h == 0), stop=True,
                                                  skip_group_check=True)
                    mm.then_inc(max_full.sem, 1)

                def shift_transposes(n, name, src, ready):
                    ps = work_claim(pe, n, name)
                    pe.wait_ge(ready.sem, ready.count(n, 1))
                    for c in range(TILES):
                        mm = nc.tensor.transpose(ps.bitcast(BF16)[:, c * P:(c + 1) * P], src[:, c, :], ident[:, :])
                    mm.then_inc(work_full.sem, 1)

                def exp_claim(n, f):
                    pe.wait_ge(exp_done.sem, exp_done.count(n, f - 1))
                    return ps_exp[:, f % 2, :]

                def window_shifted(n, g, j):
                    f = exp_window(n, g) + 2 * j
                    if j < GROUP:
                        h = group_heads(g)[j]
                        for tiles, mask in (((0, 1), mask_kq[:, 0:512]), ((2, 3), mask_kq[:, 256:640])):
                            ps = exp_claim(n, f)
                            nc.tensor.matmul(ps[:, 0:mask.shape[-1]], ident[:, :], mask, start=True, stop=False, skip_group_check=True)
                            for i, kt in enumerate(tiles):
                                q0, q1 = kt * P, min(kt + 2, TILES) * P
                                mm = nc.tensor.matmul(ps[:, 256 * i:256 * i + q1 - q0], k_rows[:, h, kt * P:(kt + 1) * P],
                                                      q_rows[:, h, q0:q1], start=False, stop=True, skip_group_check=True)
                            mm.then_inc(exp_full.sem, 1)
                            f += 1
                        return
                    ps = exp_claim(n, f)
                    nc.tensor.matmul(ps[:, 0:256], ident[:, :], mask_prefix[:, :], start=True, stop=False,
                                     skip_group_check=True)
                    for j, h in enumerate(group_heads(g)):
                        mm = nc.tensor.matmul(ps[32 * j:32 * j + 32, 0:256], k_rows[:, h, 0:32], q_rows[:, h, 256:512],
                                              start=False, stop=True, skip_group_check=True)
                    mm.then_inc(exp_full.sem, 1)

                def window_values(n, g, kt):
                    if kt == 0:
                        if isinstance(n, int) and n == 0:
                            if g >= 2:
                                pe.wait_ge(sums_ready.sem, sums_ready.count(n, g - 1))
                        elif g >= 2:
                            pe.wait_ge(oT2_ready.sem, oT2_ready.count(n, KD))
                        else:
                            pe.wait_ge(sums_ready.sem, sums_ready.count(n, 0))
                        pe.wait_ge(exp_done.sem, exp_done.count(n, exp_window(n, g) + 9))
                        if g == 0:
                            pe.wait_ge(v_ready.sem, v_ready.count(n, 2))
                            pe.wait_ge(vprefix_ready.sem, vprefix_ready.count(n, 1))
                    pr = probs[:, g % 2, :]
                    for j, h in enumerate(group_heads(g)):
                        if kt < TILES:
                            q0, q1 = kt * P, min(kt + 2, TILES) * P
                            lhsT = v_ones[:, kt, h, :]
                            rhs = pr[:, HEAD_COLS * j + 256 * kt:HEAD_COLS * j + 256 * kt + q1 - q0]
                        else:
                            q0, q1 = 256, 512
                            lhsT = v_prefix[:, h, :]
                            rhs = pr[:, GROUP * HEAD_COLS:GROUP * HEAD_COLS + 256]
                        mm = nc.tensor.matmul(ps_out[32 * j:32 * j + 32, g % 2, q0:q1], lhsT, rhs,
                                              start=(kt == 0), stop=True, skip_group_check=True)
                    if kt == TILES:
                        mm.then_inc(probs_used.sem, 1)

                def sums_transposes(n, g):
                    ps = work_claim(pe, n, f"s{g}")
                    pe.wait_ge(sums_ready.sem, sums_ready.count(n, g + 1 if g < GROUPS - 1 else 0))
                    for c in range(TILES):
                        mm = nc.tensor.transpose(ps[:, c * P:(c + 1) * P], sums[:, g % 2, c * P:(c + 1) * P], identf[:, :])
                    mm.then_inc(work_full.sem, 1)

                def heads_transposes(n):
                    for k in range(KD):
                        ps = work_claim(pe, n, f"oT{k}")
                        pe.wait_ge(heads_ready.sem, heads_ready.count(n, 0))
                        for c in range(TILES):
                            mm = nc.tensor.transpose(ps[:, c * P:(c + 1) * P], heads_out[:, c, k * P:(k + 1) * P], identf[:, :])
                        mm.then_inc(work_full.sem, 1)

                def output(n, name, src, w, ready):
                    if name[-1] == "0":
                        pe.wait_ge(ready.sem, ready.count(n, KD))
                    ps = work_claim(pe, n, name)
                    i = int(name[-1])
                    for c in (2 * i, 2 * i + 1):
                        for tile in range(KD):
                            mm = nc.tensor.matmul(ps[:, (c % 2) * D:(c % 2 + 1) * D], src[:, tile, c * P:(c + 1) * P],
                                                  w[:, tile, :], start=(tile == 0 and c % 2 == 0),
                                                  stop=(tile == KD - 1), skip_group_check=True)
                    mm.then_inc(work_full.sem, 1)

                def source_features(n):
                    ps = work_claim(pe, n, "ctxT")
                    pe.wait_ge(ctx_loaded.sem, ctx_loaded.count(n, 32))
                    for k in range(KD):
                        mm = nc.tensor.transpose(ps[:, k * P:(k + 1) * P], ctx_in[:, k * P:(k + 1) * P], identf[:, :])
                    mm.then_inc(work_full.sem, 1)

                def source_keys(n):
                    ps = work_claim(pe, n, "k2")
                    pe.wait_ge(ctxT_ready.sem, ctxT_ready.count(n, 1))
                    for tile in range(KD):
                        for k in range(KD):
                            mm = nc.tensor.matmul(ps[:, tile * CTX:(tile + 1) * CTX], w_k2[:, k, tile * P:(tile + 1) * P],
                                                  ctxT[:, k, 0, :], start=(tile == 0 and k == 0), stop=(k == KD - 1),
                                                  skip_group_check=True)
                    mm.then_inc(work_full.sem, 1)

                def source_values(n):
                    ps = work_claim(pe, n, "v2")
                    for k in range(KD):
                        mm = nc.tensor.matmul(ps[:, 0:D], ctxT[:, k, :, :].rearrange("p r c -> p (r c)"), w_v2[:, k, :],
                                              start=(k == 0), stop=(k == KD - 1))
                    mm.then_inc(work_full.sem, 1)

                def context_features(n):
                    for k in range(KD):
                        ps = work_claim(pe, n, f"xT2_{k}")
                        pe.wait_ge(ln2_done.sem, ln2_done.count(n, TILES))
                        for c in range(TILES):
                            mm = nc.tensor.transpose(ps[:, c * P:(c + 1) * P], xn2[:, c, k * P:(k + 1) * P], identf[:, :])
                        mm.then_inc(work_full.sem, 1)

                def context_queries(n, tile):
                    pe.wait_ge(xT2_ready.sem, xT2_ready.count(n, KD))
                    ps = work_claim(pe, n, f"q2_{tile}")
                    for k in range(KD):
                        mm = nc.tensor.matmul(ps, w_q2[:, k, tile * P:(tile + 1) * P], xT2[:, k, :],
                                              start=(k == 0), stop=(k == KD - 1))
                    mm.then_inc(work_full.sem, 1)

                def context_scores(n, tile, query_tiles):
                    if (tile, query_tiles[0]) == (0, 0):
                        pe.wait_ge(mask_ready.sem, mask_ready.count(n, 1))
                        pe.wait_ge(k2_loaded.sem, k2_loaded.count(n, 0))
                    for c in query_tiles:
                        f = TILES * tile + c
                        if c == 0:
                            pe.wait_ge(q2_loaded[tile].sem, q2_loaded[tile].count(n, 16 * len(STACKS)))
                        ps = max_claim(n, cross_max(n, f))
                        nc.tensor.matmul(ps.rearrange("p (h k) -> p h k", h=8), ident[:, :],
                                         mask_add[:, c, 0, :].unsqueeze(1).broadcast_to([P, 8, CTX]),
                                         start=True, stop=False, skip_group_check=True)
                        for j in range(8):
                            mm = nc.tensor.matmul(ps[:, j * CTX:(j + 1) * CTX], q2_rows[0:SPLIT_ROWS, 8 * tile + j, c * P:(c + 1) * P],
                                                  k2_rows[0:SPLIT_ROWS, 8 * tile + j, :], start=False, stop=True,
                                                  skip_group_check=True)
                        mm.then_inc(max_full.sem, 1)

                def context_shifted(n, i):
                    if i == 0:
                        pe.wait_ge(shift2_stacked.sem, shift2_stacked.count(n, 32))
                    ps = exp_claim(n, exp_cross(n, i))
                    for c in range(TILES):
                        nc.tensor.matmul(ps[:, c * P:(c + 1) * P], mask_add[:, c, :, :].rearrange("p r k -> p (r k)"),
                                         ident[:, :], start=(c == 0), stop=False, skip_group_check=True)
                    for odd in range(2):
                        mm = nc.tensor.matmul(ps[CTX * odd:CTX * odd + CTX, :], k2_rows[:, 2 * i + odd, :], q2_rows[:, 2 * i + odd, :],
                                              start=False, stop=True, skip_group_check=True)
                    mm.then_inc(exp_full.sem, 1)

                def context_values(n, tile, side):
                    if side == 0:
                        if tile == 0:
                            pe.wait_ge(v2_ready.sem, v2_ready.count(n, 0))
                        if tile == 0:
                            left = 0 if isinstance(n, int) and n == B else GROUPS // 2
                            pe.wait_ge(sums_ready.sem, sums_ready.count(n, left))
                        else:
                            pe.wait_ge(oT2_ready.sem, oT2_ready.count(n, 1))
                        pe.wait_ge(exp_done.sem, exp_done.count(n, exp_cross(n, 4 * tile + 3) + 1))
                    for j in range(GROUP):
                        w = slice(32 * (4 * tile + j), 32 * (4 * tile + j) + 32)
                        mm = nc.tensor.matmul(ps_out[32 * j:32 * j + 32, side, :],
                                              v2pair[:, w] if side == 0 else ctx_rows[:, 0:32],
                                              probs[:, tile, 512 * j:512 * j + 512],
                                              start=True, stop=True, skip_group_check=True)
                    if side == 1:
                        mm.then_inc(probs_used.sem, 1)

                def iteration(n, window=True, cross=True, last=False):
                    def maxima(lo, hi):
                        if window:
                            for f in range(max(lo, EARLY_MAX), hi):
                                window_scores(n, f)

                    maxima(0, BEFORE_S3)
                    if cross:
                        sums_transposes(n, GROUPS - 1)
                    maxima(BEFORE_S3, BEFORE_HEADS)
                    if cross:
                        heads_transposes(n)
                    maxima(BEFORE_HEADS, BEFORE_OUT0)
                    if cross:
                        output(n, "out0", oT, w_out, oT_ready)
                    maxima(BEFORE_OUT0, BEFORE_OUT1)
                    if cross:
                        output(n, "out1", oT, w_out, oT_ready)
                    maxima(BEFORE_OUT1, BEFORE_V0)
                    if window:
                        values(n, 0)
                    maxima(BEFORE_V0, BEFORE_V1)
                    if window:
                        values(n, 1)
                    if cross:
                        context_features(n)
                    maxima(BEFORE_V1, BEFORE_Q0)
                    if cross:
                        context_queries(n, 0)
                    maxima(BEFORE_Q0, BEFORE_Q1)
                    if cross:
                        context_queries(n, 1)
                    maxima(BEFORE_Q1, BEFORE_VG)
                    if window:
                        prefix_values(n)
                    maxima(BEFORE_VG, WINDOW_MAX)
                    if window:
                        shift_transposes(n, "shiftT", shift, shift_ready)
                    if cross:
                        context_scores(n, 0, range(TILES))
                    front = window and not last
                    for j in range(GROUP + 1):
                        if j < TILES and cross:
                            context_scores(n, 1, [j])
                        if window:
                            if j == 0:
                                pe.wait_ge(shift_stacked.sem, shift_stacked.count(n, 32))
                            window_shifted(n, 0, j)
                            if j == 1:
                                source_features(n)
                            if j == 3:
                                source_keys(n)
                    if cross:
                        shift_transposes(n, "shiftT2", shift2, shift2_ready)
                    if window:
                        for j in range(GROUP + 1):
                            window_shifted(n, 1, j)
                            window_values(n, 0, j)
                            if j in (3, 4) and front:
                                features(n, j - 3)
                    for j in range(GROUP + 1):
                        if j < PAIRS // 2 and cross:
                            context_shifted(n, j)
                        if window:
                            window_values(n, 1, j)
                        if j == 2 and front:
                            queries_or_keys(n, 0)
                    if front:
                        queries_or_keys(n, 1)
                    if cross:
                        for side in range(2):
                            context_values(n, 0, side)
                    for i in range(PAIRS // 2, PAIRS):
                        if cross:
                            context_shifted(n, i)
                        if i == 5 and front:
                            queries_or_keys(n, 2)
                        if i == 7 and window:
                            sums_transposes(n, 0)
                    if cross:
                        for side in range(2):
                            context_values(n, 1, side)
                    if window:
                        for j in range(GROUP + 1):
                            window_shifted(n, 2, j)
                            if j == 0 and front:
                                queries_or_keys(n, 3)
                            if j == 2:
                                source_values(n)
                    early = iter(range(EARLY_MAX if front else 0))
                    for j in range(GROUP + 1):
                        if window:
                            window_shifted(n, 3, j)
                            window_values(n, 2, j)
                        if j in (1, 2) and cross:
                            output(n, f"out2_{j - 1}", oT2, w_o2, oT2_ready)
                        if j == 3 and window:
                            sums_transposes(n, 1)
                        for f in islice(early, j > 3):
                            window_scores(n, f, early=True)
                    if window:
                        for j in range(GROUP + 1):
                            window_values(n, 3, j)
                            if j == 1:
                                sums_transposes(n, 2)
                            for f in islice(early, 2 if j else 0):
                                window_scores(n, f, early=True)

                pe.wait_ge(first_loaded.sem, 16 * (1 + KD))
                pe.sem_inc(probs_used.sem, 2)
                for k in range(KD):
                    features(-1, k)
                for j in range(len(PROJECTIONS)):
                    queries_or_keys(-1, j)
                pe.wait_ge(consts_loaded.sem, 16 * N_CONST)
                for f in range(EARLY_MAX):
                    window_scores(-1, f, early=True)
                iteration(0, cross=False)
                with pe.Fori(1, B - 1) as n:
                    iteration(n)
                iteration(B - 1, last=True)
                iteration(B, window=False)


N_CONST = 7 + 5 + 4
REGION = B * S + P
SPARE_TILES = 10
ROW = 2 * D + 4
NO_TOKEN = float(1 << 20)
E, DF = 8, 1024
KF = DF // P
MH, MD = 4, 64
M_SCALE = MD ** -0.5
POS = 16
NGROUPS = S // (TILES * POS)
STEPS = B * S // P + E
TABLE = STEPS + 2

ROUTE_FILLS = ["out0", "out1", "yT0", "yT1", "logits", "ranks", "totals"]
MIX_FILLS = ["xT0", "xT1", "q0", "q1", "out0", "out1", "k0", "k1", "v0", "v1", "yT0", "yT1", "logits",
             "shiftT", "ranks", "totals"]
MIX_WORK = [f for f in MIX_FILLS if f not in ROUTE_FILLS]


def mixing_constants(ctx, nc, t):
    shapes = {
        "identf": ([P, P], F32, "c_identity"), "ident": ([P, P], BF16, "c_identity16"),
        "mask_pos": ([P, P], BF16, "c_mask_pos"),
        "sel_head": ([P, MH, P], BF16, "c_sel_head"),
        "before": ([P, P], BF16, "c_before"),
        "descending": ([P, E], F32, "c_descending"),
        "region0": ([P, E], F32, "c_region0"),
        "token0": ([P, TILES], F32, "c_token0"),
        "tile_rows": ([P, 64], F32, "c_tile_rows"),
        "upto": ([P, E * E], F32, "c_upto"),
        "steps": ([P, TABLE], F32, "c_steps"),
        "w_qkv": ([P, KD, 3 * D], F32, "m_w_qkvT"), "w_o": ([P, KD, D], F32, "m_w_oT"), "w_g": ([P, KD, E], F32, "m_w_gT"),
        "b_q": ([P, KD], F32, "m_b_q"), "b_k": ([P, KD], F32, "m_b_k"), "b_v": ([P, D], F32, "m_b_v"),
        "b_o": ([P, D], F32, "m_b_o"), "g1": ([P, D], F32, "m_g1"), "be1": ([P, D], F32, "m_be1"),
    }
    consts, loads = {}, []
    for name, (shape, dt, src) in shapes.items():
        tensor = consts[name] = ctx.enter_context(nc.sbuf_tensor("m_" + name, shape, dt))
        if name.startswith("w_"):
            loads.append((tensor[:, :, :], t[src].rearrange("(k p) n -> p k n", p=P)))
        elif name in ("b_v", "b_o", "g1", "be1"):
            loads.append((tensor[:, :], t[src].partition_broadcast(P)))
        elif len(shape) == 3:
            loads.append((tensor[:, :, :], t[src]))
        else:
            loads.append((tensor[:, :], t[src]))
    return consts, loads


def mixing_program(nc, t, mem, consts, keep):
    ctx = ExitStack()
    with ctx:
        def sb(name, shape, dt=F32):
            return ctx.enter_context(nc.sbuf_tensor(name, shape, dt))

        def signal(name, per, ahead=0):
            return Signal(ctx, nc, name, per, ahead)

        def route_signal(name, per, ahead=0):
            return Signal(ctx, nc, name, per, ahead - per)

        (identf, ident, mask_pos, sel_head, before, descending, region0, token0, tile_rows, upto, steps,
         w_qkv, w_o, w_g, b_q, b_k, b_v, b_o, g1, be1) = consts.values()
        ones16 = sb("ones16", [P, P], BF16)
        ones64 = sb("ones64", [P, MD])
        b_qs = sb("m_b_qs", [P, KD])
        half = sb("m_half", [P, TILES])
        eps = sb("m_eps", [P, TILES])
        x_in = sb("m_x_in", [P, TILES, D])
        stats = sb("m_stats", [P, TILES, 6])
        moments = sb("m_moments", [P, TILES, 2])
        veps = sb("m_veps", [P, TILES])
        rstd = sb("m_rstd", [P, TILES])
        stats1 = sb("m_stats1", [P, TILES, 6])
        moments1 = sb("m_moments1", [P, TILES, 2])
        veps1 = sb("m_veps1", [P, TILES])
        rstd1 = sb("m_rstd1", [P, TILES])
        xn = sb("m_xn", [P, TILES, D])
        xnb = sb("m_xnb", [P, TILES, D])
        xT = sb("m_xT", [P, KD, S])
        qT = sb("m_qT", [P, KD, S])
        kT = sb("m_kT", [P, MH, S])
        v = sb("m_v", [P, TILES, D])
        top = sb("m_top", [P, TILES, MH])
        shift = sb("m_shift", [P, TILES, P], BF16)
        shiftT = sb("m_shiftT", [P, S], BF16)
        probs = sb("m_probs", [P, 2, MH * P])
        rden = sb("m_rden", [P, 2, D])
        oT = sb("m_oT", [P, KD, S])
        mixed = sb("m_mixed", [P, TILES, D])
        rows = sb("m_rows", [P, TILES, ROW])
        yT = oT
        best = sb("m_best", [P, TILES])
        is_best = sb("m_is_best", [P, TILES, E])
        order = sb("m_order", [P, TILES, E])
        first = sb("m_first", [P, TILES])
        chosen = sb("m_chosen", [P, TILES, E], BF16)
        place = sb("m_place", [P, TILES, E])
        own_place = sb("m_own_place", [P, TILES, E])
        slot_f = sb("m_slot_f", [P, TILES])
        slot = sb("m_slot", [P, TILES], U32)
        next_row = sb("m_next_row", [P, 2, E])
        token = sb("m_token", [P, TILES])
        filler = sb("m_filler", [P, ROW])
        filler_row = sb("m_filler_row", [P, E], I32)
        counts = sb("m_counts", [P, E])
        tiles_of = sb("m_tiles_of", [P, E])
        tiles_upto_all = sb("m_tiles_upto_all", [P, E, E])
        tiles_upto = sb("m_tiles_upto", [P, E])
        expert_f = sb("m_expert_f", [P, TABLE])
        step0 = sb("m_step0", [P, TABLE])
        row_a = sb("m_row_a", [P, TABLE])
        row_b = sb("m_row_b", [P, TABLE])
        row_f = sb("m_row_f", [P, TABLE])
        tile_need = probs[:, 0, :].rearrange("p (e k) -> p e k", e=E)
        gone = probs[:, 1, 0:TABLE * E].rearrange("p (j e) -> p j e", e=E)
        passed_tiles = qT[:, 0, 0:TABLE * E].rearrange("p (j e) -> p j e", e=E)
        ps_max, ps_exp, ps_out, ps_work = mem["ps_a"], mem["ps_b"], mem["ps_c"], mem["ps_d"]

        consts_set = signal("m_consts_set", 0)
        x_loaded = signal("m_x_loaded", 16 * B)
        rows_loaded = signal("m_rows_loaded", 16 * B)
        ln_stats = signal("m_ln_stats", TILES)
        ln_moments = signal("m_ln_moments", TILES)
        ln_veps = signal("m_ln_veps", 1)
        ln_rstd = signal("m_ln_rstd", 1)
        ln_done = signal("m_ln_done", TILES)
        xnb_ready = signal("m_xnb_ready", 1)
        ln1_stats = route_signal("m_ln1_stats", TILES)
        ln1_moments = route_signal("m_ln1_moments", TILES)
        ln1_veps = route_signal("m_ln1_veps", 1)
        ln1_rstd = route_signal("m_ln1_rstd", 1)
        ln1_scaled = route_signal("m_ln1_scaled", TILES)
        y_ready = route_signal("m_y_ready", TILES)
        work_full = signal("m_work_full", len(MIX_FILLS), -len(ROUTE_FILLS))
        xT_ready = signal("m_xT_ready", KD)
        q_ready = signal("m_q_ready", KD)
        k_ready = signal("m_k_ready", MH)
        v_ready = signal("m_v_ready", 2)
        max_full = signal("m_max_full", TILES)
        max_free = signal("m_max_free", TILES, 2)
        shift_hi = signal("m_shift_hi", 1)
        shift_ready = signal("m_shift_ready", 1)
        shiftT_ready = signal("m_shiftT_ready", 1)
        exp_full = signal("m_exp_full", TILES)
        exp_done = signal("m_exp_done", TILES, 2)
        probs_used = signal("m_probs_used", TILES, 2)
        recip_done = signal("m_recip_done", TILES)
        out_free = signal("m_out_free", TILES, 2)
        mixed_ready = route_signal("m_mixed_ready", 2)
        yT_ready = route_signal("m_yT_ready", KD)
        best_ready = route_signal("m_best_ready", 1)
        is_best_ready = route_signal("m_is_best_ready", 1)
        order_ready = route_signal("m_order_ready", 1)
        first_ready = route_signal("m_first_ready", 1)
        chosen_ready = route_signal("m_chosen_ready", 1)
        own_place_ready = route_signal("m_own_place_ready", 1)
        slot_f_ready = route_signal("m_slot_f_ready", 1)
        slot_ready = route_signal("m_slot_ready", 1)
        next_row_ready = route_signal("m_next_row_ready", 1, 1)
        place_ready = route_signal("m_place_ready", 1, 1)
        next_row_kept = route_signal("m_next_row_kept", 1, 1)
        token_written = route_signal("m_token_written", 1)
        token_next = route_signal("m_token_next", 1, 1)
        rows_sent = route_signal("m_rows_sent", 16 * TILES, 16)
        filler_sent = signal("m_filler_sent", 0)
        tables = signal("m_tables", 0)
        weights_loaded = signal("m_weights_loaded", 0)
        passed = signal("m_waits_passed_vector", 0)
        pool_passed = signal("m_waits_passed_pool", 0)
        sp_passed = signal("m_waits_passed_sync", 0)

        def released(n, name):
            kind, k = name.rstrip("01"), int(name[-1]) if name[-1] in "01" else 0
            sig, count = {
                "xT": (xT_ready, k + 1), "q": (q_ready, k + 1), "k": (k_ready, 2 * k + 2), "v": (v_ready, k + 1),
                "shiftT": (shiftT_ready, 1), "out": (mixed_ready, k + 1), "yT": (yT_ready, k + 1),
                "logits": (is_best_ready, 1), "ranks": (place_ready, 1), "totals": (next_row_ready, 1),
            }[kind]
            return sig.sem, sig.count(n, count)

        def work_place(n, name):
            if isinstance(n, int) and n == 0:
                j = MIX_WORK.index(name)
                return MIX_WORK, j, j % 2
            order = ROUTE_FILLS if isinstance(n, int) and n == NGROUPS else MIX_FILLS
            j = order.index(name)
            return order, j, (j + len(MIX_WORK)) % 2

        def work_claim(pe, n, name):
            order, j, bank = work_place(n, name)
            if j >= 2:
                pe.wait_ge(*released(n, order[j - 2]))
            elif order is not MIX_WORK:
                pe.wait_ge(*released(n - 1, MIX_FILLS[j - 2]))
            return ps_work[:, bank, :]

        def work_take(eng, n, name):
            order, j, bank = work_place(n, name)
            eng.wait_ge(work_full.sem, j + 1 if order is MIX_WORK else work_full.count(n, j + 1))
            return ps_work[:, bank, :]

        with nc.Block() as block:

            @block.sync
            def _(sp):
                def load_x(m):
                    for s in range(B):
                        sp.dma_start(x_in[s * POS:(s + 1) * POS, :, :],
                                     t["x2_groups"][m, s].rearrange("(c i) d -> i c d", i=POS)).then_inc(x_loaded.sem, 16)

                def load_rows(m):
                    for s in range(B):
                        sp.dma_start(rows[s * POS:(s + 1) * POS, :, D:2 * D],
                                     t["x2_groups"][m, s].rearrange("(c i) d -> i c d", i=POS)).then_inc(rows_loaded.sem, 16)

                def load_expert(e):
                    for k in range(KD):
                        sp.dma_start(keep["w1"][:, k, bass.ds(e * DF, DF)],
                                     t["e_w1"][e, k * P:(k + 1) * P, :]).then_inc(weights_loaded.sem, 16)
                    sp.dma_start(keep["w2"][:, bass.ds(e * KF * D, KF * D)].rearrange("p (j d) -> p j d", j=KF),
                                 t["e_w2"][e].rearrange("(j p) d -> p j d", p=P)).then_inc(weights_loaded.sem, 16)

                def iteration(n, last):
                    if not last:
                        sp.wait_ge(ln_done.sem, ln_done.count(n, TILES))
                        load_x(n + 1)
                    load_expert(n)
                    if not (isinstance(n, int) and n == 0):
                        sp.wait_ge(rows_sent.sem, rows_sent.count(n, 16 * TILES))
                    load_rows(n)

                load_x(0)
                sp.dma_start(keep["b1"][:, :], t["e_b1"]).then_inc(weights_loaded.sem, 16)
                iteration(0, False)
                sp.wait_ge(consts_set.sem, 9)
                for i in range(1, SPARE_TILES):
                    sp.dma_start(t["sorted"][E * REGION + i * P:E * REGION + (i + 1) * P, :],
                                 filler[:, :]).then_inc(filler_sent.sem, 16)
                with sp.Fori(1, NGROUPS - 1) as n:
                    iteration(n, False)
                iteration(NGROUPS - 1, True)
                sp.wait_ge(tables.sem, 1)
                for e in range(E):
                    row0 = sp.value_load(filler_row[0:1, e:e + 1], min_val=0, max_val=E * REGION - P)
                    sp.dma_start(t["sorted"][bass.ds(row0, P), :], filler[:, :]).then_inc(filler_sent.sem, 16)
                sp.wait_ge(weights_loaded.sem, 16 * (1 + E * (KD + 1)))
                sp.wait_ge(filler_sent.sem, 16 * (SPARE_TILES - 1 + E))

            @block.gpsimd
            def _(pool):
                nc.gpsimd.memset(half[:, :], -0.5).then_inc(consts_set.sem, 1)
                nc.gpsimd.memset(eps[:, :], EPS).then_inc(consts_set.sem, 1)
                nc.gpsimd.memset(shift[:, :, :], 0.0).then_inc(consts_set.sem, 1)
                nc.gpsimd.memset(ones16[:, :], 1.0).then_inc(consts_set.sem, 1)
                nc.gpsimd.memset(ones64[:, :], 1.0).then_inc(consts_set.sem, 1)
                nc.gpsimd.memset(kT[:, :, :], 0.0).then_inc(consts_set.sem, 1)
                nc.gpsimd.memset(rows[:, :, 2 * D:ROW], 0.0).then_inc(consts_set.sem, 1)
                nc.gpsimd.memset(filler[:, :], 0.0).then_inc(consts_set.sem, 1)
                pool.wait_ge(consts_set.sem, 8)
                nc.gpsimd.memset(filler[:, 2 * D:2 * D + 1], NO_TOKEN).then_inc(consts_set.sem, 1)
                nc.gpsimd.tensor_scalar(b_qs[:, :], b_q[:, :], M_SCALE, None, ALU.mult).then_inc(consts_set.sem, 1)
                nc.gpsimd.tensor_copy(token[:, :], token0[:, :]).then_inc(token_next.sem, 1)
                pool.wait_ge(consts_set.sem, 10)
                pool.dma_start(t["sorted"][E * REGION:E * REGION + P, :], filler[:, :]).then_inc(rows_sent.sem, 16)

                def ln_first(m):
                    layernorm_rstd(nc, pool, moments, veps, eps[:, :], half[:, :], rstd, ln_moments, ln_veps, ln_rstd, m)

                def bias(n):
                    pool.wait_ge(ln_done.sem, ln_done.count(n, TILES))
                    nc.gpsimd.tensor_tensor(xnb[:, :, :], xn[:, :, :], b_o[:, :].unsqueeze(1).broadcast_to([P, TILES, D]),
                                            ALU.add).then_inc(xnb_ready.sem, 1)

                def iteration(n, work=True, route=True, last=False):
                    if route:
                        wait_apart(pool, pool_passed, rows_sent.sem, rows_sent.count(n, 0))
                        wait_apart(pool, pool_passed, token_next.sem, token_next.count(n, 0))
                        nc.gpsimd.tensor_copy(rows[:, :, 2 * D], token[:, :]).then_inc(token_written.sem, 1)
                        wait_apart(pool, pool_passed, token_written.sem, token_written.count(n, 1))
                        nc.gpsimd.tensor_scalar(token[:, :], token[:, :], float(TILES * POS), None,
                                                ALU.add).then_inc(token_next.sem, 1)
                        layernorm_rstd(nc, pool, moments1, veps1, eps[:, :], half[:, :], rstd1, ln1_moments, ln1_veps, ln1_rstd, n)
                        if work:
                            pool.wait_ge(mixed_ready.sem, mixed_ready.count(n, 2))
                    if work:
                        bias(n)
                        if not last:
                            ln_first(n + 1)
                    if route:
                        wait_apart(pool, pool_passed, rows_loaded.sem, rows_loaded.count(n, 0))
                        wait_apart(pool, pool_passed, y_ready.sem, y_ready.count(n, TILES))
                        wait_apart(pool, pool_passed, slot_ready.sem, slot_ready.count(n, 1))
                        for c in range(TILES):
                            nc.gpsimd.indirect_dma_start(
                                out=t["sorted"], out_offset=bass.IndirectOffsetOnAxis(ap=slot[:, c:c + 1], axis=0),
                                in_=rows[:, c, :], in_offset=None).then_inc(rows_sent.sem, 16)

                ln_first(0)
                iteration(0, route=False)
                with pool.Fori(1, NGROUPS - 1) as n:
                    iteration(n)
                iteration(NGROUPS - 1, last=True)
                iteration(NGROUPS, work=False)
                pool.wait_ge(rows_sent.sem, rows_sent.count(NGROUPS, 16 * TILES))

            @block.vector
            def _(dve):
                def ln_statistics(m):
                    dve.wait_ge(x_loaded.sem, x_loaded.count(m, 16 * B))
                    layernorm_statistics(nc, dve, x_in, stats, moments, passed, ln_stats, ln_moments, m)

                def ln_apply(m):
                    if not (isinstance(m, int) and m == 0):
                        dve.wait_ge(xnb_ready.sem, xnb_ready.count(m, 0))
                    layernorm_apply(nc, dve, x_in, xn, moments, rstd, ln_rstd, ln_done, m)

                def values(n):
                    for i in range(2):
                        ps = work_take(dve, n, f"v{i}")
                        nc.vector.tensor_tensor(v[:, 2 * i:2 * i + 2, :], ps.rearrange("p (c d) -> p c d", c=2),
                                                b_v[:, :].unsqueeze(1).broadcast_to([P, 2, D]),
                                                ALU.add).then_inc(v_ready.sem, 1)

                def maxima(n):
                    for c in range(TILES):
                        dve.wait_ge(max_full.sem, max_full.count(n, c + 1))
                        nc.vector.tensor_reduce(top[:, c, :], ps_max[:, c % 2, :].rearrange("p (h k) -> p h k", h=MH),
                                                AX.X, ALU.max).then_inc(max_free.sem, 1)

                def shift_parts(n):
                    dve.wait_ge(max_free.sem, max_free.count(n, TILES))
                    nc.vector.tensor_scalar(shift[:, :, 0:MH], top[:, :, :], -1.0, None, ALU.mult).then_inc(shift_hi.sem, 1)
                    dve.wait_ge(shift_hi.sem, shift_hi.count(n, 1))
                    nc.vector.scalar_tensor_tensor(shift[:, :, MH:2 * MH], top[:, :, :], -1.0, shift[:, :, 0:MH],
                                                   ALU.mult, ALU.subtract).then_inc(shift_ready.sem, 1)

                def normalise(n, c):
                    dve.wait_ge(probs_used.sem, probs_used.count(n, c + 1))
                    nc.vector.reciprocal(rden[:, c % 2, :], ps_out[:, c % 2, D:2 * D]).then_inc(recip_done.sem, 1)
                    dve.wait_ge(recip_done.sem, recip_done.count(n, c + 1))
                    nc.vector.tensor_tensor(oT[:, :, c * P:(c + 1) * P],
                                            ps_out[:, c % 2, 0:D].rearrange("p (t q) -> p t q", t=KD),
                                            rden[:, c % 2, :].rearrange("p (t q) -> p t q", t=KD),
                                            ALU.mult).then_inc(out_free.sem, 1)

                def post_norm_statistics(n):
                    dve.wait_ge(xnb_ready.sem, xnb_ready.count(n, 0))
                    for i in range(2):
                        ps = work_take(dve, n, f"out{i}")
                        nc.vector.tensor_tensor(mixed[:, 2 * i:2 * i + 2, :], ps.rearrange("p (c d) -> p c d", c=2),
                                                xnb[:, 2 * i:2 * i + 2, :], ALU.add).then_inc(mixed_ready.sem, 1)
                    dve.wait_ge(mixed_ready.sem, mixed_ready.count(n, 2))
                    layernorm_statistics(nc, dve, mixed, stats1, moments1, passed, ln1_stats, ln1_moments, n)
                    dve.wait_ge(ln1_moments.sem, ln1_moments.count(n, TILES))
                    for c in range(TILES):
                        nc.vector.scalar_tensor_tensor(mixed[:, c, :], mixed[:, c, :], moments1[:, c, 0:1], g1[:, :],
                                                       ALU.subtract, ALU.mult).then_inc(ln1_scaled.sem, 1)

                def post_norm_apply(n):
                    dve.wait_ge(ln1_rstd.sem, ln1_rstd.count(n, 1))
                    dve.wait_ge(ln1_scaled.sem, ln1_scaled.count(n, TILES))
                    dve.wait_ge(rows_sent.sem, rows_sent.count(n, 0))
                    for c in range(TILES):
                        nc.vector.scalar_tensor_tensor(rows[:, c, 0:D], mixed[:, c, :], rstd1[:, c:c + 1], be1[:, :],
                                                       ALU.mult, ALU.add).then_inc(y_ready.sem, 1)

                def choose(n):
                    wide = [P, TILES, E]
                    ps = work_take(dve, n, "logits")[:, 0:TILES * E].rearrange("p (c e) -> p c e", c=TILES)
                    nc.vector.tensor_reduce(best[:, :], ps, AX.X, ALU.max).then_inc(best_ready.sem, 1)
                    dve.wait_ge(best_ready.sem, best_ready.count(n, 1))
                    nc.vector.tensor_tensor(is_best[:, :, :], ps, best[:, :].unsqueeze(2).broadcast_to(wide),
                                            ALU.is_equal).then_inc(is_best_ready.sem, 1)
                    dve.wait_ge(is_best_ready.sem, is_best_ready.count(n, 1))
                    nc.vector.tensor_tensor(order[:, :, :], is_best[:, :, :], descending[:, :].unsqueeze(1).broadcast_to(wide),
                                            ALU.mult).then_inc(order_ready.sem, 1)
                    dve.wait_ge(order_ready.sem, order_ready.count(n, 1))
                    nc.vector.tensor_reduce(first[:, :], order[:, :, :], AX.X, ALU.max).then_inc(first_ready.sem, 1)
                    dve.wait_ge(first_ready.sem, first_ready.count(n, 1))
                    nc.vector.tensor_tensor(chosen[:, :, :], order[:, :, :], first[:, :].unsqueeze(2).broadcast_to(wide),
                                            ALU.is_equal).then_inc(chosen_ready.sem, 1)

                def slots(n):
                    wide = [P, TILES, E]
                    ps = work_take(dve, n, "ranks")[:, 0:TILES * E].rearrange("p (c e) -> p c e", c=TILES)
                    dve.wait_ge(next_row_kept.sem, next_row_kept.count(n, 0))
                    nc.vector.tensor_tensor(place[:, :, :], ps, next_row[:, 0, :].unsqueeze(1).broadcast_to(wide),
                                            ALU.add).then_inc(place_ready.sem, 1)
                    ps = work_take(dve, n, "totals")[:, 0:E]
                    nc.vector.tensor_tensor(next_row[:, 1, :], ps, next_row[:, 0, :], ALU.add).then_inc(next_row_ready.sem, 1)
                    dve.wait_ge(place_ready.sem, place_ready.count(n, 1))
                    nc.vector.tensor_tensor(own_place[:, :, :], place[:, :, :], chosen[:, :, :],
                                            ALU.mult).then_inc(own_place_ready.sem, 1)
                    dve.wait_ge(own_place_ready.sem, own_place_ready.count(n, 1))
                    nc.vector.tensor_reduce(slot_f[:, :], own_place[:, :, :], AX.X, ALU.add).then_inc(slot_f_ready.sem, 1)
                    dve.wait_ge(slot_f_ready.sem, slot_f_ready.count(n, 1))
                    nc.vector.tensor_copy(slot[:, :], slot_f[:, :]).then_inc(slot_ready.sem, 1)
                    dve.wait_ge(next_row_ready.sem, next_row_ready.count(n, 1))
                    nc.vector.tensor_copy(next_row[:, 0, :], next_row[:, 1, :]).then_inc(next_row_kept.sem, 1)

                def iteration(n, work=True, route=True, last=False):
                    if route:
                        post_norm_statistics(n)
                        post_norm_apply(n)
                    if work:
                        values(n)
                    if work:
                        maxima(n)
                        shift_parts(n)
                    if route:
                        choose(n)
                    if work:
                        if not last:
                            ln_statistics(n + 1)
                        normalise(n, 0)
                    if route:
                        slots(n)
                    if work:
                        if not last:
                            ln_apply(n + 1)
                        for c in range(1, TILES):
                            normalise(n, c)

                def step_tables():
                    done = 1

                    def then(instruction):
                        nonlocal done
                        done += 1
                        instruction.then_inc(tables.sem, 1)
                        dve.wait_ge(tables.sem, done)

                    dve.wait_ge(next_row_kept.sem, NGROUPS + 1)
                    nc.vector.tensor_copy(filler_row[:, :], next_row[:, 0, :]).then_inc(tables.sem, 1)
                    then(nc.vector.tensor_tensor(counts[:, :], next_row[:, 0, :], region0[:, :], ALU.subtract))
                    wide = [P, E, 64]
                    then(nc.vector.tensor_tensor(tile_need[:, :, :], counts[:, :].unsqueeze(2).broadcast_to(wide),
                                                 tile_rows[:, :].unsqueeze(1).broadcast_to(wide), ALU.is_gt))
                    then(nc.vector.tensor_reduce(tiles_of[:, :], tile_need[:, :, :], AX.X, ALU.add))
                    wide = [P, E, E]
                    then(nc.vector.tensor_tensor(tiles_upto_all[:, :, :], tiles_of[:, :].unsqueeze(1).broadcast_to(wide),
                                                 upto[:, :].rearrange("p (a b) -> p a b", a=E), ALU.mult))
                    then(nc.vector.tensor_reduce(tiles_upto[:, :], tiles_upto_all[:, :, :], AX.X, ALU.add))
                    wide = [P, TABLE, E]
                    then(nc.vector.tensor_tensor(gone[:, :, :], steps[:, :].unsqueeze(2).broadcast_to(wide),
                                                 tiles_upto[:, :].unsqueeze(1).broadcast_to(wide), ALU.is_ge))
                    then(nc.vector.tensor_reduce(expert_f[:, :], gone[:, :, :], AX.X, ALU.add))
                    then(nc.vector.tensor_tensor(passed_tiles[:, :, :], gone[:, :, :],
                                                 tiles_of[:, :].unsqueeze(1).broadcast_to(wide), ALU.mult))
                    then(nc.vector.tensor_reduce(step0[:, :], passed_tiles[:, :, :], AX.X, ALU.add))
                    then(nc.vector.tensor_tensor(row_a[:, :], steps[:, :], step0[:, :], ALU.subtract))
                    then(nc.vector.tensor_scalar(row_b[:, :], row_a[:, :], float(P), None, ALU.mult))
                    then(nc.vector.scalar_tensor_tensor(row_f[:, :], expert_f[:, :], float(REGION), row_b[:, :],
                                                        ALU.mult, ALU.add))
                    then(nc.vector.tensor_copy(keep["row_table"][:, :], row_f[:, :]))
                    then(nc.vector.tensor_scalar(keep["expert_table"][:, :], expert_f[:, :], float(E - 1), None, ALU.min))

                dve.wait_ge(consts_set.sem, 10)
                dve.sem_inc(max_free.sem, 2)
                dve.sem_inc(out_free.sem, 2)
                nc.vector.tensor_copy(next_row[:, 0, :], region0[:, :]).then_inc(next_row_kept.sem, 1)
                ln_statistics(0)
                ln_apply(0)
                iteration(0, route=False)
                with dve.Fori(1, NGROUPS - 1) as n:
                    iteration(n)
                iteration(NGROUPS - 1, last=True)
                iteration(NGROUPS, work=False)
                step_tables()

            @block.scalar
            def _(act):
                def iteration(n, work=True, route=True):
                    if work:
                        for k in range(KD):
                            ps = work_take(act, n, f"xT{k}")
                            nc.scalar.activation(xT[:, k, :], ps, ACT.Copy).then_inc(xT_ready.sem, 1)
                        for tile in range(KD):
                            ps = work_take(act, n, f"q{tile}")
                            nc.scalar.activation(qT[:, tile, :], ps, ACT.Identity, scale=M_SCALE,
                                                 bias=b_qs[:, tile:tile + 1]).then_inc(q_ready.sem, 1)
                        for tile in range(KD):
                            ps = work_take(act, n, f"k{tile}")
                            for odd in range(2):
                                own = slice(MD * odd, MD * odd + MD)
                                nc.scalar.activation(kT[own, 2 * tile + odd, :], ps[own, :], ACT.Identity,
                                                     bias=b_k[own, tile:tile + 1]).then_inc(k_ready.sem, 1)
                    if route:
                        for k in range(KD):
                            ps = work_take(act, n, f"yT{k}")
                            nc.scalar.activation(yT[:, k, :], ps, ACT.Copy).then_inc(yT_ready.sem, 1)
                    if work:
                        ps = work_take(act, n, "shiftT")
                        nc.scalar.activation(shiftT[:, :], ps.bitcast(BF16)[:, 0:S], ACT.Copy).then_inc(shiftT_ready.sem, 1)
                        for c in range(TILES):
                            act.wait_ge(probs_used.sem, probs_used.count(n, c - 1))
                            act.wait_ge(exp_full.sem, exp_full.count(n, c + 1))
                            nc.scalar.activation(probs[:, c % 2, :], ps_exp[:, c % 2, :], ACT.Exp).then_inc(exp_done.sem, 1)

                act.wait_ge(consts_set.sem, 10)
                act.sem_inc(exp_done.sem, 2)
                iteration(0, route=False)
                with act.Fori(1, NGROUPS) as n:
                    iteration(n)
                iteration(NGROUPS, work=False)

            @block.tensor
            def _(pe):
                def features(n):
                    for k in range(KD):
                        ps = work_claim(pe, n, f"xT{k}")
                        pe.wait_ge(ln_done.sem, ln_done.count(n, TILES))
                        for c in range(TILES):
                            mm = nc.tensor.transpose(ps[:, c * P:(c + 1) * P], xn[:, c, k * P:(k + 1) * P], identf[:, :])
                        mm.then_inc(work_full.sem, 1)

                def queries_or_keys(n, tiles):
                    pe.wait_ge(xT_ready.sem, xT_ready.count(n, KD))
                    for j in tiles:
                        ps = work_claim(pe, n, ("q0", "q1", "k0", "k1")[j])
                        for k in range(KD):
                            mm = nc.tensor.matmul(ps, w_qkv[:, k, j * P:(j + 1) * P], xT[:, k, :],
                                                  start=(k == 0), stop=(k == KD - 1))
                        mm.then_inc(work_full.sem, 1)

                def all_values(n):
                    for i in range(2):
                        ps = work_claim(pe, n, f"v{i}")
                        for c in (2 * i, 2 * i + 1):
                            for k in range(KD):
                                mm = nc.tensor.matmul(ps[:, (c % 2) * D:(c % 2 + 1) * D], xT[:, k, c * P:(c + 1) * P],
                                                      w_qkv[:, k, 2 * D:3 * D], start=(k == 0 and c % 2 == 0),
                                                      stop=(k == KD - 1), skip_group_check=True)
                        mm.then_inc(work_full.sem, 1)

                wide = mask_pos[:, :].unsqueeze(1).broadcast_to([P, MH, P])

                def add(out, lhsT, rhs):
                    return nc.tensor.matmul(out, lhsT, rhs, start=False, stop=True, skip_group_check=True)

                def scores(n):
                    pe.wait_ge(q_ready.sem, q_ready.count(n, KD))
                    pe.wait_ge(k_ready.sem, k_ready.count(n, MH))
                    for c in range(TILES):
                        pe.wait_ge(max_free.sem, max_free.count(n, c - 1))
                        ps = ps_max[:, c % 2, :]
                        nc.tensor.matmul(ps.rearrange("p (h k) -> p h k", h=MH), ident[:, :], wide, start=True, stop=False,
                                         skip_group_check=True)
                        for h in range(MH):
                            mm = add(ps[:, h * P:(h + 1) * P], qT[:, h // 2, c * P:(c + 1) * P], kT[:, h, c * P:(c + 1) * P])
                        mm.then_inc(max_full.sem, 1)

                def shift_transposes(n):
                    ps = work_claim(pe, n, "shiftT")
                    pe.wait_ge(shift_ready.sem, shift_ready.count(n, 1))
                    for c in range(TILES):
                        mm = nc.tensor.transpose(ps.bitcast(BF16)[:, c * P:(c + 1) * P], shift[:, c, :], ident[:, :])
                    mm.then_inc(work_full.sem, 1)

                def shifted(n, c):
                    pe.wait_ge(exp_done.sem, exp_done.count(n, c - 1))
                    ps = ps_exp[:, c % 2, :]
                    nc.tensor.matmul(ps.rearrange("p (h k) -> p h k", h=MH), ident[:, :], wide, start=True, stop=False,
                                     skip_group_check=True)
                    for h in range(MH):
                        add(ps[:, h * P:(h + 1) * P], kT[:, h, c * P:(c + 1) * P], qT[:, h // 2, c * P:(c + 1) * P])
                    if c == 0:
                        pe.wait_ge(shiftT_ready.sem, shiftT_ready.count(n, 1))
                    for h in range(MH):
                        mm = add(ps[:, h * P:(h + 1) * P], sel_head[:, h, :], shiftT[:, c * P:(c + 1) * P])
                    mm.then_inc(exp_full.sem, 1)

                def values(n, c):
                    if c == 0:
                        pe.wait_ge(v_ready.sem, v_ready.count(n, 2))
                    pe.wait_ge(out_free.sem, out_free.count(n, c - 1))
                    pe.wait_ge(exp_done.sem, exp_done.count(n, c + 1))
                    for side in range(2):
                        for h in range(MH):
                            lo, col = MD * (h % 2), D * side + P * (h // 2)
                            mm = nc.tensor.matmul(ps_out[lo:lo + MD, c % 2, col:col + P],
                                                  v[:, c, MD * h:MD * h + MD] if side == 0 else ones64[:, :],
                                                  probs[:, c % 2, h * P:(h + 1) * P],
                                                  start=(side == 0 and h < 2), stop=True, skip_group_check=True)
                    mm.then_inc(probs_used.sem, 1)

                def output(n):
                    for i in range(2):
                        ps = work_claim(pe, n, f"out{i}")
                        pe.wait_ge(out_free.sem, out_free.count(n, 2 * i + 2 - TILES))
                        for c in (2 * i, 2 * i + 1):
                            for tile in range(KD):
                                mm = nc.tensor.matmul(ps[:, (c % 2) * D:(c % 2 + 1) * D], oT[:, tile, c * P:(c + 1) * P],
                                                      w_o[:, tile, :], start=(tile == 0 and c % 2 == 0),
                                                      stop=(tile == KD - 1), skip_group_check=True)
                        mm.then_inc(work_full.sem, 1)

                def y_features(n):
                    for k in range(KD):
                        ps = work_claim(pe, n, f"yT{k}")
                        pe.wait_ge(y_ready.sem, y_ready.count(n, TILES))
                        for c in range(TILES):
                            mm = nc.tensor.transpose(ps[:, c * P:(c + 1) * P], rows[:, c, k * P:(k + 1) * P], identf[:, :])
                        mm.then_inc(work_full.sem, 1)

                def logits(n):
                    ps = work_claim(pe, n, "logits")
                    pe.wait_ge(yT_ready.sem, yT_ready.count(n, KD))
                    for c in range(TILES):
                        for k in range(KD):
                            mm = nc.tensor.matmul(ps[:, c * E:(c + 1) * E], yT[:, k, c * P:(c + 1) * P], w_g[:, k, :],
                                                  start=(c == 0 and k == 0), stop=(k == KD - 1), skip_group_check=True)
                    mm.then_inc(work_full.sem, 1)

                def ranks(n):
                    ps = work_claim(pe, n, "ranks")
                    pe.wait_ge(chosen_ready.sem, chosen_ready.count(n, 1))
                    nc.tensor.matmul(ps[:, 0:TILES * E], before[:, :], chosen[:, :, :].rearrange("p c e -> p (c e)"),
                                     start=True, stop=False, skip_group_check=True)
                    for c in range(TILES - 1):
                        later = TILES - 1 - c
                        mm = nc.tensor.matmul(ps[:, (c + 1) * E:TILES * E].rearrange("p (c e) -> p c e", e=E), ones16[:, :],
                                              chosen[:, c, :].unsqueeze(1).broadcast_to([P, later, E]), start=False,
                                              stop=True, skip_group_check=True)
                    mm.then_inc(work_full.sem, 1)
                    ps = work_claim(pe, n, "totals")
                    for c in range(TILES):
                        mm = nc.tensor.matmul(ps[:, 0:E], ones16[:, :], chosen[:, c, :], start=(c == 0), stop=(c == TILES - 1))
                    mm.then_inc(work_full.sem, 1)

                def iteration(n, work=True, route=True):
                    if work:
                        features(n)
                        queries_or_keys(n, (0, 1))
                    if route:
                        output(n)
                    if work:
                        queries_or_keys(n, (2, 3))
                        all_values(n)
                    if route:
                        y_features(n)
                    if work:
                        scores(n)
                    if route:
                        logits(n)
                    if work:
                        shift_transposes(n)
                        shifted(n, 0)
                        shifted(n, 1)
                        values(n, 0)
                    if route:
                        ranks(n)
                    if work:
                        shifted(n, 2)
                        values(n, 1)
                        shifted(n, 3)
                        values(n, 2)
                        values(n, 3)

                pe.wait_ge(consts_set.sem, 10)
                pe.sem_inc(probs_used.sem, 2)
                pe.sem_inc(next_row_ready.sem, 1)
                pe.sem_inc(place_ready.sem, 1)
                iteration(0, route=False)
                with pe.Fori(1, NGROUPS) as n:
                    iteration(n)
                iteration(NGROUPS, work=False)


UNROLL = 4
ROUNDS = STEPS // UNROLL


def expert_program(nc, t, mem, identf, keep):
    ctx = ExitStack()
    with ctx:
        def sb(name, shape, dt=F32):
            return ctx.enter_context(nc.sbuf_tensor(name, shape, dt))

        def signal(name, per, ahead=0):
            return Signal(ctx, nc, name, per, ahead)

        b2 = sb("e_b2", [P, E * D])
        g2 = sb("e_g2", [P, D])
        be2 = sb("e_be2", [P, D])
        half = sb("e_half", [P, 1])
        eps = sb("e_eps", [P, 1])
        row = sb("e_row", [P, UNROLL, ROW])
        token = sb("e_token", [P, UNROLL, 1], U32)
        yT = sb("e_yT", [P, 2, KD * P])
        w1_now = sb("e_w1_now", [P, 2, KD, DF])
        hT = sb("e_hT", [P, 2, KF, P])
        yb = sb("e_yb", [P, 2, D])
        xb = sb("e_xb", [P, 2, D])
        summed = sb("e_summed", [P, 2, D])
        stats = sb("e_stats", [P, 2, 6])
        moments = sb("e_moments", [P, 2, 2])
        veps = sb("e_veps", [P, 2])
        rstd = sb("e_rstd", [P, 2])
        scaled = sb("e_scaled", [P, 2, D])
        result = sb("e_result", [P, 2, D])
        ps_h = [mem["ps_a"], mem["ps_b"]]
        ps_out, ps_yT = mem["ps_c"], mem["ps_d"]
        w1, w2, b1 = keep["w1"], keep["w2"], keep["b1"]

        consts_loaded = signal("e_consts_loaded", 0)
        consts_set = signal("e_consts_set", 0)
        row_loaded = [signal(f"e_row_loaded{u}", 16) for u in range(UNROLL)]
        yT_full = signal("e_yT_full", 1)
        yT_ready = signal("e_yT_ready", 1)
        w1_ready = signal("e_w1_ready", KD)
        h_full = signal("e_h_full", KF // 4)
        hT_ready = signal("e_hT_ready", KF)
        out_full = signal("e_out_full", 1)
        yb_ready = signal("e_yb_ready", 1)
        xb_ready = signal("e_xb_ready", 1)
        token_ready = signal("e_token_ready", 1)
        sum_ready = signal("e_sum_ready", 1)
        stats_ready = signal("e_stats_ready", 1)
        moments_ready = signal("e_moments_ready", 1)
        veps_ready = signal("e_veps_ready", 1)
        rstd_ready = signal("e_rstd_ready", 1)
        scaled_ready = signal("e_scaled_ready", 1)
        result_ready = signal("e_result_ready", 1)
        stored = [signal(f"e_stored{u}", 16) for u in range(2)]
        passed = signal("e_waits_passed_vector", 0)
        pool_passed = signal("e_waits_passed_pool", 0)

        def expert_of(eng, j):
            return eng.value_load(keep["expert_table"][0:1, bass.ds(j, 1)], min_val=0, max_val=E - 1)

        def rounds(eng, step):
            for u in range(UNROLL):
                step(0, u)
            with eng.Fori(1, ROUNDS - 1) as i:
                for u in range(UNROLL):
                    step(i, u)
            for u in range(UNROLL):
                step(ROUNDS - 1, u)

        def is_step(i, u):
            return not (isinstance(i, int) and i * UNROLL + u >= STEPS)

        def await_row(eng, i, u):
            sig = row_loaded[u % UNROLL]
            eng.wait_ge(sig.sem, sig.count(i + u // UNROLL, 16))

        with nc.Block() as block:

            @block.sync
            def _(sp):
                def load(i, u):
                    j = i * UNROLL + u
                    if not isinstance(i, int):
                        sp.wait_ge(xb_ready.sem, xb_ready.count(j - UNROLL, 1))
                        sp.wait_ge(token_ready.sem, token_ready.count(j - UNROLL, 1))
                        sp.wait_ge(yT_full.sem, yT_full.count(j - UNROLL, 1))
                    row0 = sp.value_load(keep["row_table"][0:1, bass.ds(j, 1)], min_val=0,
                                         max_val=E * REGION + (SPARE_TILES - 1) * P)
                    sp.dma_start(row[:, u, :], t["sorted"][bass.ds(row0, P), :]).then_inc(row_loaded[u].sem, 16)

                for u in range(UNROLL):
                    load(0, u)
                for dst, src in ((b2, "e_b2"), (g2, "e_g2"), (be2, "e_be2")):
                    sp.dma_start(dst[:, :], t[src].partition_broadcast(P)).then_inc(consts_loaded.sem, 16)
                with sp.Fori(1, ROUNDS) as i:
                    for u in range(UNROLL):
                        load(i, u)

            @block.gpsimd
            def _(pool):
                nc.gpsimd.memset(half[:, :], -0.5).then_inc(consts_set.sem, 1)
                nc.gpsimd.memset(eps[:, :], EPS).then_inc(consts_set.sem, 1)
                pool.wait_ge(consts_set.sem, 2)
                pool.wait_ge(consts_loaded.sem, 48)

                def residuals(i, u):
                    j = i * UNROLL + u
                    e = expert_of(pool, j)
                    await_row(pool, i, u)
                    nc.gpsimd.tensor_tensor(yb[:, u % 2, :], row[:, u % UNROLL, 0:D], b2[:, bass.ds(e * D, D)],
                                            ALU.add).then_inc(yb_ready.sem, 1)
                    nc.gpsimd.tensor_tensor(xb[:, u % 2, :], row[:, u % UNROLL, D:2 * D], be2[:, :],
                                            ALU.add).then_inc(xb_ready.sem, 1)

                def step(i, u):
                    j, s = i * UNROLL + u, u % 2
                    if is_step(i, u + 1):
                        residuals(i, u + 1)
                    pool.wait_ge(moments_ready.sem, moments_ready.count(j, 1))
                    nc.gpsimd.tensor_tensor(veps[:, s:s + 1], moments[:, s, 1:2], eps[:, :], ALU.add).then_inc(veps_ready.sem, 1)
                    pool.wait_ge(veps_ready.sem, veps_ready.count(j, 1))
                    nc.gpsimd.tensor_tensor(rstd[:, s:s + 1], veps[:, s:s + 1], half[:, :], ALU.pow).then_inc(rstd_ready.sem, 1)
                    wait_apart(pool, pool_passed, result_ready.sem, result_ready.count(j, 1))
                    nc.gpsimd.indirect_dma_start(
                        out=t["out"], out_offset=bass.IndirectOffsetOnAxis(ap=token[:, u, :], axis=0),
                        in_=result[:, s, :], in_offset=None, bounds_check=B * S - 1, oob_is_err=False
                        ).then_inc(stored[s].sem, 16)

                residuals(0, 0)
                rounds(pool, step)
                for s in range(2):
                    pool.wait_ge(stored[s].sem, 16 * (STEPS // 2))

            @block.vector
            def _(dve):
                def hidden(i, u):
                    j, s = i * UNROLL + u, u % 2
                    e = expert_of(dve, j)
                    await_row(dve, i, u)
                    nc.vector.tensor_copy(token[:, u % UNROLL, :], row[:, u % UNROLL, 2 * D:2 * D + 1]).then_inc(token_ready.sem, 1)
                    for f in range(KF):
                        if f % 4 == 0:
                            dve.wait_ge(h_full.sem, h_full.count(j, f // 4 + 1))
                        nc.vector.tensor_scalar(hT[:, s, f, :], ps_h[s][:, f // 4, (f % 4) * P:(f % 4 + 1) * P],
                                                b1[:, bass.ds(e * KF + f, 1)], 0.0, ALU.add, ALU.max
                                                ).then_inc(hT_ready.sem, 1)

                def step(i, u):
                    j, s = i * UNROLL + u, u % 2
                    if is_step(i, u + 1):
                        hidden(i, u + 1)
                    dve.wait_ge(out_full.sem, out_full.count(j, 1))
                    dve.wait_ge(yb_ready.sem, yb_ready.count(j, 1))
                    nc.vector.tensor_tensor(summed[:, s, :], ps_out[:, s, 0:D], yb[:, s, :], ALU.add).then_inc(sum_ready.sem, 1)
                    dve.wait_ge(sum_ready.sem, sum_ready.count(j, 1))
                    nc.vector.bn_stats(stats[:, s, :], summed[:, s, :]).then_inc(stats_ready.sem, 1)
                    wait_apart(dve, passed, stats_ready.sem, stats_ready.count(j, 1))
                    nc.vector.bn_aggr(moments[:, s, :], stats[:, s, :]).then_inc(moments_ready.sem, 1)
                    dve.wait_ge(moments_ready.sem, moments_ready.count(j, 1))
                    nc.vector.scalar_tensor_tensor(scaled[:, s, :], summed[:, s, :], moments[:, s, 0:1], g2[:, :],
                                                   ALU.subtract, ALU.mult).then_inc(scaled_ready.sem, 1)
                    dve.wait_ge(scaled_ready.sem, scaled_ready.count(j, 1))
                    dve.wait_ge(rstd_ready.sem, rstd_ready.count(j, 1))
                    dve.wait_ge(xb_ready.sem, xb_ready.count(j, 1))
                    if not (isinstance(i, int) and i == 0 and u < 2):
                        stores = stored[s].count(i * 2 + u // 2, 0)
                        dve.wait_ge(stored[s].sem, stores)
                    nc.vector.scalar_tensor_tensor(result[:, s, :], scaled[:, s, :], rstd[:, s:s + 1], xb[:, s, :],
                                                   ALU.mult, ALU.add).then_inc(result_ready.sem, 1)

                dve.wait_ge(consts_loaded.sem, 48)
                hidden(0, 0)
                rounds(dve, step)

            @block.scalar
            def _(act):
                def weights(j, s):
                    e = expert_of(act, j)
                    for k in range(KD):
                        nc.scalar.activation(w1_now[:, s, k, :], w1[:, k, bass.ds(e * DF, DF)], ACT.Copy).then_inc(w1_ready.sem, 1)

                def features(j, s):
                    act.wait_ge(yT_full.sem, yT_full.count(j, 1))
                    nc.scalar.activation(yT[:, s, :], ps_yT[:, s, 0:KD * P], ACT.Copy).then_inc(yT_ready.sem, 1)

                def step(i, u):
                    if is_step(i, u + 2):
                        features(i * UNROLL + (u + 2), u % 2)
                        weights(i * UNROLL + (u + 2), u % 2)

                for j in range(2):
                    weights(j, j)
                    features(j, j)
                rounds(act, step)

            @block.tensor
            def _(pe):
                def features(i, u):
                    await_row(pe, i, u)
                    for k in range(KD):
                        mm = nc.tensor.transpose(ps_yT[:, u % 2, k * P:(k + 1) * P], row[:, u % UNROLL, k * P:(k + 1) * P],
                                                 identf[:, :])
                    mm.then_inc(yT_full.sem, 1)

                def hidden(i, u):
                    j, s = i * UNROLL + u, u % 2
                    pe.wait_ge(yT_ready.sem, yT_ready.count(j, 1))
                    pe.wait_ge(w1_ready.sem, w1_ready.count(j, KD))
                    for f in range(KF):
                        for k in range(KD):
                            mm = nc.tensor.matmul(ps_h[s][:, f // 4, (f % 4) * P:(f % 4 + 1) * P],
                                                  w1_now[:, s, k, f * P:(f + 1) * P], yT[:, s, k * P:(k + 1) * P],
                                                  start=(f % 4 == 0 and k == 0), stop=(k == KD - 1), skip_group_check=True)
                        if f % 4 == 3:
                            mm.then_inc(h_full.sem, 1)

                def output(i, u):
                    j, s = i * UNROLL + u, u % 2
                    e = expert_of(pe, j)
                    pe.wait_ge(hT_ready.sem, hT_ready.count(j, KF))
                    for f in range(KF):
                        mm = nc.tensor.matmul(ps_out[:, s, 0:D], hT[:, s, f, :], w2[:, bass.ds(e * KF * D + f * D, D)],
                                              start=(f == 0), stop=(f == KF - 1))
                    mm.then_inc(out_full.sem, 1)

                def step(i, u):
                    if is_step(i, u + 2):
                        features(i, u + 2)
                    if is_step(i, u + 1):
                        hidden(i, u + 1)
                    output(i, u)

                features(0, 0)
                features(0, 1)
                hidden(0, 0)
                rounds(pe, step)


def decoder_block(nc, t):
    t["x2"] = nc.dram_tensor("x2_rows", [B, S, D], F32, kind="Internal").ap()
    t["x2_groups"] = t["x2"].rearrange("s (g p) d -> g s p d", g=NGROUPS)
    t["qk_parts"] = nc.dram_tensor("qk_parts", [2, 3, HD, HEADS, S], BF16, kind="Internal").ap()
    t["ctx_q_parts"] = nc.dram_tensor("ctx_q_parts", [3, HD, HEADS, S], BF16, kind="Internal").ap()
    t["ctx_k_parts"] = nc.dram_tensor("ctx_k_parts", [3, HD, HEADS, CTX], BF16, kind="Internal").ap()
    t["sorted"] = nc.dram_tensor("sorted_rows", [E * REGION + SPARE_TILES * P, ROW], F32, kind="Internal").ap()
    with ExitStack() as ctx:
        mem = {name: ctx.enter_context(nc.psum_tensor(name, [P, 2, 512], F32)) for name in ("ps_a", "ps_b", "ps_c", "ps_d")}
        consts, loads = mixing_constants(ctx, nc, t)
        attention_program(nc, t, mem, loads)
        shapes = {"w1": [P, KD, E * DF], "w2": [P, E * KF * D], "b1": [P, E * KF]}
        keep = {name: ctx.enter_context(nc.sbuf_tensor("keep_" + name, shape, F32)) for name, shape in shapes.items()}
        for name in ("row_table", "expert_table"):
            keep[name] = ctx.enter_context(nc.sbuf_tensor("keep_" + name, [P, TABLE], I32))
        mixing_program(nc, t, mem, consts, keep)
        expert_program(nc, t, mem, consts["identf"], keep)


def constants():
    import numpy as np
    i = np.arange(P)
    eye = np.eye(P, dtype=np.float32)
    own = np.where(i[None, :] <= i[:, None], 0, NEG)
    previous = np.where(i[None, :] > i[:, None], 0, NEG)
    first = np.where(i[None, :] < PREFIX, 0, previous)
    col = np.arange(D)
    odd = (col % 32) // HD
    prefix_rows = i[:, None] // 32 == np.arange(HEADS) % GROUP
    prefix_ones = np.zeros((P, HEADS, 32))
    prefix_ones[:, :, HD] = prefix_rows
    sel_head = np.zeros((P, MH, P))
    for h in range(MH):
        sel_head[[h, MH + h], h] = 1
    e = np.arange(E)
    fp32 = {
        "c_identity": eye, "c_prefix_rows": prefix_rows, "c_prefix_ones": prefix_ones,
        "c_ctx_rows": i[:, None] // CTX == odd,
        "c_descending": np.broadcast_to(E - e, (P, E)), "c_region0": np.broadcast_to(e * REGION, (P, E)),
        "c_token0": (i // POS * S + i % POS)[:, None] + POS * np.arange(TILES),
        "c_tile_rows": np.broadcast_to(P * np.arange(64), (P, 64)),
        "c_upto": np.broadcast_to((e[None, :] <= e[:, None]).reshape(-1), (P, E * E)),
        "c_steps": np.broadcast_to(np.arange(TABLE), (P, TABLE)),
    }
    bf16 = {
        "c_identity16": eye, "c_mask_qk": np.stack([np.concatenate([p, own], 1) for p in (first, previous)], 1),
        "c_mask_kq": np.concatenate([own.T, first.T, own.T, previous.T, own.T], 1),
        "c_mask_prefix": np.broadcast_to(np.where(i % 32 < PREFIX, 0, NEG)[:, None], (P, 256)), "c_sel_head": sel_head,
        "c_mask_pos": np.where(i[:, None] % POS == i % POS, 0, NEG), "c_before": i[:, None] < i,
    }
    out = {k: np.ascontiguousarray(v, np.float32) for k, v in fp32.items()}
    out.update({k: np.ascontiguousarray(np.asarray(v, np.float32)).astype(mybir.dt.np(BF16)) for k, v in bf16.items()})
    return out


def kernel(**inputs):
    import numpy as np
    import concourse.bacc as bacc
    from concourse.bass_utils import run_bass_kernel_spmd

    def array(name):
        return np.asarray(inputs[name])

    def columns(a):
        return a.reshape(-1, P).T

    laid = {"x": array("x"), "ctx": array("ctx_1024"), "mask": array("mask_BxSxS2_if1"),
            "w_qkvT": array("L0_attn_w_qkv").T, "w_outT": array("L0_attn_w_out").T,
            "b_q2": columns(array("L0_xattn_bq")), "b_k2": columns(array("L0_xattn_bk")),
            "b_v2": array("L0_xattn_bv"), "b_o2": array("L0_xattn_bo"),
            "m_w_qkvT": array("L0_ffn_Wqkv").T, "m_w_oT": array("L0_ffn_Wo").T, "m_w_gT": array("L0_ffn_Wg").T,
            "m_b_q": columns(array("L0_ffn_bqkv")[0:D]), "m_b_k": columns(array("L0_ffn_bqkv")[D:2 * D]),
            "m_b_v": array("L0_ffn_bqkv")[2 * D:], "m_b_o": array("L0_ffn_bo"),
            "m_g1": array("L0_ffn_g1"), "m_be1": array("L0_ffn_be1"),
            "e_w1": array("L0_ffn_W1"), "e_w2": array("L0_ffn_W2"), "e_b1": columns(array("L0_ffn_b1")),
            "e_b2": array("L0_ffn_b2").reshape(-1), "e_g2": array("L0_ffn_g2"), "e_be2": array("L0_ffn_be2")}
    for a in "qkvo":
        laid[f"w_{a}2T"] = array(f"L0_xattn_W{a}").T
    laid.update(constants())

    nc = bacc.Bacc("TRN2", target_bir_lowering=False, num_devices=1)
    arrays, t = {}, {}
    for name, a in laid.items():
        a = np.ascontiguousarray(a)
        arrays["in_" + name] = a
        t[name] = nc.dram_tensor("in_" + name, a.shape, mybir.dt.from_np(a.dtype), kind="ExternalInput").ap()
    out = nc.dram_tensor("out", [B * S, D], F32, kind="ExternalOutput").ap()
    t["out"] = out
    decoder_block(nc, t)
    r = run_bass_kernel_spmd(nc, [arrays], core_ids=[0])
    return r.results[0]["out"].reshape(B, S, D)
```
